# Optimizing a Trainium2 kernel written in Bass

```python
import numpy as np
import jax
import jax.numpy as jnp

def _softmax(x, axis=-1):
    return jax.nn.softmax(x, axis=axis)

def _gelu(x):
    return jax.nn.gelu(x, approximate=True)

def _silu(x):
    return jax.nn.silu(x)

def _sigmoid(x):
    return jax.nn.sigmoid(x)

def _layernorm(x, axis=-1, eps=1e-05):
    m = jnp.mean(x, axis=axis, keepdims=True)
    v = jnp.var(x, axis=axis, keepdims=True)
    return (x - m) / jnp.sqrt(v + eps)

def _scatter_add(tgt, idx, src, axis=0):
    return tgt.at[idx].add(src)

def _segment_sum(src, seg, n):
    return jax.ops.segment_sum(src, seg, n)
kernel_name = 'mk_decoder_preln_d2_seqx_r4_fc1d6d'

def setup_inputs(seed: int=0):
    np.random.seed(seed)
    _w = jnp.asarray

    def _rec_inputs():
        import jax
        import jax.numpy as jnp
        _rk = jax.random.key(seed)
        x = 7.22e-05 + 1 * jax.random.normal(jax.random.fold_in(_rk, 1), (4, 512, 512), jnp.float32)
        _lenS = 512 - jax.random.randint(jax.random.fold_in(_rk, 7), (4,), 0, max(1, 512 // 4) + 1, jnp.int32)
        _lenS2 = 512 - jax.random.randint(jax.random.fold_in(_rk, 8), (4,), 0, max(1, 512 // 4) + 1, jnp.int32)
        _ctx_1024P = jax.random.normal(jax.random.fold_in(_rk, 11), (4, 16, 256), jnp.float32)
        _ctx_1024c = jax.random.dirichlet(jax.random.fold_in(_rk, 511), 0.3 * jnp.ones((16,), jnp.float32), (4, 512))
        _ctx_1024t = jnp.einsum('bsk,bkd->bsd', _ctx_1024c, _ctx_1024P)
        _ctx_1024t = _ctx_1024t * jax.lax.rsqrt(jnp.mean(jnp.square(_ctx_1024t)) + 1e-12) * 0.953939
        ctx_1024 = 2.81802e-05 + 1.00001 * (_ctx_1024t + 0.3 * jax.random.normal(jax.random.fold_in(_rk, 611), (4, 512, 256), jnp.float32))
        return (x, ctx_1024)
    x, ctx_1024 = _rec_inputs()

    def _L0_attn_setup():
        import jax, jax.numpy as jnp
        import numpy as np
        HIDDEN = 512
        NUM_HEADS = 16
        NUM_KV_HEADS = 4
        HEAD_DIM = HIDDEN // NUM_HEADS
        Q_PER_KV = NUM_HEADS // NUM_KV_HEADS
        GROUP_SIZE = (Q_PER_KV + 2) * HEAD_DIM
        TOTAL_PROJ = NUM_KV_HEADS * GROUP_SIZE
        SEQ, BATCH = (512, 2)
        key = jax.random.key(seed)
        k1, k2, k3 = jax.random.split(key, 3)
        x = jax.random.normal(k1, (SEQ, BATCH, HIDDEN), dtype=jnp.float32)
        weight_qkv = jax.random.normal(k2, (TOTAL_PROJ, HIDDEN), dtype=jnp.float32) * 0.02
        weight_proj = jax.random.normal(k3, (HIDDEN, NUM_HEADS * HEAD_DIM), dtype=jnp.float32) * 0.02
        return {'x': x, 'weight_qkv': weight_qkv, 'weight_proj': weight_proj}
    _L0_attn_all = _L0_attn_setup()
    _L0_attn_in = {k: v for k, v in _L0_attn_all.items() if k in ('weight_qkv', 'weight_proj')}
    del _L0_attn_all

    def _L0_xattn_setup():
        import jax, jax.numpy as jnp
        import numpy as np
        key = jax.random.key(seed)
        ks = jax.random.split(key, 6)
        B, L, N, C, D = (8, 128, 512, 256, 128)
        return {'teacher_logits': jax.random.normal(ks[0], (B, L, N), dtype=jnp.float32), 'teacher_features': jax.random.normal(ks[1], (B, N, C), dtype=jnp.float32), 'Wq': jax.random.normal(ks[2], (D, C), dtype=jnp.float32) * (1.0 / np.sqrt(C)), 'bq': jnp.zeros((D,), dtype=jnp.float32), 'Wk': jax.random.normal(ks[3], (D, C), dtype=jnp.float32) * (1.0 / np.sqrt(C)), 'bk': jnp.zeros((D,), dtype=jnp.float32)}
    _L0_xattn_all = _L0_xattn_setup()
    _L0_xattn_in = {k: v for k, v in _L0_xattn_all.items() if k in ('Wq', 'bq', 'Wk', 'bk')}
    del _L0_xattn_all

    def _L0_ffn_setup():
        import jax, jax.numpy as jnp
        import numpy as np

        def _sparsify_2to4(h):
            B, S, I = h.shape
            g = h.reshape(B, S, I // 4, 4)
            a = jnp.abs(g)
            _, idx = jax.lax.top_k(a, 2)
            pos = jnp.arange(4)
            mask = (pos == idx[..., 0:1]) | (pos == idx[..., 1:2])
            return (g * mask.astype(g.dtype)).reshape(B, S, I)
        key = jax.random.key(seed)
        k1, k2, k3, k4 = jax.random.split(key, 4)
        B, S, H, I = (4, 512, 512, 2048)
        x = jax.random.normal(k1, (B, S, H), dtype=jnp.float32)
        w_gate = jax.random.normal(k2, (H, I), dtype=jnp.float32) / np.sqrt(H)
        w_up = jax.random.normal(k3, (H, I), dtype=jnp.float32) / np.sqrt(H)
        w_down = jax.random.normal(k4, (I, H), dtype=jnp.float32) / np.sqrt(I)
        return {'x': x, 'w_gate': w_gate, 'w_up': w_up, 'w_down': w_down}
    _L0_ffn_all = _L0_ffn_setup()
    _L0_ffn_in = {k: v for k, v in _L0_ffn_all.items() if k in ('w_gate', 'w_up', 'w_down')}
    del _L0_ffn_all

    def _L1_attn_setup():
        import jax, jax.numpy as jnp
        import numpy as np
        H, DN, DR, DV, QL, KVL = (16, 128, 64, 128, 384, 128)
        LN_EPS = 1e-05
        ROPE_BASE = 10000.0

        def _ln(x, g, b):
            mu = jnp.mean(x, axis=-1, keepdims=True)
            d = x - mu
            var = jnp.mean(d * d, axis=-1, keepdims=True)
            return d * jax.lax.rsqrt(var + LN_EPS) * g + b

        def _rope(x, cos, sin):
            x1, x2 = (x[..., 0::2], x[..., 1::2])
            r = jnp.stack([x1 * cos - x2 * sin, x1 * sin + x2 * cos], axis=-1)
            return r.reshape(x.shape)

        def _reference_tuple_inner(x, Wq_down, q_ln_g, q_ln_b, Wq_up, bq_up, Wkv_down, kv_ln_g, kv_ln_b, Wkv_up, bkv_up, Wo):
            B, T, C = x.shape
            pos = jnp.arange(T, dtype=jnp.float32)
            inv_freq = 1.0 / ROPE_BASE ** (jnp.arange(0, DR, 2, dtype=jnp.float32) / DR)
            ang = pos[:, None] * inv_freq
            cos, sin = (jnp.cos(ang), jnp.sin(ang))
            cq = _ln(x @ Wq_down.T, q_ln_g, q_ln_b)
            q = (cq @ Wq_up.T + bq_up).reshape(B, T, H, DN + DR).transpose(0, 2, 1, 3)
            q_nope, q_rope = (q[..., :DN], q[..., DN:])
            q_rope = _rope(q_rope, cos, sin)
            kv = x @ Wkv_down.T
            c_kv = _ln(kv[..., :KVL], kv_ln_g, kv_ln_b)
            k_rope = _rope(kv[..., KVL:], cos, sin)
            new_kr_cache = jnp.concatenate([c_kv, k_rope], axis=-1)
            kvu = (c_kv @ Wkv_up.T + bkv_up).reshape(B, T, H, DN + DV).transpose(0, 2, 1, 3)
            k_nope, v = (kvu[..., :DN], kvu[..., DN:])
            q_full = jnp.concatenate([q_nope, q_rope], axis=-1)
            k_full = jnp.concatenate([k_nope, jnp.broadcast_to(k_rope[:, None], (B, H, T, DR))], axis=-1)
            scores = jnp.einsum('bhqd,bhkd->bhqk', q_full, k_full) / float(np.sqrt(DN + DR))
            attn = jax.nn.softmax(scores, axis=-1)
            out = jnp.einsum('bhqk,bhkd->bhqd', attn, v)
            out = out.transpose(0, 2, 1, 3).reshape(B, T, H * DV)
            return (out @ Wo.T, new_kr_cache)
        key = jax.random.key(seed)
        ks = jax.random.split(key, 8)
        s = 0.02
        B, T, C = (2, 512, 512)
        return {'x': jax.random.normal(ks[0], (B, T, C), jnp.float32), 'Wq_down': jax.random.normal(ks[1], (QL, C), jnp.float32) * s, 'q_ln_g': jnp.ones((QL,), jnp.float32), 'q_ln_b': jnp.zeros((QL,), jnp.float32), 'Wq_up': jax.random.normal(ks[2], (H * (DN + DR), QL), jnp.float32) * s, 'bq_up': jax.random.normal(ks[3], (H * (DN + DR),), jnp.float32) * s, 'Wkv_down': jax.random.normal(ks[4], (KVL + DR, C), jnp.float32) * s, 'kv_ln_g': jnp.ones((KVL,), jnp.float32), 'kv_ln_b': jnp.zeros((KVL,), jnp.float32), 'Wkv_up': jax.random.normal(ks[5], (H * (DN + DV), KVL), jnp.float32) * s, 'bkv_up': jax.random.normal(ks[6], (H * (DN + DV),), jnp.float32) * s, 'Wo': jax.random.normal(ks[7], (C, H * DV), jnp.float32) * s}
    _L1_attn_all = _L1_attn_setup()
    _L1_attn_in = {k: v for k, v in _L1_attn_all.items() if k in ('Wq_down', 'q_ln_g', 'q_ln_b', 'Wq_up', 'bq_up', 'Wkv_down', 'kv_ln_g', 'kv_ln_b', 'Wkv_up', 'bkv_up', 'Wo')}
    del _L1_attn_all

    def _L1_xattn_setup():
        import jax, jax.numpy as jnp
        import numpy as np
        B_, L_, D_MODEL = (4, 512, 256)
        D_STATE, D_CONV, EXPAND = (16, 4, 2)
        D_INNER = EXPAND * D_MODEL
        DT_RANK = (D_MODEL + 15) // 16

        def silu(x):
            return x * jax.nn.sigmoid(x)
        key = jax.random.key(seed)
        ks = jax.random.split(key, 10)
        f32 = jnp.float32
        hidden_states = jax.random.normal(ks[0], (B_, L_, D_MODEL), dtype=f32)
        z = jax.random.normal(ks[1], (B_, D_INNER, L_), dtype=f32)
        in_proj_w = jax.random.normal(ks[2], (D_INNER, D_MODEL), dtype=f32) * 0.02
        conv_w = jax.random.normal(ks[3], (D_INNER, 1, D_CONV), dtype=f32) * 0.1
        conv_b = jax.random.normal(ks[4], (D_INNER,), dtype=f32) * 0.02
        x_proj_w = jax.random.normal(ks[5], (DT_RANK + 2 * D_STATE, D_INNER), dtype=f32) * 0.02
        dt_proj_w = jax.random.uniform(ks[6], (D_INNER, DT_RANK), dtype=f32, minval=-DT_RANK ** (-0.5), maxval=DT_RANK ** (-0.5))
        dt = jnp.exp(jax.random.uniform(ks[7], (D_INNER,), dtype=f32, minval=np.log(0.001), maxval=np.log(0.1)))
        dt_proj_b = jnp.log(jnp.expm1(dt))
        A_log = jnp.log(jnp.broadcast_to(jnp.arange(1, D_STATE + 1, dtype=f32), (D_INNER, D_STATE)))
        D = jnp.ones((D_INNER,), f32)
        return {'hidden_states': hidden_states, 'z': z, 'in_proj_w': in_proj_w, 'conv_w': conv_w, 'conv_b': conv_b, 'x_proj_w': x_proj_w, 'dt_proj_w': dt_proj_w, 'dt_proj_b': dt_proj_b, 'A_log': A_log, 'D': D}
    _L1_xattn_all = _L1_xattn_setup()
    _L1_xattn_in = {k: v for k, v in _L1_xattn_all.items() if k in ('in_proj_w', 'conv_w', 'conv_b', 'x_proj_w', 'dt_proj_w', 'dt_proj_b', 'A_log', 'D')}
    del _L1_xattn_all

    def _L1_ffn_setup():
        import jax, jax.numpy as jnp
        import numpy as np
        D_MODEL = 512
        HIDDEN = 1408
        BATCH, SEQ = (4, 512)

        def _activation_quant(x):
            scale = 127.0 / jnp.clip(jnp.max(jnp.abs(x), axis=-1, keepdims=True), 1e-05, None)
            xq = jnp.clip(jnp.round(x * scale), -128.0, 127.0) / scale
            return x + jax.lax.stop_gradient(xq - x)

        def _weight_quant(w):
            scale = 1.0 / jnp.clip(jnp.mean(jnp.abs(w)), 1e-05, None)
            wq = jnp.clip(jnp.round(w * scale), -1.0, 1.0) / scale
            return w + jax.lax.stop_gradient(wq - w)

        def _bitlinear(x, w):
            return jnp.einsum('bsi,oi->bso', _activation_quant(x), _weight_quant(w))
        key = jax.random.key(seed)
        kx, k1, k2, k3 = jax.random.split(key, 4)
        x = jax.random.normal(kx, (BATCH, SEQ, D_MODEL), dtype=jnp.float32)
        w1 = jax.random.normal(k1, (HIDDEN, D_MODEL), dtype=jnp.float32) * 0.02
        w2 = jax.random.normal(k2, (HIDDEN, D_MODEL), dtype=jnp.float32) * 0.02
        w3 = jax.random.normal(k3, (D_MODEL, HIDDEN), dtype=jnp.float32) * 0.02
        return {'x': x, 'w1': w1, 'w2': w2, 'w3': w3}
    _L1_ffn_all = _L1_ffn_setup()
    _L1_ffn_in = {k: v for k, v in _L1_ffn_all.items() if k in ('w1', 'w2', 'w3')}
    del _L1_ffn_all
    return {'x': x, 'ctx_1024': ctx_1024, 'L0_attn_weight_qkv': _L0_attn_in['weight_qkv'], 'L0_attn_weight_proj': _L0_attn_in['weight_proj'], 'L0_xattn_Wq': _L0_xattn_in['Wq'], 'L0_xattn_bq': _L0_xattn_in['bq'], 'L0_xattn_Wk': _L0_xattn_in['Wk'], 'L0_xattn_bk': _L0_xattn_in['bk'], 'L0_ffn_w_gate': _L0_ffn_in['w_gate'], 'L0_ffn_w_up': _L0_ffn_in['w_up'], 'L0_ffn_w_down': _L0_ffn_in['w_down'], 'L1_attn_Wq_down': _L1_attn_in['Wq_down'], 'L1_attn_q_ln_g': _L1_attn_in['q_ln_g'], 'L1_attn_q_ln_b': _L1_attn_in['q_ln_b'], 'L1_attn_Wq_up': _L1_attn_in['Wq_up'], 'L1_attn_bq_up': _L1_attn_in['bq_up'], 'L1_attn_Wkv_down': _L1_attn_in['Wkv_down'], 'L1_attn_kv_ln_g': _L1_attn_in['kv_ln_g'], 'L1_attn_kv_ln_b': _L1_attn_in['kv_ln_b'], 'L1_attn_Wkv_up': _L1_attn_in['Wkv_up'], 'L1_attn_bkv_up': _L1_attn_in['bkv_up'], 'L1_attn_Wo': _L1_attn_in['Wo'], 'L1_xattn_in_proj_w': _L1_xattn_in['in_proj_w'], 'L1_xattn_conv_w': _L1_xattn_in['conv_w'], 'L1_xattn_conv_b': _L1_xattn_in['conv_b'], 'L1_xattn_x_proj_w': _L1_xattn_in['x_proj_w'], 'L1_xattn_dt_proj_w': _L1_xattn_in['dt_proj_w'], 'L1_xattn_dt_proj_b': _L1_xattn_in['dt_proj_b'], 'L1_xattn_A_log': _L1_xattn_in['A_log'], 'L1_xattn_D': _L1_xattn_in['D'], 'L1_ffn_w1': _L1_ffn_in['w1'], 'L1_ffn_w2': _L1_ffn_in['w2'], 'L1_ffn_w3': _L1_ffn_in['w3']}

def reference(x, ctx_1024, L0_attn_weight_qkv, L0_attn_weight_proj, L0_xattn_Wq, L0_xattn_bq, L0_xattn_Wk, L0_xattn_bk, L0_ffn_w_gate, L0_ffn_w_up, L0_ffn_w_down, L1_attn_Wq_down, L1_attn_q_ln_g, L1_attn_q_ln_b, L1_attn_Wq_up, L1_attn_bq_up, L1_attn_Wkv_down, L1_attn_kv_ln_g, L1_attn_kv_ln_b, L1_attn_Wkv_up, L1_attn_bkv_up, L1_attn_Wo, L1_xattn_in_proj_w, L1_xattn_conv_w, L1_xattn_conv_b, L1_xattn_x_proj_w, L1_xattn_dt_proj_w, L1_xattn_dt_proj_b, L1_xattn_A_log, L1_xattn_D, L1_ffn_w1, L1_ffn_w2, L1_ffn_w3):
    import jax
    import jax.numpy as jnp

    def _L0_attn_ref(x, weight_qkv, weight_proj):
        import jax, jax.numpy as jnp
        import numpy as np
        HIDDEN = 512
        NUM_HEADS = 16
        NUM_KV_HEADS = 4
        HEAD_DIM = HIDDEN // NUM_HEADS
        Q_PER_KV = NUM_HEADS // NUM_KV_HEADS
        GROUP_SIZE = (Q_PER_KV + 2) * HEAD_DIM
        TOTAL_PROJ = NUM_KV_HEADS * GROUP_SIZE
        SEQ, BATCH = (512, 2)
        seq, batch, hidden = x.shape
        q_size = Q_PER_KV * HEAD_DIM
        qkv = x.reshape(-1, hidden) @ weight_qkv.T
        qkv = qkv.reshape(-1, NUM_KV_HEADS, GROUP_SIZE)
        q = qkv[:, :, :q_size].reshape(seq, batch, NUM_HEADS, HEAD_DIM)
        k = qkv[:, :, q_size:q_size + HEAD_DIM].reshape(seq, batch, NUM_KV_HEADS, HEAD_DIM)
        v = qkv[:, :, q_size + HEAD_DIM:].reshape(seq, batch, NUM_KV_HEADS, HEAD_DIM)
        k = jnp.repeat(k, Q_PER_KV, axis=2)
        v = jnp.repeat(v, Q_PER_KV, axis=2)
        q = q.transpose(1, 2, 0, 3)
        k = k.transpose(1, 2, 0, 3)
        v = v.transpose(1, 2, 0, 3)
        scale = 1.0 / np.sqrt(HEAD_DIM)
        scores = jnp.einsum('bhqd,bhkd->bhqk', q, k) * scale
        causal = jnp.tril(jnp.ones((seq, seq), dtype=bool))
        scores = jnp.where(causal, scores, jnp.float32(-jnp.inf))
        probs = jax.nn.softmax(scores, axis=-1)
        attn = jnp.einsum('bhqk,bhkd->bhqd', probs, v)
        attn = attn.transpose(2, 0, 1, 3).reshape(seq * batch, NUM_HEADS * HEAD_DIM)
        out = attn @ weight_proj.T
        return out.reshape(seq, batch, hidden)

    def _L0_xattn_ref(teacher_logits, teacher_features, Wq, bq, Wk, bk):
        import jax, jax.numpy as jnp
        import numpy as np
        query = jnp.einsum('bnc,dc->bnd', teacher_features, Wq) + bq
        key = jnp.einsum('bnc,dc->bnd', teacher_features, Wk) + bk
        energy = jnp.einsum('bnd,bmd->bnm', query, key)
        attention = jax.nn.softmax(energy, axis=-1)
        x_m = jnp.einsum('bln,bmn->blm', teacher_logits, attention)
        return x_m

    def _L0_ffn_ref(x, w_gate, w_up, w_down):
        import jax, jax.numpy as jnp
        import numpy as np

        def _sparsify_2to4(h):
            B, S, I = h.shape
            g = h.reshape(B, S, I // 4, 4)
            a = jnp.abs(g)
            _, idx = jax.lax.top_k(a, 2)
            pos = jnp.arange(4)
            mask = (pos == idx[..., 0:1]) | (pos == idx[..., 1:2])
            return (g * mask.astype(g.dtype)).reshape(B, S, I)
        h = jax.nn.silu(jnp.einsum('bsh,hi->bsi', x, w_gate)) * jnp.einsum('bsh,hi->bsi', x, w_up)
        h_sparse = _sparsify_2to4(h)
        return jnp.einsum('bsi,ih->bsh', h_sparse, w_down)

    def _L1_attn_ref(x, Wq_down, q_ln_g, q_ln_b, Wq_up, bq_up, Wkv_down, kv_ln_g, kv_ln_b, Wkv_up, bkv_up, Wo):
        import jax, jax.numpy as jnp
        import numpy as np
        H, DN, DR, DV, QL, KVL = (16, 128, 64, 128, 384, 128)
        LN_EPS = 1e-05
        ROPE_BASE = 10000.0

        def _ln(x, g, b):
            mu = jnp.mean(x, axis=-1, keepdims=True)
            d = x - mu
            var = jnp.mean(d * d, axis=-1, keepdims=True)
            return d * jax.lax.rsqrt(var + LN_EPS) * g + b

        def _rope(x, cos, sin):
            x1, x2 = (x[..., 0::2], x[..., 1::2])
            r = jnp.stack([x1 * cos - x2 * sin, x1 * sin + x2 * cos], axis=-1)
            return r.reshape(x.shape)

        def _reference_tuple_inner(x, Wq_down, q_ln_g, q_ln_b, Wq_up, bq_up, Wkv_down, kv_ln_g, kv_ln_b, Wkv_up, bkv_up, Wo):
            B, T, C = x.shape
            pos = jnp.arange(T, dtype=jnp.float32)
            inv_freq = 1.0 / ROPE_BASE ** (jnp.arange(0, DR, 2, dtype=jnp.float32) / DR)
            ang = pos[:, None] * inv_freq
            cos, sin = (jnp.cos(ang), jnp.sin(ang))
            cq = _ln(x @ Wq_down.T, q_ln_g, q_ln_b)
            q = (cq @ Wq_up.T + bq_up).reshape(B, T, H, DN + DR).transpose(0, 2, 1, 3)
            q_nope, q_rope = (q[..., :DN], q[..., DN:])
            q_rope = _rope(q_rope, cos, sin)
            kv = x @ Wkv_down.T
            c_kv = _ln(kv[..., :KVL], kv_ln_g, kv_ln_b)
            k_rope = _rope(kv[..., KVL:], cos, sin)
            new_kr_cache = jnp.concatenate([c_kv, k_rope], axis=-1)
            kvu = (c_kv @ Wkv_up.T + bkv_up).reshape(B, T, H, DN + DV).transpose(0, 2, 1, 3)
            k_nope, v = (kvu[..., :DN], kvu[..., DN:])
            q_full = jnp.concatenate([q_nope, q_rope], axis=-1)
            k_full = jnp.concatenate([k_nope, jnp.broadcast_to(k_rope[:, None], (B, H, T, DR))], axis=-1)
            scores = jnp.einsum('bhqd,bhkd->bhqk', q_full, k_full) / float(np.sqrt(DN + DR))
            attn = jax.nn.softmax(scores, axis=-1)
            out = jnp.einsum('bhqk,bhkd->bhqd', attn, v)
            out = out.transpose(0, 2, 1, 3).reshape(B, T, H * DV)
            return (out @ Wo.T, new_kr_cache)
        return _reference_tuple_inner(x, Wq_down, q_ln_g, q_ln_b, Wq_up, bq_up, Wkv_down, kv_ln_g, kv_ln_b, Wkv_up, bkv_up, Wo)[0]

    def _L1_xattn_ref(hidden_states, z, in_proj_w, conv_w, conv_b, x_proj_w, dt_proj_w, dt_proj_b, A_log, D):
        import jax, jax.numpy as jnp
        import numpy as np
        B_, L_, D_MODEL = (4, 512, 256)
        D_STATE, D_CONV, EXPAND = (16, 4, 2)
        D_INNER = EXPAND * D_MODEL
        DT_RANK = (D_MODEL + 15) // 16

        def silu(x):
            return x * jax.nn.sigmoid(x)
        Bsz, L, _ = hidden_states.shape
        d_inner, _, d_conv = conv_w.shape
        dt_rank = dt_proj_w.shape[1]
        d_state = A_log.shape[1]
        x = jnp.einsum('bld,ed->bel', hidden_states, in_proj_w)
        xc = jax.lax.conv_general_dilated(x, conv_w, window_strides=(1,), padding=[(d_conv - 1, 0)], feature_group_count=d_inner, dimension_numbers=('NCH', 'OIH', 'NCH'))
        x = silu(xc + conv_b[None, :, None])
        x_dbl = jnp.einsum('bdl,ed->bel', x, x_proj_w)
        dt_low, Bm, Cm = jnp.split(x_dbl, [dt_rank, dt_rank + d_state], axis=1)
        dt = jnp.einsum('brl,dr->bdl', dt_low, dt_proj_w)
        dt = jax.nn.softplus(dt + dt_proj_b[None, :, None])
        A = -jnp.exp(A_log)
        dt_t = jnp.moveaxis(dt, -1, 0)
        B_t = jnp.moveaxis(Bm, -1, 0)
        C_t = jnp.moveaxis(Cm, -1, 0)
        u_t = jnp.moveaxis(x, -1, 0)

        def step(state, inp):
            d, b, c, u = inp
            dA = jnp.exp(d[..., None] * A)
            state = state * dA + (d * u)[..., None] * b[:, None, :]
            y = jnp.einsum('bdn,bn->bd', state, c)
            return (state, y)
        state0 = jnp.zeros((Bsz, d_inner, d_state), x.dtype)
        _, ys = jax.lax.scan(step, state0, (dt_t, B_t, C_t, u_t))
        y = jnp.moveaxis(ys, 0, 2)
        y = y + D[None, :, None] * x
        y = y * silu(z)
        return jnp.swapaxes(y, 1, 2)

    def _L1_ffn_ref(x, w1, w2, w3):
        import jax, jax.numpy as jnp
        import numpy as np
        D_MODEL = 512
        HIDDEN = 1408
        BATCH, SEQ = (4, 512)

        def _activation_quant(x):
            scale = 127.0 / jnp.clip(jnp.max(jnp.abs(x), axis=-1, keepdims=True), 1e-05, None)
            xq = jnp.clip(jnp.round(x * scale), -128.0, 127.0) / scale
            return x + jax.lax.stop_gradient(xq - x)

        def _weight_quant(w):
            scale = 1.0 / jnp.clip(jnp.mean(jnp.abs(w)), 1e-05, None)
            wq = jnp.clip(jnp.round(w * scale), -1.0, 1.0) / scale
            return w + jax.lax.stop_gradient(wq - w)

        def _bitlinear(x, w):
            return jnp.einsum('bsi,oi->bso', _activation_quant(x), _weight_quant(w))
        h = jax.nn.silu(_bitlinear(x, w1)) * _bitlinear(x, w2)
        return _bitlinear(h, w3)
    x = x + _L0_attn_ref(_layernorm(x, axis=-1), L0_attn_weight_qkv, L0_attn_weight_proj)
    x = x + _L0_xattn_ref(_layernorm(x, axis=-1), ctx_1024, L0_xattn_Wq, L0_xattn_bq, L0_xattn_Wk, L0_xattn_bk)
    x = x + _L0_ffn_ref(_layernorm(x, axis=-1), L0_ffn_w_gate, L0_ffn_w_up, L0_ffn_w_down)
    x = x + _L1_attn_ref(_layernorm(x, axis=-1), L1_attn_Wq_down, L1_attn_q_ln_g, L1_attn_q_ln_b, L1_attn_Wq_up, L1_attn_bq_up, L1_attn_Wkv_down, L1_attn_kv_ln_g, L1_attn_kv_ln_b, L1_attn_Wkv_up, L1_attn_bkv_up, L1_attn_Wo)
    x = x + _L1_xattn_ref(ctx_1024, _layernorm(x, axis=-1), L1_xattn_in_proj_w, L1_xattn_conv_w, L1_xattn_conv_b, L1_xattn_x_proj_w, L1_xattn_dt_proj_w, L1_xattn_dt_proj_b, L1_xattn_A_log, L1_xattn_D)
    x = x + _L1_ffn_ref(_layernorm(x, axis=-1), L1_ffn_w1, L1_ffn_w2, L1_ffn_w3)
    return x

_drawn_inputs = setup_inputs


def setup_inputs(seed=0):
    import zlib

    import numpy as np

    out = dict(_drawn_inputs(seed))
    spreads = {'L0_xattn_bq': (0.0, 0.1),
     'L0_xattn_bk': (0.0, 0.8),
     'L1_attn_q_ln_g': (1.0, 0.6),
     'L1_attn_q_ln_b': (0.0, 0.8),
     'L1_attn_kv_ln_g': (1.0, 0.6),
     'L1_attn_kv_ln_b': (0.0, 0.573),
     'L1_xattn_D': (1.0, 0.6)}
    factors = {'L1_attn_Wq_down': 8.0,
     'L1_attn_Wq_up': 8.0,
     'L1_attn_bq_up': 8.0,
     'L1_attn_Wkv_down': 7.026,
     'L1_attn_Wkv_up': 3.492,
     'L1_attn_bkv_up': 4.451,
     'L1_attn_Wo': 2.73,
     'L1_xattn_in_proj_w': 4.166,
     'L1_xattn_conv_w': 4.253,
     'L1_xattn_conv_b': 8.0,
     'L1_xattn_x_proj_w': 8.0,
     'L1_xattn_dt_proj_w': 8.0,
     'L1_xattn_dt_proj_b': 8.0,
     'L1_xattn_A_log': 8.0,
     'L1_ffn_w1': 3.225,
     'L1_ffn_w2': 2.971,
     'L1_ffn_w3': 2.981}
    for name, (base, spread) in spreads.items():
        noise = np.random.default_rng([zlib.crc32(name.encode()), seed]).standard_normal(out[name].shape)
        drawn = base * np.exp(spread * noise) if base else spread * noise
        out[name] = jnp.asarray(drawn.astype(out[name].dtype))
    for name, factor in factors.items():
        out[name] = (out[name] * factor).astype(out[name].dtype)
    return out
```

```python
from contextlib import ExitStack

import concourse.bass as bass
from concourse import mybir

F32 = mybir.dt.float32
F32R = mybir.dt.float32r
BF16 = mybir.dt.bfloat16
ALU = mybir.AluOpType
ACT = mybir.ActivationFunctionType
AX_X = mybir.AxisListType.X

P = 128
NB = 4
NT = 512
NP = NT // P
D = 512
KD = D // P
EPS = 1e-5

H0, KV0, DH0 = 16, 4, 32
R0 = H0 // KV0
QKV0 = H0 * DH0 + 2 * KV0 * DH0
DC = 256
KC = DC // P
DI = 512
CT = DI // P
NS = 16
DTR = 16
NCONV = 4
SMALL = 2.0 ** -7
FF0 = 2048
C0 = FF0 // (4 * P)
PIECE = 2 * KD * P + D
H1, DN, DR, DV, QL, KVL = 16, 128, 64, 128, 384, 128
KQ = QL // P
PAIRS = H1 // 2
WQ1, WKV1, WO1 = KQ * 4 * P, 4 * P, 2 * D
WPAIR = WQ1 + WKV1 + WO1
SCALE1 = float((DN + DR) ** -0.5)
FF1 = 1408
KF1 = FF1 // P
MAGIC = 12582912.0


class State:
    pass


def clear_semaphores(nc, handles):
    nc.clear_and_free_semaphores(handles)
    with nc.Block():
        pass


def tensors(nc, ctx):
    handles = []
    ctx.callback(clear_semaphores, nc, handles)

    def sb(name, shape, dt=F32):
        return ctx.enter_context(nc.sbuf_tensor(name, shape, dt))

    def ps(name, shape, dt=F32):
        return ctx.enter_context(nc.psum_tensor(name, shape, dt))

    def sems(prefix, names):
        made = {n: nc.alloc_semaphore(f"{prefix}_{n}") for n in names.split()}
        handles.extend(made.values())
        return made

    return sb, ps, sems


def mm3(pe, out, a, b, start=True, stop=True):
    pe.matmul(out, a[0], b[0], start=start, stop=False)
    pe.matmul(out, a[0], b[1], start=False, stop=False)
    return pe.matmul(out, a[1], b[0], start=False, stop=stop)


def lo_part(dve, out, full, hi):
    return dve.tensor_tensor(out, full, hi.bitcast(F32), ALU.subtract)


def ln_semaphores(sems, prefix):
    return sems(prefix, "stats passed var sd rstd norm xt hi lo")


def ln_dve_normalise(dve, s, tiles, stats, mv, sd, rstd, xn, count, first, width=D):
    n = len(tiles)
    for k, tile in enumerate(tiles):
        last = dve.bn_stats(stats[:, k, :], tile)
    last.then_inc(s["stats"], 1)
    dve.wait_ge(s["stats"], count + 1)
    dve.sem_inc(s["passed"], 1)
    for k in range(n):
        last = dve.bn_aggr(mv[:, k, :], stats[:, k, :])
    last.then_inc(s["var"], 1)
    dve.wait_ge(s["sd"], count + 1)
    dve.reciprocal(rstd[:, 0:n], sd[:, 0:n]).then_inc(s["rstd"], 1)
    dve.wait_ge(s["rstd"], count + 1)
    if first is not None:
        dve.wait_ge(s["xt"], first)
    for k, tile in enumerate(tiles):
        dve.tensor_scalar(xn[:, k, :], tile, mv[:, k, 0:1], rstd[:, k:k + 1], ALU.subtract,
                          ALU.mult).then_inc(s["norm"], 1)


def ln_act_sqrt(act, s, mv, sd, eps, n, count):
    act.wait_ge(s["var"], count + 1)
    act.activation(sd[:, 0:n], mv[:, 0:n, 1], ACT.Sqrt, bias=eps[:, 0:1]).then_inc(s["sd"], 1)


def stage_context(nc, g):
    with ExitStack() as ctx:
        sb, ps, sems = tensors(nc, ctx)
        s = sems("ctx", "load consts w_hi w_lo c_load c_hi c_lo q_ps k_ps q_hi k_hi qk_lo x_ps x_in x_used "
                        "e_ps e_max e_exp e_rec a_norm a_ps a_hi a_lo t1 t2 t3 conv u u_hi u_lo xd_ps d_hi d_lo bc dt_ps "
                        "dt_abs dt_exp dt_ln dt_relu dt_sum ser dt st_u st_bc st_dt pad")
        craw = sb("ctx_raw", [P, KC, NT])
        c = sb("ctx_split", [P, 2, KC, NT], F32R)
        wraw = sb("ctx_wraw", [P, g.dram["ctx_w"].shape[1]])
        w = sb("ctx_w", [P, 2, g.dram["ctx_w"].shape[1]], F32R)
        dtw_raw = sb("ctx_dtw_raw", [48, DI])
        dtw = sb("ctx_dtw", [48, 2, DI], F32R)
        small = sb("ctx_small", [P, 2 + CT * NCONV + 2 * CT])
        qk = sb("ctx_qk", [P, 2, 2, NT], F32R)
        e = sb("ctx_exp", [P, NP, NT])
        nmax, esum, erec = sb("ctx_nmax", [P, NP]), sb("ctx_esum", [P, NP]), sb("ctx_erec", [P, NP])
        xin = sb("ctx_xin", [P, CT, NT + NCONV - 1])
        ta, tb = sb("ctx_ta", [P, CT, NT]), sb("ctx_tb", [P, CT, NT])
        u = sb("ctx_u", [P, CT, NT])
        us = sb("ctx_us", [P, 2, CT, NT], F32R)
        dlow = sb("ctx_dlow", [48, 2, NT], F32R)
        bc = sb("ctx_bc", [32, NT])
        pa = [ps(f"ctx_p{k}", [P, NT]) for k in range(8)]

        CW = 2 * P + DI

        def wcol(k, a, n):
            return [w[:, h, k * CW + a:k * CW + a + n] for h in range(2)]

        def xproj(k):
            return [w[:, h, KC * CW + 48 * k:KC * CW + 48 * k + 48] for h in range(2)]

        conv_w = lambda ct, t: small[:, 2 + ct * NCONV + t:3 + ct * NCONV + t]
        conv_b = lambda ct: small[:, 2 + CT * NCONV + ct:3 + CT * NCONV + ct]
        dt_b = lambda ct: small[:, 2 + CT * (NCONV + 1) + ct:3 + CT * (NCONV + 1) + ct]

        with nc.Block() as block:
            @block.sync
            def _(sp):
                sp.dma_start(wraw[:], g.dram["ctx_w"]).then_inc(s["load"], 16)
                sp.dma_start(dtw_raw[32:48, :], g.dram["dt_w"]).then_inc(s["load"], 16)
                sp.dma_start(small[:], g.dram["ctx_small"]).then_inc(s["load"], 16)
                sp.dma_start(g.ident[:], g.dram["ident_in"]).then_inc(s["load"], 16)
                sp.dma_start(g.X[:, 0:2], g.x_in[:, 0:2]).then_inc(s["load"], 16)
                sp.dma_start(g.X[:, 2:4], g.x_in[:, 2:4]).then_inc(s["load"], 16)
                with sp.Fori(0, NB) as b:
                    sp.wait_ge(s["c_lo"], b)
                    sp.dma_start(craw[:], g.dram["ctx_in"][:, :, bass.ds(b * NT, NT)]).then_inc(s["c_load"], 16)
                    sp.wait_ge(s["u"], CT * b + CT)
                    sp.dma_start(g.u_dram[b], u[:]).then_inc(s["st_u"], 16)
                    sp.wait_ge(s["bc"], b + 1)
                    sp.dma_start(g.bc_dram[b], bc[:]).then_inc(s["st_bc"], 16)
                    sp.wait_ge(s["dt"], b + 1)
                    sp.dma_start(g.dt_dram[b], tb[:]).then_inc(s["st_dt"], 16)
                sp.wait_ge(s["st_u"], 16 * NB)
                sp.wait_ge(s["st_bc"], 16 * NB)
                sp.wait_ge(s["st_dt"], 16 * NB)
                sp.wait_ge(s["load"], 96)

            @block.scalar
            def _(act):
                act.wait_ge(s["load"], 96)
                act.copy(w[:, 0], wraw[:]).then_inc(s["w_hi"], 1)
                act.copy(dtw[32:48, 0], dtw_raw[32:48]).then_inc(s["w_hi"], 1)
                with act.Fori(0, NB) as b:
                    act.wait_ge(s["c_load"], 16 * b + 16)
                    act.wait_ge(s["x_ps"], CT * b)
                    act.copy(c[:, 0], craw[:]).then_inc(s["c_hi"], 1)
                    for n, (ready, done) in enumerate(((s["q_ps"], s["q_hi"]), (s["k_ps"], s["k_hi"]))):
                        act.wait_ge(ready, b + 1)
                        act.activation(qk[:, 0, n], pa[n][:], ACT.Identity, bias=small[:, n:n + 1]).then_inc(done, 1)
                    act.wait_ge(s["dt"], b)
                    act.wait_ge(s["pad"], 1)
                    for ct in range(CT):
                        act.wait_ge(s["x_ps"], CT * b + ct + 1)
                        act.copy(xin[:, ct, NCONV - 1:], pa[2 + ct][:]).then_inc(s["x_in"], 1)
                    act.wait_ge(s["a_ps"], NP * b)
                    for n in range(NP):
                        act.wait_ge(s["e_max"], NP * b + n + 1)
                        act.activation(e[:, n], pa[(6 + n) % 8][:], ACT.Exp, bias=nmax[:, n:n + 1],
                                       accum_out=esum[:, n:n + 1]).then_inc(s["e_exp"], 1)
                    act.wait_ge(s["st_u"], 16 * b)
                    act.wait_ge(s["u_lo"], CT * b)
                    for ct in range(CT):
                        act.wait_ge(s["conv"], CT * b + ct + 1)
                        act.activation(u[:, ct], tb[:, ct], ACT.Silu, bias=conv_b(ct)).then_inc(s["u"], 1)
                    for ct in range(CT):
                        act.wait_ge(s["u"], CT * b + ct + 1)
                        act.wait_ge(s["xd_ps"], b)
                        act.copy(us[:, 0, ct], u[:, ct]).then_inc(s["u_hi"], 1)
                    for n in range(NP):
                        act.wait_ge(s["a_ps"], NP * b + n + 1)
                        act.copy(g.A[:, 0, b, n], pa[n % 2][:]).then_inc(s["a_hi"], 1)
                    act.wait_ge(s["xd_ps"], b + 1)
                    act.wait_ge(s["dt_ps"], CT * b)
                    act.copy(dlow[32:48, 0], pa[2][32:48]).then_inc(s["d_hi"], 1)
                    act.wait_ge(s["st_bc"], 16 * b)
                    act.copy(bc[:], pa[2][0:32]).then_inc(s["bc"], 1)
                    for ct in range(CT):
                        act.wait_ge(s["dt_relu"], CT * b + ct + 1)
                        act.activation(ta[:, ct], pa[3 + ct][:], ACT.Abs, bias=dt_b(ct)).then_inc(s["dt_abs"], 1)
                    act.wait_ge(s["dt_abs"], CT * b + CT)
                    act.activation(ta[:], ta[:], ACT.Exp, scale=-1.0).then_inc(s["dt_exp"], 1)
                    act.wait_ge(s["dt_exp"], b + 1)
                    act.wait_ge(s["a_ps"], NP * b + NP)
                    act.activation(e[:], ta[:], ACT.Ln, bias=g.one[:, 0:1]).then_inc(s["dt_ln"], 1)

            @block.vector
            def _(dve):
                dve.memset(g.one[:], 1.0)
                dve.memset(g.eps[:], EPS)
                dve.memset(xin[:, :, 0:NCONV - 1], 0.0).then_inc(s["pad"], 1)
                dve.wait_ge(s["w_hi"], 2)
                lo_part(dve, w[:, 1], wraw[:], w[:, 0]).then_inc(s["w_lo"], 1)
                lo_part(dve, dtw[32:48, 1], dtw_raw[32:48], dtw[32:48, 0]).then_inc(s["w_lo"], 1)
                with dve.Fori(0, NB) as b:
                    dve.wait_ge(s["c_hi"], b + 1)
                    lo_part(dve, c[:, 1], craw[:], c[:, 0]).then_inc(s["c_lo"], 1)
                    for n, ready in enumerate((s["q_hi"], s["k_hi"])):
                        dve.wait_ge(ready, b + 1)
                        dve.scalar_tensor_tensor(out=qk[:, 1, n], in0=pa[n][:], scalar=small[:, n:n + 1],
                                                 in1=qk[:, 0, n].bitcast(F32), op0=ALU.add,
                                                 op1=ALU.subtract).then_inc(s["qk_lo"], 1)
                    for n in range(NP):
                        dve.wait_ge(s["e_ps"], NP * b + n + 1)
                        dve.tensor_reduce(nmax[:, n:n + 1], pa[(6 + n) % 8][:], AX_X, ALU.max,
                                          negate=True).then_inc(s["e_max"], 1)
                    dve.wait_ge(s["st_dt"], 16 * b)
                    dve.wait_ge(s["dt"], b)
                    for ct in range(CT):
                        k = CT * b + ct + 1
                        dve.wait_ge(s["x_in"], k)
                        dve.tensor_scalar(ta[:, ct], xin[:, ct, 0:NT], conv_w(ct, 0), None, ALU.mult).then_inc(s["t1"], 1)
                        for t, (src, dst, before, after) in enumerate(((ta, tb, s["t1"], s["t2"]), (tb, ta, s["t2"], s["t3"]),
                                                                       (ta, tb, s["t3"], s["conv"])), 1):
                            dve.wait_ge(before, k)
                            dve.scalar_tensor_tensor(out=dst[:, ct], in0=xin[:, ct, t:t + NT], scalar=conv_w(ct, t),
                                                     in1=src[:, ct], op0=ALU.mult, op1=ALU.add).then_inc(after, 1)
                    for ct in range(CT):
                        dve.wait_ge(s["u_hi"], CT * b + ct + 1)
                        lo_part(dve, us[:, 1, ct], u[:, ct], us[:, 0, ct]).then_inc(s["u_lo"], 1)
                    dve.wait_ge(s["e_exp"], NP * b + NP)
                    dve.reciprocal(erec[:], esum[:]).then_inc(s["e_rec"], 1)
                    dve.wait_ge(s["e_rec"], b + 1)
                    for n in range(NP):
                        dve.tensor_scalar(e[:, n], e[:, n], erec[:, n:n + 1], None, ALU.mult).then_inc(s["a_norm"], 1)
                    for n in range(NP):
                        dve.wait_ge(s["a_hi"], NP * b + n + 1)
                        lo_part(dve, g.A[:, 1, b, n], pa[n % 2][:], g.A[:, 0, b, n]).then_inc(s["a_lo"], 1)
                    dve.wait_ge(s["d_hi"], b + 1)
                    dve.wait_ge(s["bc"], b + 1)
                    lo_part(dve, dlow[32:48, 1], pa[2][32:48], dlow[32:48, 0]).then_inc(s["d_lo"], 1)
                    for ct in range(CT):
                        dve.wait_ge(s["dt_ps"], CT * b + ct + 1)
                        dve.tensor_scalar(tb[:, ct], pa[3 + ct][:], dt_b(ct), 0.0, ALU.add, ALU.max).then_inc(s["dt_relu"], 1)
                    series = xin[:, :, NCONV - 1:]
                    dve.wait_ge(s["dt_exp"], b + 1)
                    dve.tensor_scalar(series, ta[:], -0.25, 1.0 / 3.0, ALU.mult, ALU.add).then_inc(s["ser"], 1)
                    dve.wait_ge(s["ser"], 6 * b + 1)
                    dve.tensor_tensor(series, series, ta[:], ALU.mult).then_inc(s["ser"], 1)
                    for n, term in ((2, -0.5), (3, 1.0)):
                        for ct in range(CT):
                            dve.wait_ge(s["ser"], 6 * b + n)
                            last = dve.scalar_tensor_tensor(out=series[:, ct], in0=series[:, ct], scalar=term, in1=ta[:, ct],
                                                            op0=ALU.add, op1=ALU.mult)
                        last.then_inc(s["ser"], 1)
                    dve.wait_ge(s["dt_ln"], b + 1)
                    dve.wait_ge(s["ser"], 6 * b + 4)
                    dve.tensor_tensor(series, series, e[:], ALU.subtract).then_inc(s["ser"], 1)
                    dve.wait_ge(s["dt_relu"], CT * b + CT)
                    dve.tensor_tensor(tb[:], tb[:], e[:], ALU.add).then_inc(s["dt_sum"], 1)
                    dve.wait_ge(s["ser"], 6 * b + 5)
                    for ct in range(CT):
                        last = dve.scalar_tensor_tensor(out=series[:, ct], in0=ta[:, ct], scalar=SMALL, in1=series[:, ct],
                                                        op0=ALU.is_lt, op1=ALU.mult)
                    last.then_inc(s["ser"], 1)
                    dve.wait_ge(s["ser"], 6 * b + 6)
                    dve.wait_ge(s["dt_sum"], b + 1)
                    dve.tensor_tensor(tb[:], tb[:], series, ALU.add).then_inc(s["dt"], 1)

            @block.tensor
            def _(pe):
                pe.wait_ge(s["w_lo"], 2)
                with pe.Fori(0, NB) as b:
                    pe.wait_ge(s["c_lo"], b + 1)
                    cs = lambda k: [c[:, h, k] for h in range(2)]
                    pe.wait_ge(s["dt_relu"], CT * b)
                    pe.wait_ge(s["e_exp"], NP * b)
                    pe.wait_ge(s["bc"], b)
                    pe.wait_ge(s["a_lo"], NP * b)
                    for n, done in enumerate((s["q_ps"], s["k_ps"])):
                        for k in range(KC):
                            last = mm3(pe, pa[n][:], wcol(k, n * P, P), cs(k), k == 0, k == KC - 1)
                        last.then_inc(done, 1)
                    pe.wait_ge(s["dt_abs"], CT * b)
                    for ct in range(CT):
                        for k in range(KC):
                            last = mm3(pe, pa[2 + ct][:], wcol(k, (2 + ct) * P, P), cs(k), k == 0, k == KC - 1)
                        last.then_inc(s["x_ps"], 1)
                    pe.wait_ge(s["qk_lo"], 2 * b + 2)
                    for n in range(NP):
                        q = [qk[:, h, 0, n * P:(n + 1) * P] for h in range(2)]
                        last = mm3(pe, pa[(6 + n) % 8][:], q, [qk[:, h, 1] for h in range(2)]).then_inc(s["e_ps"], 1)
                    pe.wait_ge(s["x_in"], CT * b + CT)
                    pe.wait_ge(s["u_lo"], CT * b + CT)
                    for ct in range(CT):
                        last = mm3(pe, pa[2][0:48], xproj(ct), [us[:, h, ct] for h in range(2)], ct == 0, ct == CT - 1)
                    last.then_inc(s["xd_ps"], 1)
                    pe.wait_ge(s["a_norm"], NP * b + NP)
                    for n in range(NP):
                        pe.wait_ge(s["a_lo"], NP * b + max(0, n - 1))
                        for m in range(NP):
                            last = pe.transpose(pa[n % 2][:, m * P:(m + 1) * P], e[:, m, n * P:(n + 1) * P], g.ident[:])
                        last.then_inc(s["a_ps"], 1)
                    pe.wait_ge(s["d_lo"], b + 1)
                    for ct in range(CT):
                        mm3(pe, pa[3 + ct][:], [dtw[32:48, h, ct * P:(ct + 1) * P] for h in range(2)],
                            [dlow[32:48, h] for h in range(2)]).then_inc(s["dt_ps"], 1)


def ln_pe_transpose(pe, s, xn, banks, ident, n, base):
    for k in range(n):
        pe.wait_ge(s["norm"], base + k + 1)
        pe.wait_ge(s["lo"], base + max(0, k - 1))
        for c in range(KD):
            last = pe.transpose(banks[k % 2][:, c * P:(c + 1) * P], xn[:, k, c * P:(c + 1) * P], ident[:])
        last.then_inc(s["xt"], 1)


def ln_act_hi(act, s, xt, banks, n, base):
    for k in range(n):
        act.wait_ge(s["xt"], base + k + 1)
        act.copy(xt[:, 0, :, k * P:(k + 1) * P], banks[k % 2][:].rearrange("p (c t) -> p c t", c=KD)).then_inc(s["hi"], 1)


def ln_dve_lo(dve, s, xt, banks, n, base):
    for k in range(n):
        dve.wait_ge(s["hi"], base + k + 1)
        lo_part(dve, xt[:, 1, :, k * P:(k + 1) * P], banks[k % 2][:].rearrange("p (c t) -> p c t", c=KD),
                xt[:, 0, :, k * P:(k + 1) * P]).then_inc(s["lo"], 1)


def stage_attention0(nc, g):
    with ExitStack() as ctx:
        sb, ps, sems = tensors(nc, ctx)
        ln = ln_semaphores(sems, "att0_ln")
        s = sems("att0", "load w_hi w_lo qkv_ps qkv_in prod dot mx sub ex sm rc probs pv sum1 att at_ps at_hi at_lo o_ps x_add mask passed")
        NW = KD * QKV0
        wraw = sb("att0_wraw", [P, KD * (QKV0 + D)])
        w = sb("att0_w", [P, 2, KD * (QKV0 + D)], F32R)
        stats, mv = sb("att0_stats", [P, NB, 6]), sb("att0_mv", [P, NB, 2])
        sd, rstd = sb("att0_sd", [P, NB]), sb("att0_rstd", [P, NB])
        xn = sb("att0_xn", [P, NB, D])
        xt = sb("att0_xt", [P, 2, KD, NB * P], F32R)
        qkv = sb("att0_qkv", [P, NB, QKV0])
        prod = sb("att0_prod", [P, 2, D])
        score = sb("att0_score", [P, NB, H0, NB])
        shifted, probs = sb("att0_shifted", [P, NB, H0, NB]), sb("att0_probs", [P, NB, H0, NB])
        mx, sm, rc = (sb(f"att0_{n}", [P, NB * H0]) for n in ("mx", "sm", "rc"))
        pv = wraw[:, 0:2 * NB * D].rearrange("p (i j f) -> p i j f", i=2, j=NB)
        att, at = xn, xt
        tp = [ps(f"att0_tp{k}", [P, NT]) for k in range(2)]
        qp = [ps(f"att0_q{k}", [P, NT]) for k in range(2)]
        kp = [ps(f"att0_k{k}", [P, NT]) for k in range(2)]
        op = [ps(f"att0_o{k}", [P, NT]) for k in range(2)]
        pairs = [(i, j) for i in range(NB) for j in range(i + 1)]
        NPAIR = len(pairs)
        KO, VO = H0 * DH0, H0 * DH0 + KV0 * DH0

        def wslice(k, a, n):
            return [w[:, h, k * QKV0 + a:k * QKV0 + a + n] for h in range(2)]

        def wo(k):
            return [w[:, h, NW + k * D:NW + (k + 1) * D] for h in range(2)]

        def heads(t):
            return t.rearrange("p (g r d) -> p g r d", g=KV0, r=R0)

        def grouped(t):
            return t.rearrange("p (g r d) -> p g r d", g=KV0, r=1).to_broadcast([P, KV0, R0, DH0])

        with nc.Block() as block:
            @block.sync
            def _(sp):
                sp.dma_start(wraw[:], g.dram["att0_w"]).then_inc(s["load"], 16)

            @block.scalar
            def _(act):
                act.wait_ge(s["load"], 16)
                act.copy(w[:, 0], wraw[:]).then_inc(s["w_hi"], 1)
                with act.Fori(0, NP) as p:
                    ln_act_sqrt(act, ln, mv, sd, g.eps, NB, p)
                    act.wait_ge(s["o_ps"], NB * p)
                    ln_act_hi(act, ln, xt, tp, NB, NB * p)
                    act.wait_ge(s["pv"], NPAIR * p)
                    for b in range(NB):
                        act.wait_ge(s["qkv_ps"], NB * p + b + 1)
                        act.copy(qkv[:, b, 0:KO], qp[b % 2][:])
                        act.copy(qkv[:, b, KO:], kp[b % 2][:, 0:QKV0 - KO]).then_inc(s["qkv_in"], 1)
                    act.wait_ge(s["sub"], p + 1)
                    act.activation(probs[:], shifted[:], ACT.Exp, scale=float(DH0 ** -0.5)).then_inc(s["ex"], 1)
                    for i in range(NB):
                        act.wait_ge(s["at_ps"], NB * p + i + 1)
                        act.copy(at[:, 0, :, i * P:(i + 1) * P],
                                 tp[i % 2][:].rearrange("p (c t) -> p c t", c=KD)).then_inc(s["at_hi"], 1)

            @block.gpsimd
            def _(pool):
                with pool.Fori(0, NP) as p:
                    for n, (i, j) in enumerate(pairs):
                        pool.wait_ge(s["qkv_in"], NB * p + i + 1)
                        pool.wait_ge(s["dot"], NPAIR * p + max(0, n - 1))
                        pool.tensor_tensor(heads(prod[:, n % 2]), heads(qkv[:, i, 0:KO]), grouped(qkv[:, j, KO:VO]),
                                           ALU.mult).then_inc(s["prod"], 1)
                    for i in range(NB):
                        pool.wait_ge(s["pv"], NPAIR * p + (i + 1) * (i + 2) // 2)
                        pool.wait_ge(s["at_ps"], NB * p)
                        v = pv[:, i % 2]
                        if i == 0:
                            pool.sem_inc(s["passed"], 1)
                            pool.tensor_copy(att[:, 0], v[:, 0]).then_inc(s["att"], 1)
                        elif i == 1:
                            pool.tensor_tensor(att[:, 1], v[:, 0], v[:, 1], ALU.add).then_inc(s["att"], 1)
                        elif i == 2:
                            pool.tensor_tensor(v[:, 0], v[:, 0], v[:, 1], ALU.add).then_inc(s["sum1"], 1)
                            pool.wait_ge(s["sum1"], 3 * p + 1)
                            pool.tensor_tensor(att[:, 2], v[:, 0], v[:, 2], ALU.add).then_inc(s["att"], 1)
                        else:
                            pool.tensor_tensor(v[:, 0], v[:, 0], v[:, 1], ALU.add).then_inc(s["sum1"], 1)
                            pool.tensor_tensor(v[:, 2], v[:, 2], v[:, 3], ALU.add).then_inc(s["sum1"], 1)
                            pool.wait_ge(s["sum1"], 3 * p + 3)
                            pool.tensor_tensor(att[:, 3], v[:, 0], v[:, 2], ALU.add).then_inc(s["att"], 1)

            @block.vector
            def _(dve):
                dve.memset(score[:], -1e30).then_inc(s["mask"], 1)
                dve.wait_ge(s["w_hi"], 1)
                lo_part(dve, w[:, 1], wraw[:], w[:, 0]).then_inc(s["w_lo"], 1)
                dve.wait_ge(s["mask"], 1)
                with dve.Fori(0, NP) as p:
                    dve.wait_ge(s["at_ps"], NB * p)
                    ln_dve_normalise(dve, ln, [g.X[:, b, p, :] for b in range(NB)], stats, mv, sd, rstd, xn, p, NB * p)
                    ln_dve_lo(dve, ln, xt, tp, NB, NB * p)
                    for n, (i, j) in enumerate(pairs):
                        dve.wait_ge(s["prod"], NPAIR * p + n + 1)
                        dve.tensor_reduce(score[:, i, :, j], prod[:, n % 2].rearrange("p (h d) -> p h d", h=H0), AX_X,
                                          ALU.add).then_inc(s["dot"], 1)
                    flat = lambda t: t[:].rearrange("p i h j -> p (i h) j")
                    each = lambda t: t[:].rearrange("p (n o) -> p n o", o=1).to_broadcast([P, NB * H0, NB])
                    dve.wait_ge(s["dot"], NPAIR * (p + 1))
                    dve.tensor_reduce(mx[:], flat(score), AX_X, ALU.max).then_inc(s["mx"], 1)
                    dve.wait_ge(s["mx"], p + 1)
                    dve.tensor_tensor(flat(shifted), flat(score), each(mx), ALU.subtract).then_inc(s["sub"], 1)
                    dve.wait_ge(s["ex"], p + 1)
                    dve.tensor_reduce(sm[:], flat(probs), AX_X, ALU.add).then_inc(s["sm"], 1)
                    dve.wait_ge(s["sm"], p + 1)
                    dve.reciprocal(rc[:], sm[:]).then_inc(s["rc"], 1)
                    dve.wait_ge(s["rc"], p + 1)
                    dve.tensor_tensor(flat(probs), flat(probs), each(rc), ALU.mult).then_inc(s["probs"], 1)
                    dve.wait_ge(s["probs"], p + 1)
                    for i, j in pairs:
                        if j == 0:
                            dve.wait_ge(s["att"], NB * p + max(0, i - 1))
                        pr = probs[:, i, :, j:j + 1].rearrange("p (g r) o -> p g r o", g=KV0).to_broadcast([P, KV0, R0, DH0])
                        dve.tensor_tensor(heads(pv[:, i % 2, j]), grouped(qkv[:, j, VO:]), pr, ALU.mult).then_inc(s["pv"], 1)
                    for i in range(NB):
                        dve.wait_ge(s["at_hi"], NB * p + i + 1)
                        lo_part(dve, at[:, 1, :, i * P:(i + 1) * P], tp[i % 2][:].rearrange("p (c t) -> p c t", c=KD),
                                at[:, 0, :, i * P:(i + 1) * P]).then_inc(s["at_lo"], 1)
                    for i in range(NB):
                        dve.wait_ge(s["o_ps"], NB * p + i + 1)
                        dve.tensor_tensor(g.X[:, i, p, :], g.X[:, i, p, :], op[i % 2][:], ALU.add).then_inc(s["x_add"], 1)

            @block.tensor
            def _(pe):
                pe.wait_ge(s["w_lo"], 1)
                with pe.Fori(0, NP) as p:
                    pe.wait_ge(s["at_lo"], NB * p)
                    ln_pe_transpose(pe, ln, xn, tp, g.ident, NB, NB * p)
                    for b in range(NB):
                        pe.wait_ge(ln["lo"], NB * p + b + 1)
                        pe.wait_ge(s["qkv_in"], NB * p + max(0, b - 1))
                        x = lambda k: [xt[:, h, k, b * P:(b + 1) * P] for h in range(2)]
                        for k in range(KD):
                            mm3(pe, qp[b % 2][:], x(k), wslice(k, 0, KO), k == 0, k == KD - 1)
                        for k in range(KD):
                            last = mm3(pe, kp[b % 2][:, 0:QKV0 - KO], x(k), wslice(k, KO, QKV0 - KO), k == 0, k == KD - 1)
                        last.then_inc(s["qkv_ps"], 1)
                    for i in range(NB):
                        pe.wait_ge(s["att"], NB * p + i + 1)
                        pe.wait_ge(s["at_lo"], NB * p + max(0, i - 1))
                        for c in range(KD):
                            last = pe.transpose(tp[i % 2][:, c * P:(c + 1) * P], att[:, i, c * P:(c + 1) * P], g.ident[:])
                        last.then_inc(s["at_ps"], 1)
                    for i in range(NB):
                        pe.wait_ge(s["at_lo"], NB * p + i + 1)
                        pe.wait_ge(s["x_add"], NB * p + max(0, i - 1))
                        for k in range(KD):
                            last = mm3(pe, op[i % 2][:], [at[:, h, k, i * P:(i + 1) * P] for h in range(2)], wo(k),
                                       k == 0, k == KD - 1)
                        last.then_inc(s["o_ps"], 1)


def stage_cross0(nc, g):
    with ExitStack() as ctx:
        sb, ps, sems = tensors(nc, ctx)
        ln = ln_semaphores(sems, "cross_ln")
        s = sems("cross", "o_ps x_add")
        stats, mv = sb("cross_stats", [P, NP, 6]), sb("cross_mv", [P, NP, 2])
        sd, rstd = sb("cross_sd", [P, NP]), sb("cross_rstd", [P, NP])
        xn = sb("cross_xn", [P, NP, D])
        xt = sb("cross_xt", [P, 2, KD, NT], F32R)
        tp = [ps(f"cross_tp{k}", [P, NT]) for k in range(2)]
        op = [ps(f"cross_o{k}", [P, NT]) for k in range(4)]
        with nc.Block() as block:
            @block.scalar
            def _(act):
                with act.Fori(0, NB) as b:
                    ln_act_sqrt(act, ln, mv, sd, g.eps, NP, b)
                    act.wait_ge(s["o_ps"], NP * b)
                    ln_act_hi(act, ln, xt, tp, NP, NP * b)

            @block.vector
            def _(dve):
                with dve.Fori(0, NB) as b:
                    ln_dve_normalise(dve, ln, [g.X[:, b, t, :] for t in range(NP)], stats, mv, sd, rstd, xn, b, NP * b)
                    ln_dve_lo(dve, ln, xt, tp, NP, NP * b)
                    for t in range(NP):
                        dve.wait_ge(s["o_ps"], NP * b + t + 1)
                        dve.tensor_tensor(g.X[:, b, t, :], g.X[:, b, t, :], op[t][:], ALU.add).then_inc(s["x_add"], 1)

            @block.tensor
            def _(pe):
                with pe.Fori(0, NB) as b:
                    ln_pe_transpose(pe, ln, xn, tp, g.ident, NP, NP * b)
                    for t in range(NP):
                        pe.wait_ge(ln["lo"], NP * b + t + 1)
                        pe.wait_ge(s["x_add"], NP * b)
                        for k in range(KD):
                            last = mm3(pe, op[t][:], [xt[:, h, k, t * P:(t + 1) * P] for h in range(2)],
                                       [g.A[:, h, b, k] for h in range(2)], k == 0, k == KD - 1)
                        last.then_inc(s["o_ps"], 1)


def stage_ffn0(nc, g):
    with ExitStack() as ctx:
        sb, ps, sems = tensors(nc, ctx)
        ln = ln_semaphores(sems, "ffn0_ln")
        s = sems("ffn0", "w_load w_hi w_lo gu_ps sg h a cm t1 t2 hs h_hi h_lo o_ps x_add")
        M = 4
        GU = 2 * KD * P
        wraw = sb("ffn0_wraw", [P, PIECE])
        w = sb("ffn0_w", [P, 2, M, PIECE], F32R)
        xt = sb("ffn0_xt", [P, 2, KD, NB * NT], F32R)
        stats, mv = sb("ffn0_stats", [P, NP, 6]), sb("ffn0_mv", [P, NP, 2])
        sd, rstd = sb("ffn0_sd", [P, NP]), sb("ffn0_rstd", [P, NP])
        sg = sb("ffn0_sg", [P, 2, NT])
        h = sb("ffn0_h", [P, 2, M, NT])
        a = sb("ffn0_abs", [P, M, NT])
        xn = a
        ge = sb("ffn0_ge", [P, 6, NT], BF16)
        rank = sb("ffn0_rank", [P, M, NT], BF16)
        hh = sb("ffn0_hh", [P, 2, M, NT], F32R)
        gp = [ps(f"ffn0_g{k}", [P, NT]) for k in range(2)]
        up = [ps(f"ffn0_u{k}", [P, NT]) for k in range(2)]
        op = [ps(f"ffn0_o{k}", [P, NT]) for k in range(NP)]

        def wgu(j, which, k):
            at = (which * KD + k) * P
            return [w[:, x, j, at:at + P] for x in range(2)]

        with nc.Block() as block:
            @block.sync
            def _(sp):
                with sp.Fori(0, C0) as c:
                    for j in range(M):
                        sp.wait_ge(s["w_lo"], M * c + j)
                        sp.dma_start(wraw[:], g.dram["ffn0_w"][M * c + j]).then_inc(s["w_load"], 16)

            @block.scalar
            def _(act):
                with act.Fori(0, NB) as b:
                    ln_act_sqrt(act, ln, mv, sd, g.eps, NP, b)
                    ln_act_hi(act, ln, xt[:, :, :, bass.ds(b * NT, NT)], gp, NP, NP * b)

                with act.Fori(0, C0) as c:
                    def silu(b):
                        for j in range(M):
                            n = M * (NB * c + b) + j
                            act.wait_ge(s["gu_ps"], n + 1)
                            if b or j >= 2:
                                act.wait_ge(s["h"], n - 1)
                            act.activation(sg[:, j % 2], gp[j % 2][:], ACT.Silu).then_inc(s["sg"], 1)

                    act.wait_ge(s["o_ps"], NP * NB * c)
                    act.wait_ge(s["h"], M * NB * c)
                    for j in range(M):
                        act.wait_ge(s["w_load"], 16 * (M * c + j + 1))
                        act.copy(w[:, 0, j], wraw[:]).then_inc(s["w_hi"], 1)
                    silu(0)
                    for b in range(NB):
                        u = NB * c + b
                        act.wait_ge(s["h"], M * u + M)
                        act.wait_ge(s["cm"], 3 * u)
                        act.activation(a[:], h[:, b % 2], ACT.Abs).then_inc(s["a"], 1)
                        if b < NB - 1:
                            silu(b + 1)
                        act.wait_ge(s["hs"], M * u + M)
                        act.wait_ge(s["o_ps"], NP * u)
                        act.copy(hh[:, 0], h[:, b % 2]).then_inc(s["h_hi"], 1)

            @block.vector
            def _(dve):
                with dve.Fori(0, NB) as b:
                    ln_dve_normalise(dve, ln, [g.X[:, b, t, :] for t in range(NP)], stats, mv, sd, rstd, xn, b, NP * b)
                    ln_dve_lo(dve, ln, xt[:, :, :, bass.ds(b * NT, NT)], gp, NP, NP * b)

                with dve.Fori(0, C0) as c:
                    def times_up(b, j):
                        n = M * (NB * c + b) + j
                        dve.wait_ge(s["sg"], n + 1)
                        dve.wait_ge(s["h_lo"], max(0, b - 1) + NB * c)
                        dve.tensor_tensor(h[:, b % 2, j], sg[:, j % 2], up[j % 2][:], ALU.mult).then_inc(s["h"], 1)

                    def compare(b, u):
                        dve.wait_ge(s["a"], u + 1)
                        dve.wait_ge(s["t2"], M * u)
                        for i, at, n in ((0, 0, 3), (1, 3, 2), (2, 5, 1)):
                            one = a[:, i:i + 1].to_broadcast([P, n, NT])
                            dve.tensor_tensor(ge[:, at:at + n], one, a[:, i + 1:], ALU.is_ge).then_inc(s["cm"], 1)

                    def rank_a(b, u):
                        dve.wait_ge(s["cm"], 3 * u + 3)
                        dve.wait_ge(s["hs"], M * u)
                        for j, (x, y) in enumerate(((0, 1), (3, 4), (1, 3), (4, 5))):
                            dve.tensor_tensor(rank[:, j], ge[:, x], ge[:, y], ALU.add).then_inc(s["t1"], 1)

                    def rank_b(b, u):
                        dve.wait_ge(s["t1"], M * u + M)
                        dve.tensor_tensor(rank[:, 0], rank[:, 0], ge[:, 2], ALU.add).then_inc(s["t2"], 1)
                        dve.tensor_tensor(rank[:, 1], rank[:, 1], ge[:, 0], ALU.subtract).then_inc(s["t2"], 1)
                        dve.tensor_tensor(rank[:, 2], ge[:, 5], rank[:, 2], ALU.subtract).then_inc(s["t2"], 1)
                        dve.tensor_tensor(rank[:, 3], rank[:, 3], ge[:, 2], ALU.add).then_inc(s["t2"], 1)

                    def select(b, u):
                        dve.wait_ge(s["t2"], M * u + M)
                        for j, (bound, op0) in enumerate(((2.0, ALU.is_ge), (1.0, ALU.is_ge), (0.0, ALU.is_ge), (1.0, ALU.is_le))):
                            dve.scalar_tensor_tensor(out=h[:, b % 2, j], in0=rank[:, j], scalar=bound, in1=h[:, b % 2, j],
                                                     op0=op0, op1=ALU.mult).then_inc(s["hs"], 1)

                    def add(b):
                        for t in range(NP):
                            dve.wait_ge(s["o_ps"], NP * (NB * c + b) + t + 1)
                            dve.tensor_tensor(g.X[:, b, t], g.X[:, b, t], op[t][:], ALU.add).then_inc(s["x_add"], 1)

                    for j in range(M):
                        dve.wait_ge(s["w_hi"], M * c + j + 1)
                        lo_part(dve, w[:, 1, j], wraw[:], w[:, 0, j]).then_inc(s["w_lo"], 1)
                    dve.wait_ge(s["x_add"], NP * NB * c)
                    for j in range(M):
                        times_up(0, j)
                    for b in range(NB):
                        for j, step in enumerate((compare, rank_a, rank_b, select)):
                            step(b, NB * c + b)
                            if b < NB - 1:
                                times_up(b + 1, j)
                        dve.wait_ge(s["h_hi"], NB * c + b + 1)
                        dve.wait_ge(s["hs"], M * (NB * c + b) + M)
                        lo_part(dve, hh[:, 1], h[:, b % 2], hh[:, 0]).then_inc(s["h_lo"], 1)
                        if b:
                            add(b - 1)
                    add(NB - 1)

            @block.tensor
            def _(pe):
                with pe.Fori(0, NB) as b:
                    ln_pe_transpose(pe, ln, xn, gp, g.ident, NP, NP * b)
                pe.wait_ge(ln["lo"], NP * NB)

                with pe.Fori(0, C0) as c:
                    def gate_up(b):
                        x = lambda k: [xt[:, y, k, b * NT:(b + 1) * NT] for y in range(2)]
                        for j in range(M):
                            n = M * (NB * c + b) + j
                            if b == 0:
                                pe.wait_ge(s["w_lo"], M * c + j + 1)
                            if b or j >= 2:
                                pe.wait_ge(s["sg"], n - 1)
                                pe.wait_ge(s["h"], n - 1)
                            for which, bank in enumerate((gp, up)):
                                for k in range(KD):
                                    last = mm3(pe, bank[j % 2][:], wgu(j, which, k), x(k), k == 0, k == KD - 1)
                            last.then_inc(s["gu_ps"], 1)

                    def down(b):
                        u = NB * c + b
                        pe.wait_ge(s["h_lo"], u + 1)
                        pe.wait_ge(s["x_add"], NP * u)
                        for t in range(NP):
                            for j in range(M):
                                last = mm3(pe, op[t][:], [hh[:, y, j, t * P:(t + 1) * P] for y in range(2)],
                                           [w[:, y, j, GU:] for y in range(2)], j == 0, j == M - 1)
                            last.then_inc(s["o_ps"], 1)

                    pe.wait_ge(s["h"], M * NB * c)
                    gate_up(0)
                    for b in range(NB):
                        if b < NB - 1:
                            gate_up(b + 1)
                        down(b)


def latent_down(nc, g, bp, s, ln, ln2):
    with ExitStack() as ctx:
        def sb(name, shape, dt=F32):
            return ctx.enter_context(nc.sbuf_tensor(name, shape, dt))

        def ps(name, shape, dt=F32):
            return ctx.enter_context(nc.psum_tensor(name, shape, dt))

        QK = QL + KVL + DR
        wraw = sb("down_wraw", [P, KD * QK])
        w = sb("down_w", [P, 2, KD * QK], F32R)
        stats, mv = sb("down_stats", [P, NP, 6]), sb("down_mv", [P, NP, 2])
        sd, rstd = sb("down_sd", [P, NP]), sb("down_rstd", [P, NP])
        stats2, mv2 = sb("down_stats2", [P, 2 * NP, 6]), sb("down_mv2", [P, 2 * NP, 2])
        sd2, rstd2 = sb("down_sd2", [P, 2 * NP]), sb("down_rstd2", [P, 2 * NP])
        xn = sb("down_xn", [P, NP, D])
        xt = sb("down_xt", [P, 2, KD, NT], F32R)
        down = sb("down_x", [P, NP, QK])
        kr = sb("down_kr", [P, NP, 2, DR])
        kr2 = sb("down_kr2", [P, NP, DR])
        tmp = sb("down_tmp", [P, 2, NT])
        table = sb("down_rope", [P, 2, NP, DR])
        gb = sb("down_gb", [P, 2 * KQ + 2])
        tp = [ps(f"down_tp{k}", [P, NT]) for k in range(2)]
        cp = [ps(f"down_c{k}", [P, NT]) for k in range(2)]
        kp = [ps(f"down_k{k}", [P, NT]) for k in range(2)]
        up = [ps(f"down_t{k}", [P, NT]) for k in range(2)]
        gain = [gb[:, k:k + 1] for k in range(KQ)] + [gb[:, 2 * KQ:2 * KQ + 1]]
        offset = [gb[:, KQ + k:KQ + k + 1] for k in range(KQ)] + [gb[:, 2 * KQ + 1:2 * KQ + 2]]
        NCH = KQ + 1

        def dst(c, bb):
            cols = slice(bb * NT, (bb + 1) * NT)
            return g.cq[:, :, c, cols] if c < KQ else g.ckv[:, :, cols]

        with nc.Block() as block:
            @block.sync
            def _(sp):
                sp.dma_start(wraw[:], g.dram["down1_w"]).then_inc(s["load"], 16)
                sp.dma_start(table[:], g.dram["rope_t"]).then_inc(s["load"], 16)
                sp.dma_start(gb[:], g.dram["ln_gb"]).then_inc(s["load"], 16)

            @block.scalar
            def _(act):
                act.wait_ge(s["load"], 48 * bp + 48)
                act.copy(w[:, 0], wraw[:]).then_inc(s["w_hi"], 1)
                for bb in range(2):
                    b = 2 * bp + bb
                    ln_act_sqrt(act, ln, mv, sd, g.eps, NP, b)
                    ln_act_hi(act, ln, xt, tp, NP, NP * b)
                    act.wait_ge(s["t_ps"], 5 * b)
                    for t in range(NP):
                        act.wait_ge(s["d_ps"], NP * b + t + 1)
                        act.copy(down[:, t, 0:QL], cp[t % 2][:, 0:QL])
                        act.copy(down[:, t, QL:], kp[t % 2][:, 0:QK - QL]).then_inc(s["d_in"], 1)
                    act.wait_ge(ln2["var"], b + 1)
                    act.activation(sd2[:], mv2[:, :, 1], ACT.Sqrt, bias=g.eps[:, 0:1]).then_inc(ln2["sd"], 1)
                    for c in range(NCH):
                        act.wait_ge(s["t_mul"], NCH * b + c + 1)
                        act.copy(dst(c, bb)[:, 0], tmp[:, c % 2]).then_inc(s["t_hi"], 1)
                    act.wait_ge(s["t_ps"], 5 * b + 5)
                    act.copy(g.kr[:, bb], up[NCH % 2][:]).then_inc(s["kr_hi"], 1)

            @block.vector
            def _(dve):
                dve.wait_ge(s["w_hi"], bp + 1)
                lo_part(dve, w[:, 1], wraw[:], w[:, 0]).then_inc(s["w_lo"], 1)
                for bb in range(2):
                    b = 2 * bp + bb
                    ln_dve_normalise(dve, ln, [g.X[:, b, t, :] for t in range(NP)], stats, mv, sd, rstd, xn, b, NP * b)
                    ln_dve_lo(dve, ln, xt, tp, NP, NP * b)
                    for t in range(NP):
                        dve.wait_ge(s["d_in"], NP * b + t + 1)
                        dve.bn_stats(stats2[:, 2 * t, :], down[:, t, 0:QL])
                        last = dve.bn_stats(stats2[:, 2 * t + 1, :], down[:, t, QL:QL + KVL])
                    last.then_inc(ln2["stats"], 1)
                    a = down[:, :, QL + KVL:]
                    half = DR // 2
                    dve.wait_ge(s["t_ps"], 5 * b)
                    dve.tensor_tensor(kr[:, :, 0], a, table[:, 0], ALU.mult).then_inc(s["kr"], 1)
                    dve.tensor_tensor(kr2[:, :, 0:half], a[:, :, half:], table[:, 1, :, 0:half], ALU.mult).then_inc(s["kr"], 1)
                    dve.tensor_tensor(kr2[:, :, half:], a[:, :, 0:half], table[:, 1, :, half:], ALU.mult).then_inc(s["kr"], 1)
                    dve.wait_ge(s["kr"], 5 * b + 3)
                    dve.tensor_tensor(kr[:, :, 0], kr[:, :, 0], kr2[:], ALU.add).then_inc(s["kr"], 1)
                    dve.wait_ge(s["kr"], 5 * b + 4)
                    dve.tensor_copy(kr[:, :, 1], kr[:, :, 0]).then_inc(s["kr"], 1)
                    dve.wait_ge(ln2["stats"], b + 1)
                    dve.sem_inc(ln2["passed"], 1)
                    for n in range(2 * NP):
                        last = dve.bn_aggr(mv2[:, n, :], stats2[:, n, :])
                    last.then_inc(ln2["var"], 1)
                    dve.wait_ge(ln2["sd"], b + 1)
                    dve.reciprocal(rstd2[:], sd2[:]).then_inc(ln2["rstd"], 1)
                    dve.wait_ge(ln2["rstd"], b + 1)
                    for n in range(2 * NP):
                        part = down[:, n // 2, 0:QL] if n % 2 == 0 else down[:, n // 2, QL:QL + KVL]
                        dve.tensor_scalar(part, part, mv2[:, n, 0:1], rstd2[:, n:n + 1], ALU.subtract,
                                          ALU.mult).then_inc(ln2["norm"], 1)
                    for c in range(NCH):
                        dve.wait_ge(s["t_ps"], 5 * b + c + 1)
                        if c >= 2:
                            dve.wait_ge(s["t_lo"], NCH * b + c - 1)
                        dve.tensor_scalar(tmp[:, c % 2], up[c % 2][:], gain[c], offset[c], ALU.mult, ALU.add).then_inc(s["t_mul"], 1)
                        dve.wait_ge(s["t_hi"], NCH * b + c + 1)
                        dve.wait_ge(s["t_mul"], NCH * b + c + 1)
                        lo_part(dve, dst(c, bb)[:, 1], tmp[:, c % 2], dst(c, bb)[:, 0]).then_inc(s["t_lo"], 1)
                    dve.wait_ge(s["kr_hi"], b + 1)
                    up_half = slice(DR, 2 * DR)
                    lo_part(dve, g.kr[up_half, bb], up[NCH % 2][up_half], g.kr[up_half, bb]).then_inc(s["kr_lo"], 1)

            @block.tensor
            def _(pe):
                pe.wait_ge(s["w_lo"], bp + 1)
                for bb in range(2):
                    b = 2 * bp + bb
                    ln_pe_transpose(pe, ln, xn, tp, g.ident, NP, NP * b)
                    for t in range(NP):
                        pe.wait_ge(ln["lo"], NP * b + t + 1)
                        pe.wait_ge(s["d_in"], NP * b + max(0, t - 1))
                        for bank, at, n in ((cp, 0, QL), (kp, QL, QK - QL)):
                            for k in range(KD):
                                last = mm3(pe, bank[t % 2][:, 0:n], [xt[:, h, k, t * P:(t + 1) * P] for h in range(2)],
                                           [w[:, h, k * QK + at:k * QK + at + n] for h in range(2)], k == 0, k == KD - 1)
                        last.then_inc(s["d_ps"], 1)
                    pe.wait_ge(ln2["norm"], 2 * NP * (b + 1))
                    pe.wait_ge(s["kr"], 5 * b + 5)
                    pe.wait_ge(s["kr_lo"], b)
                    for c in range(NCH + 1):
                        if c >= 2:
                            pe.wait_ge(s["t_mul"], NCH * b + c - 1)
                        for t in range(NP):
                            src = down[:, t, c * P:(c + 1) * P] if c < NCH else kr[:, t].rearrange("p a d -> p (a d)")
                            last = pe.transpose(up[c % 2][:, t * P:(t + 1) * P], src, g.ident[:])
                        last.then_inc(s["t_ps"], 1)


def latent_heads(nc, g, bp, s):
    with ExitStack() as ctx:
        def sb(name, shape, dt=F32):
            return ctx.enter_context(nc.sbuf_tensor(name, shape, dt))

        def ps(name, shape, dt=F32):
            return ctx.enter_context(nc.psum_tensor(name, shape, dt))

        U = 4
        w = sb("pair_w", [P, 2, WPAIR], F32R)
        raw = sb("pair_raw", [P, WQ1])
        bias_all = sb("pair_bias_all", [P, PAIRS, 8])
        bias = sb("pair_bias", [P, 8])
        rope = sb("pair_rope", [P, 2, NT])
        qn = sb("pair_qn", [P, 2, 2, NT], F32R)
        kn = sb("pair_kn", [P, 2, 2, NT], F32R)
        qr1 = sb("pair_qr1", [P, 2, NT], F32R)
        qr2 = sb("pair_qr2", [DR, 2, NT], F32R)
        rot = sb("pair_rot", [P, 2, NT])
        v = sb("pair_v", [P, 2, NP, 2 * DV], F32R)
        pr_ = sb("pair_probs", [P, NP, NT])
        pt = sb("pair_pt", [P, 2, NP, NT], F32R)
        ot = sb("pair_ot", [P, 2, 2, NT], F32R)
        nmax, psum_, prec = (sb(f"pair_{n}", [P, NP]) for n in ("nmax", "psum", "prec"))
        NQ = NS // 4
        rows = sb("scan_rows", [P, 2, NQ, NT])
        dt, du = sb("scan_dt", [P, NT]), sb("scan_du", [P, NT])
        da = sb("scan_da", [P, 2, NT])
        st = sb("scan_state", [P, 3, NT])
        y = sb("scan_y", [P, NT])
        a_all = sb("scan_a_all", [P, CT, NS])
        a4 = sb("scan_a", [P, CT, NQ])
        sc = [ps(f"pair_s{k}", [P, NT]) for k in range(2)]
        tb = [ps(f"pair_t{k}", [P, NT]) for k in range(2)]
        gb = [ps(f"pair_g{k}", [P, NT]) for k in range(2)]
        ob = [ps(f"pair_o{k}", [P, NT]) for k in range(2)]
        KVO, OO = WQ1, WQ1 + WKV1
        PIECES = ((0, WQ1), (KVO, WKV1), (OO, WO1))

        FILLS = [("v", 0, 0), ("v", 0, 1), ("ra", 0, 0), ("rb", 0, 0), ("qn", 0, 0), ("kn", 0, 0), ("qn", 1, 0), ("kn", 1, 0),
                 ("ra", 2, 0), ("rb", 2, 0), ("qn", 2, 0), ("kn", 2, 0), ("qn", 3, 0), ("kn", 3, 0), ("v", 2, 0), ("v", 2, 1)]
        NF = len(FILLS)
        HI = [kind in ("v", "qn", "kn") for kind, _, _ in FILLS]
        NHI = sum(HI)
        GROUPS = {"start": range(0, 8), 0: range(8, 12), 1: range(12, 14), "v1": range(14, 16)}

        def target(kind, u, x):
            if kind == "v":
                return v[:, :, 2 * x:2 * x + 2, :]
            return (qn if kind == "qn" else kn)[:, u % 2]

        def bank(f):
            return gb[f % 2][:].rearrange("p (t d) -> p t d", t=2) if FILLS[f][0] == "v" else gb[f % 2][:]

        def bias_of(kind, u):
            c = {"qn": 0, "kn": 4}[kind] + u % 2
            return bias[:, c:c + 1]

        with nc.Block() as block:
            @block.sync
            def _(sp):
                sp.dma_start(bias_all[:], g.dram["pair_b"].rearrange("r p c -> p r c")).then_inc(s["c_load"], 16)
                sp.dma_start(rope[:], g.dram["rope_f"]).then_inc(s["c_load"], 16)
                sp.dma_start(a_all[:], g.dram["scan_ad"][:, 0:CT * NS].rearrange("p (c n) -> p c n", c=CT)).then_inc(s["c_load"], 16)
                base = 26 * bp

                def piece(pair, n, number):
                    sp.wait_ge(s["pw_lo"], base + number)
                    at, size = PIECES[n]
                    sp.dma_start(raw[:, 0:size], g.dram["pair_w"][pair, :, at:at + size]).then_inc(s["pw_load"], 16)

                piece(0, 0, 0)
                piece(0, 1, 1)
                with sp.Fori(0, PAIRS) as r:
                    t = bp * PAIRS + r
                    b, q = bp * 2 + r // 4, r % 4
                    sp.wait_ge(s["z"], 16 * t)
                    for n in range(2):
                        src = g.bc_dram[b, bass.ds(n * NS + q * NQ, NQ), :].rearrange("(o n) t -> o n t", o=1)
                        sp.dma_start(rows[:, n], src.to_broadcast([P, NQ, NT])).then_inc(s["rows"], 16)

                    for ct in range(CT):
                        sp.wait_ge(s["da"], 16 * t + 4 * ct)
                        sp.dma_start(dt[:], g.dt_dram[b, :, ct, :]).then_inc(s["dtu"], 16)
                        sp.wait_ge(s["dbu"], 16 * t + 4 * ct)
                        sp.dma_start(du[:], g.u_dram[b, :, ct, :]).then_inc(s["dtu"], 16)
                        if ct == 0:
                            piece(r, 2, 3 * r + 2)
                        if ct == 2:
                            piece((r + 1) % PAIRS, 0, 3 * r + 3)
                        if ct:
                            sp.wait_ge(s["y"], 16 * t + 4 * ct)
                            sp.dma_start(g.y_dram[t, :, ct - 1, :], y[:]).then_inc(s["y_st"], 16)
                    piece((r + 1) % PAIRS, 1, 3 * r + 4)
                    sp.wait_ge(s["y"], 16 * t + 16)
                    sp.dma_start(g.y_dram[t, :, CT - 1, :], y[:]).then_inc(s["y_st"], 16)
                sp.wait_ge(s["y_st"], 64 * PAIRS * (bp + 1))
                sp.sem_inc(s["sp_passed"], 1)

            @block.gpsimd
            def _(pool):
                with pool.Fori(0, PAIRS) as r:
                    t = bp * PAIRS + r
                    pool.wait_ge(s["rows"], 32 * t + 32)

                    def dbu(m):
                        ct, n = m // NQ, m % NQ
                        if n == 0:
                            pool.wait_ge(s["dtu"], 128 * t + 32 * ct + 32)
                            pool.tensor_tensor(du[:], du[:], dt[:], ALU.mult).then_inc(s["du"], 1)
                            pool.wait_ge(s["du"], 4 * t + ct + 1)
                        pool.wait_ge(s["z"], 16 * t + max(0, m - 2))
                        pool.wait_ge(s["y"], 16 * t + max(0, m - 2))
                        pool.tensor_tensor(st[:, m % 3], du[:], rows[:, 0, n], ALU.mult).then_inc(s["dbu"], 1)

                    dbu(0)
                    for m in range(16):
                        ct, n = m // NQ, m % NQ
                        if m < 15:
                            dbu(m + 1)
                        pool.wait_ge(s["scan"], 16 * t + m + 1)
                        if n == 0:
                            pool.wait_ge(s["y_st"], 64 * t + 16 * ct)
                            pool.tensor_tensor(y[:], st[:, m % 3], rows[:, 1, n], ALU.mult).then_inc(s["z"], 1)
                            pool.wait_ge(s["z"], 16 * t + m + 1)
                            pool.sem_inc(s["y"], 1)
                        else:
                            pool.tensor_tensor(st[:, m % 3], st[:, m % 3], rows[:, 1, n], ALU.mult).then_inc(s["z"], 1)
                            pool.wait_ge(s["z"], 16 * t + m + 1)
                            pool.tensor_tensor(y[:], y[:], st[:, m % 3], ALU.add).then_inc(s["y"], 1)

            @block.scalar
            def _(act):
                act.wait_ge(s["c_load"], 48 * (bp + 1))
                act.activation(a_all[:], a_all[:], ACT.Exp).then_inc(s["a_exp"], 1)
                base = 26 * bp

                def split(n, number):
                    at, size = PIECES[n]
                    act.wait_ge(s["pw_load"], 16 * (base + number + 1))
                    act.activation(w[:, 0, at:at + size], raw[:, 0:size], ACT.Copy,
                                   scale=SCALE1 if n == 0 else 1.0).then_inc(s["pw_hi"], 1)

                split(0, 0)
                split(1, 1)
                with act.Fori(0, PAIRS) as r:
                    t = bp * PAIRS + r

                    def fill(f):
                        kind, u, x = FILLS[f]
                        if kind == "ra":
                            return
                        if kind == "rb":
                            pb = 2 * t + u // 2
                            act.wait_ge(s["rot"], 3 * pb + 3)
                            for hd in range(2):
                                for half in range(2):
                                    last = act.copy(qr1[half * DR:(half + 1) * DR, hd], rot[hd * DR:(hd + 1) * DR, 0])
                            last.then_inc(s["qr_hi"], 1)
                            return
                        act.wait_ge(s["f_ps"], NF * t + f + 1)
                        if kind == "v":
                            last = act.copy(target(kind, u, x)[:, 0], bank(f))
                        else:
                            last = act.activation(target(kind, u, x)[:, 0], bank(f), ACT.Identity, bias=bias_of(kind, u))
                        last.then_inc(s["f_hi"], 1)

                    def exp(u, q):
                        act.wait_ge(s["nmax"], NP * (U * t + u) + q + 1)
                        act.activation(pr_[:, q], sc[q % 2][:], ACT.Exp, bias=nmax[:, q:q + 1],
                                       accum_out=psum_[:, q:q + 1]).then_inc(s["exp"], 1)

                    def norm(u, q):
                        act.wait_ge(s["prec"], NP * (U * t + u) + q + 1)
                        act.activation(pr_[:, q], pr_[:, q], ACT.Copy, scale=prec[:, q:q + 1]).then_inc(s["norm"], 1)

                    def decay(m):
                        act.wait_ge(s["dtu"], 128 * t + 32 * (m // NQ) + 32)
                        act.wait_ge(s["scan"], 16 * t + max(0, m - 1))
                        act.activation(da[:, m % 2], dt[:], ACT.Exp, scale=a4[:, m // NQ, m % NQ:m % NQ + 1]).then_inc(s["da"], 1)

                    act.wait_ge(s["a4"], t + 1)
                    for f in GROUPS["start"]:
                        fill(f)
                    split(2, 3 * r + 2)
                    for q in range(NP):
                        exp(0, q)
                        if q:
                            norm(0, q - 1)
                    norm(0, NP - 1)
                    for u in range(U):
                        for q in range(NP):
                            act.wait_ge(s["t_ps2"], NP * (U * t + u) + q + 1)
                            act.copy(pt[:, 0, :, q * P:(q + 1) * P], tb[q % 2][:].rearrange("p (k q) -> p k q", k=NP)).then_inc(s["pt_hi"], 1)
                            decay(NP * u + q)
                            if u < U - 1:
                                exp(u + 1, q)
                                if q:
                                    norm(u + 1, q - 1)
                        if u < U - 1:
                            norm(u + 1, NP - 1)
                        for f in GROUPS.get(u, ()):
                            fill(f)
                        act.wait_ge(s["o_ps"], U * t + u + 1)
                        act.activation(ot[:, u % 2, 0], ob[0][:], ACT.Identity, bias=bias[:, 6 + u % 2:7 + u % 2]).then_inc(s["ot_hi"], 1)
                        if u == 1:
                            for f in GROUPS["v1"]:
                                fill(f)
                        if u == 2:
                            split(0, 3 * r + 3)
                            split(1, 3 * r + 4)

            @block.vector
            def _(dve):
                dve.wait_ge(s["c_load"], 48 * (bp + 1))
                dve.wait_ge(s["a_exp"], bp + 1)
                dve.tensor_scalar(a_all[:], a_all[:], -1.0, None, ALU.mult).then_inc(s["consts"], 1)
                dve.tensor_scalar(bias_all[:, :, 0:4], bias_all[:, :, 0:4], SCALE1, None, ALU.mult).then_inc(s["consts"], 1)
                base = 26 * bp

                def split(n, number):
                    at, size = PIECES[n]
                    dve.wait_ge(s["pw_hi"], base + number + 1)
                    dve.scalar_tensor_tensor(out=w[:, 1, at:at + size], in0=raw[:, 0:size], scalar=SCALE1 if n == 0 else 1.0,
                                             in1=w[:, 0, at:at + size].bitcast(F32), op0=ALU.mult,
                                             op1=ALU.subtract).then_inc(s["pw_lo"], 1)

                split(0, 0)
                split(1, 1)
                dve.wait_ge(s["consts"], 2 * bp + 2)
                dve.sem_inc(s["dve_passed"], 1)
                with dve.Fori(0, PAIRS) as r:
                    t = bp * PAIRS + r

                    def fill(f):
                        kind, u, x = FILLS[f]
                        if kind in ("ra", "rb"):
                            n = int(kind == "rb")
                            pb = 2 * t + u // 2
                            dve.wait_ge(s["f_ps"], NF * t + f + 1)
                            if kind == "ra":
                                dve.wait_ge(s["qr_hi"], pb)
                                dve.wait_ge(s["qr_lo"], 2 * pb)
                            dve.scalar_tensor_tensor(out=rot[:, n], in0=gb[f % 2][:], scalar=bias[:, 2 + n:3 + n],
                                                     in1=rope[:, n], op0=ALU.add, op1=ALU.mult).then_inc(s["rot"], 1)
                            if kind == "ra":
                                return
                            dve.wait_ge(s["rot"], 3 * pb + 2)
                            dve.tensor_tensor(rot[:, 0], rot[:, 0], rot[:, 1], ALU.add).then_inc(s["rot"], 1)
                            dve.wait_ge(s["rot"], 3 * pb + 3)
                            dve.wait_ge(s["qr_hi"], pb + 1)
                            for hd in range(2):
                                lanes = slice(hd * DR, (hd + 1) * DR)
                                lo_part(dve, qr2[:, hd], rot[lanes, 0], qr1[lanes, hd]).then_inc(s["qr_lo"], 1)
                            return
                        dve.wait_ge(s["f_hi"], NHI * t + sum(HI[:f]) + 1)
                        out, hi = target(kind, u, x)[:, 1], target(kind, u, x)[:, 0]
                        if kind == "v":
                            last = lo_part(dve, out, bank(f), hi)
                        else:
                            last = dve.scalar_tensor_tensor(out=out, in0=bank(f), scalar=bias_of(kind, u), in1=hi.bitcast(F32),
                                                            op0=ALU.add, op1=ALU.subtract)
                        last.then_inc(s["f_lo"], 1)

                    def maximum(u, q):
                        dve.wait_ge(s["s_ps"], NP * (U * t + u) + q + 1)
                        dve.tensor_reduce(nmax[:, q:q + 1], sc[q % 2][:], AX_X, ALU.max, negate=True).then_inc(s["nmax"], 1)

                    def invert(u, q):
                        dve.wait_ge(s["exp"], NP * (U * t + u) + q + 1)
                        dve.reciprocal(prec[:, q:q + 1], psum_[:, q:q + 1]).then_inc(s["prec"], 1)

                    def scan(m):
                        dve.wait_ge(s["da"], 16 * t + m + 1)
                        dve.wait_ge(s["dbu"], 16 * t + m + 1)
                        dve.tensor_tensor_scan(st[:, m % 3], da[:, m % 2], st[:, m % 3], 0.0, ALU.mult, ALU.add).then_inc(s["scan"], 1)

                    def add(bb, tok):
                        dve.wait_ge(s["w_ps"], NP * (2 * t + bb) + tok + 1)
                        x = g.X[:, 2 * bp + bb, tok]
                        dve.wait_ge(s["x_add"], NP * 2 * t)
                        dve.tensor_tensor(x, x, ob[(tok + 1) % 2][:], ALU.add).then_inc(s["x_add"], 1)

                    dve.wait_ge(s["ot_hi"], U * t)
                    dve.wait_ge(s["ot_lo"], U * t)
                    dve.wait_ge(s["da"], 16 * t)
                    dve.tensor_copy(bias[:], bias_all[:, r, :])
                    dve.tensor_copy(a4[:], a_all[:, :, bass.ds((r % 4) * NQ, NQ)]).then_inc(s["a4"], 1)
                    dve.wait_ge(s["a4"], t + 1)
                    for f in GROUPS["start"]:
                        fill(f)
                    split(2, 3 * r + 2)
                    for q in range(NP):
                        maximum(0, q)
                        if q:
                            invert(0, q - 1)
                    invert(0, NP - 1)
                    for u in range(U):
                        for q in range(NP):
                            dve.wait_ge(s["pt_hi"], NP * (U * t + u) + q + 1)
                            lo_part(dve, pt[:, 1, :, q * P:(q + 1) * P], tb[q % 2][:].rearrange("p (k q) -> p k q", k=NP),
                                    pt[:, 0, :, q * P:(q + 1) * P]).then_inc(s["pt_lo"], 1)
                            if u < U - 1:
                                maximum(u + 1, q)
                            scan(NP * u + q)
                            if u < U - 1 and q:
                                invert(u + 1, q - 1)
                            if u == 2:
                                add(0, q)
                        if u < U - 1:
                            invert(u + 1, NP - 1)
                        for f in GROUPS.get(u, ()):
                            fill(f)
                        dve.wait_ge(s["ot_hi"], U * t + u + 1)
                        dve.scalar_tensor_tensor(out=ot[:, u % 2, 1], in0=ob[0][:], scalar=bias[:, 6 + u % 2:7 + u % 2],
                                                 in1=ot[:, u % 2, 0].bitcast(F32), op0=ALU.add, op1=ALU.subtract).then_inc(s["ot_lo"], 1)
                        if u == 1:
                            for f in GROUPS["v1"]:
                                fill(f)
                        if u == 2:
                            split(0, 3 * r + 3)
                            split(1, 3 * r + 4)
                    for tok in range(NP):
                        add(1, tok)

            @block.tensor
            def _(pe):
                base = 26 * bp
                with pe.Fori(0, PAIRS) as r:
                    t = bp * PAIRS + r

                    def fill(f):
                        kind, u, x = FILLS[f]
                        bb = u // 2
                        if f >= 2:
                            before = FILLS[f - 2][0]
                            if before in ("ra", "rb"):
                                pb = 2 * t + FILLS[f - 2][1] // 2
                                pe.wait_ge(s["rot"], 3 * pb + (1 if before == "ra" else 2))
                            else:
                                pe.wait_ge(s["f_lo"], NHI * t + sum(HI[:f - 2]) + 1)
                        out = gb[f % 2]
                        if kind == "v":
                            for half in range(2):
                                tok = bb * NT + (2 * x + half) * P
                                last = mm3(pe, out[:, half * 2 * DV:(half + 1) * 2 * DV], [g.ckv[:, h, tok:tok + P] for h in range(2)],
                                           [w[:, h, KVO + 2 * DN:KVO + 4 * DN] for h in range(2)])
                        elif kind == "kn":
                            at = KVO + (u % 2) * DN
                            last = mm3(pe, out[:], [w[:, h, at:at + DN] for h in range(2)],
                                       [g.ckv[:, h, bb * NT:(bb + 1) * NT] for h in range(2)])
                        else:
                            at = {"qn": u % 2, "ra": 2, "rb": 3}[kind] * P
                            for k in range(KQ):
                                last = mm3(pe, out[:], [w[:, h, k * 4 * P + at:k * 4 * P + at + P] for h in range(2)],
                                           [g.cq[:, h, k, bb * NT:(bb + 1) * NT] for h in range(2)], k == 0, k == KQ - 1)
                        last.then_inc(s["f_ps"], 1)

                    def scores(u, q):
                        if q == 0:
                            f = FILLS.index(("kn", u, 0))
                            pe.wait_ge(s["f_lo"], NHI * t + sum(HI[:f]) + 1)
                            pe.wait_ge(s["qr_lo"], 2 * (2 * t + u // 2) + 2)
                        n = NP * (U * t + u) + q
                        if u or q >= 2:
                            pe.wait_ge(s["exp"], n - 1)
                        cols = slice(q * P, (q + 1) * P)
                        bb, hd = u // 2, u % 2
                        mm3(pe, sc[q % 2][:], [qn[:, u % 2, h, cols] for h in range(2)], [kn[:, u % 2, h] for h in range(2)], True, False)
                        pe.matmul(sc[q % 2][:], qr1[:, hd, cols], g.kr[:, bb], start=False, stop=False)
                        pe.matmul(sc[q % 2][:], qr2[:, hd, cols], g.kr[0:DR, bb], start=False, stop=True).then_inc(s["s_ps"], 1)

                    def turn(u, q):
                        n = NP * (U * t + u) + q
                        pe.wait_ge(s["norm"], n + 1)
                        if u or q >= 2:
                            pe.wait_ge(s["pt_lo"], n - 1)
                        for k in range(NP):
                            last = pe.transpose(tb[q % 2][:, k * P:(k + 1) * P], pr_[:, q, k * P:(k + 1) * P], g.ident[:])
                        last.then_inc(s["t_ps2"], 1)

                    def values(u):
                        pe.wait_ge(s["pt_lo"], NP * (U * t + u) + NP)
                        f = FILLS.index(("v", u // 2 * 2, 1))
                        pe.wait_ge(s["f_lo"], NHI * t + sum(HI[:f]) + 1)
                        if u == 3:
                            pe.wait_ge(s["x_add"], NP * (2 * t + 1))
                        if u == 0:
                            pe.wait_ge(s["x_add"], NP * 2 * t)
                        if u:
                            pe.wait_ge(s["ot_lo"], U * t + u)
                        if u == 2:
                            pe.wait_ge(s["x_add"], NP * (2 * t + 1))
                        hd = u % 2
                        for k in range(NP):
                            last = mm3(pe, ob[0][:], [v[:, h, k, hd * DV:(hd + 1) * DV] for h in range(2)],
                                       [pt[:, h, k] for h in range(2)], k == 0, k == NP - 1)
                        last.then_inc(s["o_ps"], 1)

                    def project(bb, tok):
                        if tok == 0:
                            pe.wait_ge(s["ot_lo"], U * t + 2 * bb + 2)
                        if bb or tok >= 2:
                            pe.wait_ge(s["x_add"], NP * (2 * t + bb) + max(0, tok - 1))
                        cols = slice(tok * P, (tok + 1) * P)
                        for hd in range(2):
                            last = mm3(pe, ob[(tok + 1) % 2][:], [ot[:, hd, h, cols] for h in range(2)],
                                       [w[:, h, OO + hd * D:OO + (hd + 1) * D] for h in range(2)], hd == 0, hd == 1)
                        last.then_inc(s["w_ps"], 1)

                    pe.wait_ge(s["pw_lo"], base + 3 * r + 2)
                    pe.wait_ge(s["x_add"], NP * 2 * t)
                    pe.wait_ge(s["exp"], NP * U * t)
                    pe.wait_ge(s["pt_lo"], NP * U * t)
                    pe.wait_ge(s["f_lo"], NHI * t)
                    for f in GROUPS["start"]:
                        fill(f)
                    for q in range(NP):
                        scores(0, q)
                    for u in range(U):
                        for q in range(NP):
                            turn(u, q)
                            if u < U - 1:
                                scores(u + 1, q)
                            if u == 2:
                                if q == 0:
                                    pe.wait_ge(s["pw_lo"], base + 3 * r + 3)
                                project(0, q)
                        for f in GROUPS.get(u, ()):
                            fill(f)
                        values(u)
                        if u == 1:
                            for f in GROUPS["v1"]:
                                fill(f)
                    for tok in range(NP):
                        project(1, tok)


def stage_latent1(nc, g):
    with ExitStack() as ctx:
        sb, ps, sems = tensors(nc, ctx)
        ln, ln2 = ln_semaphores(sems, "down_ln"), ln_semaphores(sems, "down_ln2")
        s1 = sems("down", "load w_hi w_lo d_ps d_in t_ps t_mul t_hi t_lo kr kr_hi kr_lo")
        s2 = sems("pair", "c_load a_exp consts a4 pw_load pw_hi pw_lo rows dtu du dbu da scan z y y_st f_ps f_hi f_lo "
                          "rot qr_hi qr_lo s_ps nmax exp prec norm t_ps2 pt_hi pt_lo o_ps ot_hi ot_lo w_ps x_add sp_passed dve_passed")
        g.cq = sb("latent_cq", [P, 2, KQ, 2 * NT], F32R)
        g.ckv = sb("latent_ckv", [P, 2, 2 * NT], F32R)
        g.kr = sb("latent_kr", [P, 2, NT], F32R)
        with nc.Fori(0, NB // 2) as bp:
            latent_down(nc, g, bp, s1, ln, ln2)
            latent_heads(nc, g, bp, s2)


def stage_gate1(nc, g):
    with ExitStack() as ctx:
        sb, ps, sems = tensors(nc, ctx)
        ln = ln_semaphores(sems, "gate_ln")
        s = sems("gate", "load y_load silu y01 y23 y yd gated t_ps x_add")
        stats, mv = sb("gate_stats", [P, NP, 6]), sb("gate_mv", [P, NP, 2])
        sd, rstd = sb("gate_sd", [P, NP]), sb("gate_rstd", [P, NP])
        xn = sb("gate_xn", [P, NP, D])
        y = sb("gate_y", [P, 4, CT, NT])
        u = sb("gate_u", [P, CT, NT])
        skip = sb("gate_skip", [P, CT])
        tb = [ps(f"gate_t{k}", [P, NT]) for k in range(NP)]
        with nc.Block() as block:
            @block.sync
            def _(sp):
                sp.dma_start(skip[:], g.dram["scan_ad"][:, CT * NS:]).then_inc(s["load"], 16)
                with sp.Fori(0, NB) as b:
                    sp.wait_ge(s["t_ps"], NP * b)
                    for q in range(4):
                        sp.dma_start(y[:, q], g.y_dram[4 * b + q]).then_inc(s["y_load"], 16)
                    sp.dma_start(u[:], g.u_dram[b]).then_inc(s["y_load"], 16)

            @block.scalar
            def _(act):
                with act.Fori(0, NB) as b:
                    ln_act_sqrt(act, ln, mv, sd, g.eps, NP, b)
                    for ct in range(CT):
                        act.wait_ge(ln["norm"], CT * b + ct + 1)
                        act.activation(xn[:, ct], xn[:, ct], ACT.Silu).then_inc(s["silu"], 1)

            @block.gpsimd
            def _(pool):
                with pool.Fori(0, NB) as b:
                    pool.wait_ge(s["y_load"], 80 * b + 80)
                    pool.tensor_tensor(y[:, 2], y[:, 2], y[:, 3], ALU.add).then_inc(s["y23"], 1)

            @block.vector
            def _(dve):
                dve.wait_ge(s["load"], 16)
                with dve.Fori(0, NB) as b:
                    dve.wait_ge(s["gated"], CT * b)
                    ln_dve_normalise(dve, ln, [g.X[:, b, t, :] for t in range(NP)], stats, mv, sd, rstd, xn, b, None)
                    dve.wait_ge(s["y_load"], 80 * b + 80)
                    dve.tensor_tensor(y[:, 0], y[:, 0], y[:, 1], ALU.add).then_inc(s["y01"], 1)
                    dve.wait_ge(s["y01"], b + 1)
                    for ct in range(CT):
                        last = dve.scalar_tensor_tensor(out=y[:, 0, ct], in0=u[:, ct], scalar=skip[:, ct:ct + 1], in1=y[:, 0, ct],
                                                        op0=ALU.mult, op1=ALU.add)
                    last.then_inc(s["yd"], 1)
                    dve.wait_ge(s["yd"], b + 1)
                    dve.wait_ge(s["y23"], b + 1)
                    dve.tensor_tensor(y[:, 0], y[:, 0], y[:, 2], ALU.add).then_inc(s["y"], 1)
                    dve.wait_ge(s["y"], b + 1)
                    for ct in range(CT):
                        dve.wait_ge(s["silu"], CT * b + ct + 1)
                        dve.tensor_tensor(y[:, 0, ct], y[:, 0, ct], xn[:, ct], ALU.mult).then_inc(s["gated"], 1)
                    for t in range(NP):
                        dve.wait_ge(s["t_ps"], NP * b + t + 1)
                        dve.tensor_tensor(g.X[:, b, t, :], g.X[:, b, t, :], tb[t][:], ALU.add).then_inc(s["x_add"], 1)

            @block.tensor
            def _(pe):
                with pe.Fori(0, NB) as b:
                    pe.wait_ge(s["gated"], CT * b + CT)
                    pe.wait_ge(s["x_add"], NP * b)
                    for t in range(NP):
                        for ct in range(CT):
                            last = pe.transpose(tb[t][:, ct * P:(ct + 1) * P], y[:, 0, ct, t * P:(t + 1) * P], g.ident[:])
                        last.then_inc(s["t_ps"], 1)


def stage_ffn1(nc, g):
    with ExitStack() as ctx:
        sb, ps, sems = tensors(nc, ctx)
        ln = ln_semaphores(sems, "ffn1_ln")
        s = sems("ffn1", "w1_load w2_load w3_load w_sum ones tot mean mclip mrec mq w_a w_b w_q idb a_step xq t_ps t_in g_ps u_ps sg "
                         "h b_step hq1 hq ht_ps ht_in o_ps x_out out passed")
        w_load = (s["w1_load"], s["w2_load"], s["w3_load"])
        NW = KD * FF1
        NTILE = NB * NP
        stats, mv = sb("ffn1_stats", [P, NTILE, 6]), sb("ffn1_mv", [P, NTILE, 2])
        sd, rstd = sb("ffn1_sd", [P, NTILE]), sb("ffn1_rstd", [P, NTILE])
        wraw = sb("ffn1_wraw", [P, 2, NW])
        wq = sb("ffn1_wq", [P, 3, NW], BF16)
        wsum = sb("ffn1_wsum", [P, 3])
        ones = sb("ffn1_ones", [P, P])
        mean, mrec, m127 = (sb(f"ffn1_{n}", [P, 3]) for n in ("mean", "mrec", "m127"))
        idb = sb("ffn1_idb", [P, P], BF16)
        xn = sb("ffn1_xn", [P, D])
        xq = sb("ffn1_xq", [P, D], BF16)
        xt = sb("ffn1_xt", [P, KD, P], BF16)
        xm, xr, xs = (sb(f"ffn1_{n}", [P, NTILE]) for n in ("xm", "xr", "xs"))
        hm, hr, hs = (sb(f"ffn1_{n}", [P, 1]) for n in ("hm", "hr", "hs"))
        dq = sb("ffn1_dq", [P, NTILE, 2])
        dq3 = sb("ffn1_dq3", [P, NTILE])
        sg = sb("ffn1_sg", [P, FF1])
        h = sb("ffn1_h", [P, 2, FF1])
        hq = sb("ffn1_hq", [P, 2, FF1], BF16)
        ht = sb("ffn1_ht", [P, KF1, P], BF16)
        gp, up = ps("ffn1_g", [P, 3 * NT]), ps("ffn1_u", [P, 3 * NT])
        tp = ps("ffn1_t", [P, 2 * NT], BF16)
        op = ps("ffn1_o", [P, NT])
        X = g.X[:].rearrange("p b t f -> p (b t) f")
        out = g.out.rearrange("t b p f -> t (b p) f")
        LOOP = NTILE - 3
        NA, NBS = 5, 5
        sizes = [(0, NT), (NT, NT), (2 * NT, FF1 - 2 * NT)]

        def steps(loop, body):
            with loop(0, LOOP) as t:
                body(t, 3)
            for left in (2, 1, 0):
                body(NTILE - 1 - left, left)

        with nc.Block() as block:
            @block.sync
            def _(sp):
                for n, src in enumerate((g.dram["ffn1_w1"], g.dram["ffn1_w2"], g.dram["ffn1_w3"])):
                    if n == 2:
                        sp.wait_ge(s["w_a"], 1)
                    sp.dma_start(wraw[:, n % 2], src).then_inc(w_load[n], 16)

                def store(t, left):
                    sp.wait_ge(s["x_out"], t + 1)
                    sp.dma_start(out[:, t, :], X[:, t, :]).then_inc(s["out"], 16)

                steps(sp.Fori, store)
                sp.wait_ge(s["out"], 16 * NTILE)

            @block.scalar
            def _(act):
                act.copy(idb[:], g.ident[:]).then_inc(s["idb"], 1)
                act.wait_ge(ln["var"], 1)
                act.activation(sd[:], mv[:, :, 1], ACT.Sqrt, bias=g.eps[:, 0:1]).then_inc(ln["sd"], 1)

                def x_in(t):
                    act.wait_ge(s["t_ps"], t + 1)
                    act.copy(xt[:], tp[:, 0:D].rearrange("p (c t) -> p c t", c=KD)).then_inc(s["t_in"], 1)

                def silu(t):
                    act.wait_ge(s["g_ps"], t + 1)
                    act.wait_ge(s["h"], t)
                    act.activation(sg[:], gp[:, 0:FF1], ACT.Silu, scale=dq[:, t, 0:1]).then_inc(s["sg"], 1)

                def h_in(t):
                    for n, (a, k) in enumerate(((0, 8), (8, KF1 - 8))):
                        act.wait_ge(s["ht_ps"], 2 * t + n + 1)
                        act.copy(ht[:, a:a + k], tp[:, 0:k * P].rearrange("p (c t) -> p c t", c=k)).then_inc(s["ht_in"], 1)

                x_in(0)
                silu(0)
                x_in(1)

                def tile(t, left):
                    if left >= 1:
                        silu(t + 1)
                    if left >= 2:
                        x_in(t + 2)
                    h_in(t)

                steps(act.Fori, tile)

            @block.gpsimd
            def _(pool):
                def quantise(t, par):
                    pool.wait_ge(s["b_step"], NBS * t + NBS)
                    pool.sem_inc(s["passed"], 1)
                    pool.tensor_scalar(h[:, par], h[:, par], hs[:], MAGIC, ALU.mult, ALU.add).then_inc(s["hq1"], 1)
                    pool.wait_ge(s["hq1"], t + 1)
                    pool.wait_ge(s["ht_ps"], 2 * t)
                    pool.sem_inc(s["passed"], 1)
                    pool.tensor_scalar(hq[:, par], h[:, par], -MAGIC, 1.0, ALU.add, ALU.mult).then_inc(s["hq"], 1)

                quantise(0, 0)

                def tile(t, left):
                    if left >= 1:
                        quantise(t + 1, 0)

                steps(pool.Fori, tile)

            @block.vector
            def _(dve):
                for t in range(NTILE):
                    last = dve.bn_stats(stats[:, t, :], X[:, t, :])
                last.then_inc(ln["stats"], 1)
                dve.memset(ones[:], 1.0).then_inc(s["ones"], 1)
                dve.wait_ge(ln["stats"], 1)
                for t in range(NTILE):
                    last = dve.bn_aggr(mv[:, t, :], stats[:, t, :])
                last.then_inc(ln["var"], 1)
                dve.wait_ge(ln["sd"], 1)
                dve.reciprocal(rstd[:], sd[:]).then_inc(ln["rstd"], 1)

                for n in range(3):
                    dve.wait_ge(w_load[n], 16)
                    dve.tensor_reduce(wsum[:, n:n + 1], wraw[:, n % 2], AX_X, ALU.add, apply_absolute_value=True).then_inc(s["w_sum"], 1)
                    dve.wait_ge(s["tot"], n + 1)
                    col = slice(n, n + 1)
                    dve.tensor_scalar(mean[:, col], op[:, col], 1.0 / (D * FF1), 1e-5, ALU.mult, ALU.max).then_inc(s["mean"], 1)
                    dve.wait_ge(s["mean"], n + 1)
                    dve.reciprocal(mrec[:, col], mean[:, col]).then_inc(s["mrec"], 1)
                    dve.tensor_scalar(m127[:, col], mean[:, col], 1.0 / 127.0, None, ALU.mult).then_inc(s["mq"], 1)
                    dve.wait_ge(s["mrec"], n + 1)
                    r = wraw[:, n % 2]
                    dve.tensor_scalar(r, r, mrec[:, col], MAGIC, ALU.mult, ALU.add).then_inc(s["w_b"], 1)
                    dve.wait_ge(s["w_b"], 2 * n + 1)
                    dve.tensor_scalar(r, r, MAGIC, 1.0, ALU.subtract, ALU.min).then_inc(s["w_b"], 1)
                    dve.wait_ge(s["w_b"], 2 * n + 2)
                    dve.tensor_scalar(wq[:, n], r, -1.0, None, ALU.max).then_inc(s["w_a"], 1)
                dve.wait_ge(s["mq"], 3)
                dve.wait_ge(ln["rstd"], 1)

                def x_quant(t):
                    one = lambda a: a[:, bass.ds(t, 1)]
                    dve.wait_ge(s["xq"], t)
                    dve.tensor_scalar(xn[:], X[:, t, :], mv[:, t, 0:1], one(rstd), ALU.subtract, ALU.mult).then_inc(s["a_step"], 1)
                    dve.wait_ge(s["a_step"], NA * t + 1)
                    dve.tensor_reduce(one(xm), xn[:], AX_X, ALU.max, apply_absolute_value=True).then_inc(s["a_step"], 1)
                    dve.wait_ge(s["a_step"], NA * t + 2)
                    dve.tensor_scalar(one(xr), one(xm), 1e-5, 1.0 / 127.0, ALU.max, ALU.mult).then_inc(s["a_step"], 1)
                    dve.wait_ge(s["a_step"], NA * t + 3)
                    dve.reciprocal(one(xs), one(xr)).then_inc(s["a_step"], 1)
                    dve.tensor_scalar(dq[:, t, :], mean[:, 0:2], one(xr), None, ALU.mult)
                    dve.wait_ge(s["a_step"], NA * t + 4)
                    dve.tensor_scalar(xn[:], xn[:], one(xs), MAGIC, ALU.mult, ALU.add).then_inc(s["a_step"], 1)
                    dve.wait_ge(s["a_step"], NA * t + 5)
                    dve.wait_ge(s["t_ps"], t)
                    dve.tensor_scalar(xq[:], xn[:], MAGIC, 127.0, ALU.subtract, ALU.min).then_inc(s["xq"], 1)

                def hidden(t, par):
                    one = lambda a: a[:, bass.ds(t, 1)]
                    dve.wait_ge(s["sg"], t + 1)
                    dve.wait_ge(s["u_ps"], t + 1)
                    dve.wait_ge(s["hq"], t)
                    dve.scalar_tensor_tensor(out=h[:, par], in0=up[:, 0:FF1], scalar=dq[:, t, 1:2], in1=sg[:],
                                             op0=ALU.mult, op1=ALU.mult).then_inc(s["h"], 1)
                    dve.wait_ge(s["h"], t + 1)
                    dve.tensor_reduce(hm[:], h[:, par], AX_X, ALU.max, apply_absolute_value=True).then_inc(s["b_step"], 1)
                    dve.wait_ge(s["b_step"], NBS * t + 1)
                    dve.tensor_scalar(hr[:], hm[:], 1e-5, 1.0 / 127.0, ALU.max, ALU.mult).then_inc(s["b_step"], 1)
                    dve.wait_ge(s["b_step"], NBS * t + 2)
                    dve.reciprocal(hs[:], hr[:]).then_inc(s["b_step"], 1)
                    dve.tensor_tensor(one(dq3), hr[:], mean[:, 2:3], ALU.mult).then_inc(s["b_step"], 2)

                def result(t):
                    dve.wait_ge(s["o_ps"], t + 1)
                    dve.scalar_tensor_tensor(out=X[:, t, :], in0=op[:], scalar=dq3[:, bass.ds(t, 1)], in1=X[:, t, :],
                                             op0=ALU.mult, op1=ALU.add).then_inc(s["x_out"], 1)

                x_quant(0)
                x_quant(1)
                hidden(0, 0)
                x_quant(2)

                def tile(t, left):
                    if left >= 1:
                        hidden(t + 1, 0)
                    if left >= 3:
                        x_quant(t + 3)
                    result(t)

                steps(dve.Fori, tile)

            @block.tensor
            def _(pe):
                pe.wait_ge(s["ones"], 1)
                for n in range(3):
                    pe.wait_ge(s["w_sum"], n + 1)
                    pe.wait_ge(s["mean"], n)
                    pe.matmul(op[:, n:n + 1], ones[:], wsum[:, n:n + 1], start=True, stop=True).then_inc(s["tot"], 1)
                pe.wait_ge(s["idb"], 1)
                pe.wait_ge(s["w_a"], 3)

                def turn_x(t):
                    pe.wait_ge(s["xq"], t + 1)
                    for c in range(KD):
                        last = pe.transpose(tp[:, c * P:(c + 1) * P], xq[:, c * P:(c + 1) * P], idb[:])
                    last.then_inc(s["t_ps"], 1)

                def gate_up(t):
                    pe.wait_ge(s["t_in"], t + 1)
                    for n, (bank, free, done) in enumerate(((gp, s["sg"], s["g_ps"]), (up, s["h"], s["u_ps"]))):
                        pe.wait_ge(free, t)
                        for a, size in sizes:
                            for k in range(KD):
                                last = pe.matmul(bank[:, a:a + size], xt[:, k, :], wq[:, n, k * FF1 + a:k * FF1 + a + size],
                                                 start=k == 0, stop=k == KD - 1)
                        last.then_inc(done, 1)

                def turn_h(t, par):
                    pe.wait_ge(s["hq"], t + 1)
                    for n, (a, k) in enumerate(((0, 8), (8, KF1 - 8))):
                        if n:
                            pe.wait_ge(s["ht_in"], 2 * t + 1)
                        for c in range(k):
                            last = pe.transpose(tp[:, c * P:(c + 1) * P], hq[:, par, (a + c) * P:(a + c + 1) * P], idb[:])
                        last.then_inc(s["ht_ps"], 1)

                def down(t):
                    pe.wait_ge(s["ht_in"], 2 * t + 2)
                    pe.wait_ge(s["x_out"], t)
                    for c in range(KF1):
                        last = pe.matmul(op[:], ht[:, c, :], wq[:, 2, c * D:(c + 1) * D], start=c == 0, stop=c == KF1 - 1)
                    last.then_inc(s["o_ps"], 1)

                turn_x(0)
                gate_up(0)
                turn_x(1)

                def tile(t, left):
                    if left >= 1:
                        gate_up(t + 1)
                    if left >= 2:
                        pe.wait_ge(s["ht_in"], 2 * t)
                        turn_x(t + 2)
                        pe.wait_ge(s["t_in"], t + 3)
                    turn_h(t, 0)
                    down(t)

                steps(pe.Fori, tile)


def decoder(nc, a, stages):
    with ExitStack() as ctx:
        sb, ps, sems = tensors(nc, ctx)
        g = State()
        g.dram = a
        g.x_in = a["x"].rearrange("b (p t) f -> t b p f", t=P)
        g.out = a["out"].rearrange("b (p t) f -> t b p f", t=P)
        g.u_dram = nc.dram_tensor("u_dram", (NB, P, CT, NT), F32).ap()
        g.dt_dram = nc.dram_tensor("dt_dram", (NB, P, CT, NT), F32).ap()
        g.bc_dram = nc.dram_tensor("bc_dram", (NB, 2 * NS, NT), F32).ap()
        g.y_dram = nc.dram_tensor("y_dram", (16, P, CT, NT), F32).ap()
        g.X = sb("X", [P, NB, NP, D])
        g.ident = sb("ident", [P, P])
        g.one, g.eps = sb("one", [P, 1]), sb("eps", [P, 1])
        with ExitStack() as cross:
            g.A = cross.enter_context(nc.sbuf_tensor("attention", [P, 2, NB, NP, NT], F32R))
            for f in (stage_context, stage_attention0, stage_cross0)[:stages]:
                f(nc, g)
        for f in (stage_ffn0, stage_latent1, stage_gate1, stage_ffn1)[:max(0, stages - 3)]:
            f(nc, g)
        if stages < 7:
            done = sems("end", "out")["out"]
            with nc.Block() as block:
                @block.sync
                def _(sp):
                    sp.dma_start(g.out, g.X[:]).then_inc(done, 16)
                    sp.wait_ge(done, 16)


STAGES = 7


def layouts(v):
    import numpy as np
    c = np.ascontiguousarray

    def rows(w, n):
        return w.reshape(n, P, -1).transpose(1, 0, 2)

    a = {"x": v["x"], "ident_in": np.eye(P, dtype=np.float32)}
    a["ctx_in"] = v["ctx_1024"].transpose(2, 0, 1).reshape(KC, P, NB * NT).transpose(1, 0, 2)
    wq, wk, wi = v["L0_xattn_Wq"].T, v["L0_xattn_Wk"].T, v["L1_xattn_in_proj_w"].T
    xp = v["L1_xattn_x_proj_w"]
    xp = np.concatenate([xp[DTR:], xp[:DTR]], 0).T
    a["ctx_w"] = np.concatenate([rows(np.concatenate([wq, wk, wi], 1), KC).reshape(P, -1), rows(xp, CT).reshape(P, -1)], 1)
    a["dt_w"] = v["L1_xattn_dt_proj_w"].T
    a["ctx_small"] = np.concatenate([
        v["L0_xattn_bq"][:, None], v["L0_xattn_bk"][:, None],
        v["L1_xattn_conv_w"].reshape(CT, P, NCONV).transpose(1, 0, 2).reshape(P, -1),
        v["L1_xattn_conv_b"].reshape(CT, P).T, v["L1_xattn_dt_proj_b"].reshape(CT, P).T], 1)
    grp = v["L0_attn_weight_qkv"].reshape(KV0, (R0 + 2) * DH0, D)
    n = R0 * DH0
    qkv = np.concatenate([grp[:, :n].reshape(-1, D), grp[:, n:n + DH0].reshape(-1, D), grp[:, n + DH0:].reshape(-1, D)], 0)
    a["att0_w"] = np.concatenate([rows(qkv.T, KD).reshape(P, -1), rows(v["L0_attn_weight_proj"].T, KD).reshape(P, -1)], 1)
    wg, wu = (v[k].reshape(KD, P, C0, P, 4).transpose(2, 4, 1, 0, 3).reshape(C0 * 4, P, KD * P) for k in ("L0_ffn_w_gate", "L0_ffn_w_up"))
    wd = v["L0_ffn_w_down"].reshape(C0, P, 4, D).transpose(0, 2, 1, 3).reshape(C0 * 4, P, D)
    a["ffn0_w"] = np.concatenate([wg, wu, wd], 2)
    def halves(w, axis):
        return np.concatenate([w.take(range(0, DR, 2), axis), w.take(range(1, DR, 2), axis)], axis)
    kvd = v["L1_attn_Wkv_down"]
    a["down1_w"] = rows(np.concatenate([v["L1_attn_Wq_down"], kvd[:KVL], halves(kvd[KVL:], 0)], 0).T, KD).reshape(P, -1)
    wq = np.concatenate([v["L1_attn_Wq_up"], v["L1_attn_bq_up"][:, None]], 1).reshape(H1, DN + DR, QL + 1)
    rope = halves(wq[:, DN:], 1)
    swap = np.concatenate([rope[:, DR // 2:], rope[:, :DR // 2]], 1)
    pair = lambda t: t.reshape(PAIRS, -1, QL + 1)
    wq = np.concatenate([pair(wq[:, :DN]), pair(rope), pair(swap)], 1)
    bq, wq = wq[:, :, QL], wq[:, :, :QL]
    wkv = np.concatenate([v["L1_attn_Wkv_up"], v["L1_attn_bkv_up"][:, None]], 1).reshape(PAIRS, 2, 2, P, KVL + 1)
    wkv = wkv.transpose(0, 2, 1, 3, 4).reshape(PAIRS, 4 * P, KVL + 1)
    bkv, wkv = wkv[:, :, KVL], wkv[:, :, :KVL]
    wo = v["L1_attn_Wo"].T.reshape(PAIRS, 2, P, D)
    a["pair_w"] = np.concatenate([wq.transpose(0, 2, 1).reshape(PAIRS, KQ, P, 4 * P).transpose(0, 2, 1, 3).reshape(PAIRS, P, -1),
                                  wkv.transpose(0, 2, 1), wo.transpose(0, 2, 1, 3).reshape(PAIRS, P, -1)], 2)
    a["pair_b"] = np.concatenate([bq.reshape(PAIRS, 4, P), bkv.reshape(PAIRS, 4, P)], 1).transpose(0, 2, 1)
    a["ln_gb"] = np.stack([v[k].reshape(-1, P)[j] for k in ("L1_attn_q_ln_g", "L1_attn_q_ln_b") for j in range(KQ)]
                          + [v["L1_attn_kv_ln_g"], v["L1_attn_kv_ln_b"]], 1)
    freq = (1.0 / np.float32(10000.0) ** (np.arange(0, DR, 2, dtype=np.float32) / np.float32(DR))).astype(np.float32)
    ang = np.arange(NT, dtype=np.float32)[:, None] * freq
    cos, sin = np.cos(ang).astype(np.float32), np.sin(ang).astype(np.float32)
    cs = np.stack([np.concatenate([cos, cos], 1), np.concatenate([-sin, sin], 1)], 0)
    a["rope_t"] = cs.reshape(2, NP, P, DR).transpose(2, 0, 1, 3)
    a["rope_f"] = np.concatenate([cs, cs], 2).transpose(2, 0, 1)
    a["scan_ad"] = np.concatenate([v["L1_xattn_A_log"].reshape(CT, P, NS).transpose(1, 0, 2).reshape(P, -1),
                                   v["L1_xattn_D"].reshape(CT, P).T], 1)
    a["ffn1_w1"], a["ffn1_w2"] = (rows(v[k].T, KD).reshape(P, -1) for k in ("L1_ffn_w1", "L1_ffn_w2"))
    a["ffn1_w3"] = rows(v["L1_ffn_w3"].T, KF1).reshape(P, -1)
    return {k: c(t) for k, t in a.items()}


def kernel(**inputs):
    import numpy as np
    import concourse.bacc as bacc
    from concourse.bass_utils import run_bass_kernel_spmd

    nc = bacc.Bacc("TRN2", target_bir_lowering=False, num_devices=1)
    arrays = {f"in_{k}": t for k, t in layouts({k: np.asarray(t) for k, t in inputs.items()}).items()}
    drams = {k[3:]: nc.dram_tensor(k, t.shape, mybir.dt.from_np(t.dtype), kind="ExternalInput").ap() for k, t in arrays.items()}
    drams["out"] = nc.dram_tensor("out_dram", (NB, NT, D), F32, kind="ExternalOutput").ap()
    decoder(nc, drams, STAGES)
    r = run_bass_kernel_spmd(nc, [arrays], core_ids=[0])
    return r.results[0]["out_dram"]
```

```python
from contextlib import ExitStack

import concourse.bass as bass
from concourse import mybir

F32 = mybir.dt.float32
F32R = mybir.dt.float32r
BF16 = mybir.dt.bfloat16
ALU = mybir.AluOpType
ACT = mybir.ActivationFunctionType
AX_X = mybir.AxisListType.X

P = 128
NB = 4
NT = 512
NP = NT // P
D = 512
KD = D // P
EPS = 1e-5

H0, KV0, DH0 = 16, 4, 32
R0 = H0 // KV0
QKV0 = H0 * DH0 + 2 * KV0 * DH0
DC = 256
KC = DC // P
DI = 512
CT = DI // P
NS = 16
DTR = 16
NCONV = 4
SMALL = 2.0 ** -7
FF0 = 2048
C0 = FF0 // (4 * P)
PIECE = 2 * KD * P + D
H1, DN, DR, DV, QL, KVL = 16, 128, 64, 128, 384, 128
KQ = QL // P
PAIRS = H1 // 2
WQ1, WKV1, WO1 = KQ * 4 * P, 4 * P, 2 * D
WPAIR = WQ1 + WKV1 + WO1
SCALE1 = float((DN + DR) ** -0.5)
FF1 = 1408
KF1 = FF1 // P
MAGIC = 12582912.0


class State:
    pass


def clear_semaphores(nc, handles):
    nc.clear_and_free_semaphores(handles)
    with nc.Block():
        pass


def tensors(nc, ctx):
    handles = []
    ctx.callback(clear_semaphores, nc, handles)

    def sb(name, shape, dt=F32):
        return ctx.enter_context(nc.sbuf_tensor(name, shape, dt))

    def ps(name, shape, dt=F32):
        return ctx.enter_context(nc.psum_tensor(name, shape, dt))

    def sems(prefix, names):
        made = {n: nc.alloc_semaphore(f"{prefix}_{n}") for n in names.split()}
        handles.extend(made.values())
        return made

    return sb, ps, sems


def mm3(pe, out, a, b, start=True, stop=True):
    pe.matmul(out, a[0], b[0], start=start, stop=False)
    pe.matmul(out, a[0], b[1], start=False, stop=False)
    return pe.matmul(out, a[1], b[0], start=False, stop=stop)


def lo_part(dve, out, full, hi):
    return dve.tensor_tensor(out, full, hi.bitcast(F32), ALU.subtract)


def ln_semaphores(sems, prefix):
    return sems(prefix, "stats passed var sd rstd norm xt hi lo")


def ln_dve_normalise(dve, s, tiles, stats, mv, sd, rstd, xn, count, first, width=D):
    n = len(tiles)
    for k, tile in enumerate(tiles):
        last = dve.bn_stats(stats[:, k, :], tile)
    last.then_inc(s["stats"], 1)
    dve.wait_ge(s["stats"], count + 1)
    dve.sem_inc(s["passed"], 1)
    for k in range(n):
        last = dve.bn_aggr(mv[:, k, :], stats[:, k, :])
    last.then_inc(s["var"], 1)
    dve.wait_ge(s["sd"], count + 1)
    dve.reciprocal(rstd[:, 0:n], sd[:, 0:n]).then_inc(s["rstd"], 1)
    dve.wait_ge(s["rstd"], count + 1)
    if first is not None:
        dve.wait_ge(s["xt"], first)
    for k, tile in enumerate(tiles):
        dve.tensor_scalar(xn[:, k, :], tile, mv[:, k, 0:1], rstd[:, k:k + 1], ALU.subtract,
                          ALU.mult).then_inc(s["norm"], 1)


def ln_act_sqrt(act, s, mv, sd, eps, n, count):
    act.wait_ge(s["var"], count + 1)
    act.activation(sd[:, 0:n], mv[:, 0:n, 1], ACT.Sqrt, bias=eps[:, 0:1]).then_inc(s["sd"], 1)


def stage_context(nc, g):
    with ExitStack() as ctx:
        sb, ps, sems = tensors(nc, ctx)
        s = sems("ctx", "load x_load w_hi w_lo c_load c_hi c_lo q_ps k_ps q_hi k_hi qk_lo x_ps x_in "
                        "e_ps e_max e_exp e_rec a_norm a_ps a_in t1 t2 t3 conv u u_hi u_lo xd_ps d_hi d_lo bc dt_ps "
                        "dt_abs dt_exp dt_ln dt_relu dt_sum ser dt du st_du st_u st_bc st_dt pad")
        craw = sb("ctx_raw", [P, KC, NT])
        c = sb("ctx_split", [P, 2, KC, NT], F32R)
        wraw = sb("ctx_wraw", [P, g.dram["ctx_w"].shape[1]])
        w = sb("ctx_w", [P, 2, g.dram["ctx_w"].shape[1]], F32R)
        dtw_raw = sb("ctx_dtw_raw", [48, DI])
        dtw = sb("ctx_dtw", [48, 2, DI], F32R)
        small = sb("ctx_small", [P, 2 + CT * NCONV + 2 * CT])
        qk = sb("ctx_qk", [P, 2, 2, NT], F32R)
        e = sb("ctx_exp", [P, NP, NT])
        nmax, esum, erec = sb("ctx_nmax", [P, NP]), sb("ctx_esum", [P, NP]), sb("ctx_erec", [P, NP])
        xin = sb("ctx_xin", [P, CT, NT + NCONV - 1])
        ta, tb = sb("ctx_ta", [P, CT, NT]), sb("ctx_tb", [P, CT, NT])
        series, logs = sb("ctx_series", [P, CT, NT]), sb("ctx_logs", [P, CT, NT])
        u = sb("ctx_u", [P, CT, NT])
        us = sb("ctx_us", [P, 2, CT, NT], F32R)
        dlow = sb("ctx_dlow", [48, 2, NT], F32R)
        bc = sb("ctx_bc", [32, NT])
        pa = [ps(f"ctx_p{k}", [P, NT]) for k in range(8)]

        CW = 2 * P + DI

        def wcol(k, a, n):
            return [w[:, h, k * CW + a:k * CW + a + n] for h in range(2)]

        def xproj(k):
            return [w[:, h, KC * CW + 48 * k:KC * CW + 48 * k + 48] for h in range(2)]

        conv_w = lambda ct, t: small[:, 2 + ct * NCONV + t:3 + ct * NCONV + t]
        conv_b = lambda ct: small[:, 2 + CT * NCONV + ct:3 + CT * NCONV + ct]
        dt_b = lambda ct: small[:, 2 + CT * (NCONV + 1) + ct:3 + CT * (NCONV + 1) + ct]

        def batches(loop, body):
            with loop(0, NB - 1) as b:
                body(b, False)
            body(NB - 1, True)

        with nc.Block() as block:
            @block.sync
            def _(sp):
                sp.dma_start(craw[:], g.dram["ctx_in"][:, :, 0:NT]).then_inc(s["c_load"], 16)
                sp.dma_start(wraw[:], g.dram["ctx_w"]).then_inc(s["load"], 16)
                sp.dma_start(dtw_raw[32:48, :], g.dram["dt_w"]).then_inc(s["load"], 16)
                sp.dma_start(small[:], g.dram["ctx_small"]).then_inc(s["load"], 16)
                sp.dma_start(g.ident[:], g.dram["ident_in"]).then_inc(s["load"], 16)
                sp.dma_start(g.X[:, 0:2], g.x_in[:, 0:2]).then_inc(s["x_load"], 16)
                sp.dma_start(g.X[:, 2:4], g.x_in[:, 2:4]).then_inc(s["x_load"], 16)

                def batch(b, last):
                    if not last:
                        sp.wait_ge(s["c_lo"], b + 1)
                        sp.dma_start(craw[:], g.dram["ctx_in"][:, :, bass.ds((b + 1) * NT, NT)]).then_inc(s["c_load"], 16)
                    sp.wait_ge(s["u"], CT * b + CT)
                    sp.dma_start(g.u_dram[b], u[:]).then_inc(s["st_u"], 16)
                    sp.wait_ge(s["bc"], b + 1)
                    sp.dma_start(g.bc_dram[b], bc[:]).then_inc(s["st_bc"], 16)
                    sp.wait_ge(s["dt"], b + 1)
                    sp.dma_start(g.dt_dram[b], tb[:]).then_inc(s["st_dt"], 16)
                    sp.wait_ge(s["du"], b + 1)
                    sp.dma_start(g.du_dram[b], series[:]).then_inc(s["st_du"], 16)

                batches(sp.Fori, batch)
                for stored in ("st_u", "st_bc", "st_dt", "st_du"):
                    sp.wait_ge(s[stored], 16 * NB)
                sp.wait_ge(s["load"], 64)
                sp.wait_ge(s["x_load"], 32)

            @block.scalar
            def _(act):
                act.wait_ge(s["load"], 64)
                act.copy(w[:, 0], wraw[:]).then_inc(s["w_hi"], 1)
                act.copy(dtw[32:48, 0], dtw_raw[32:48]).then_inc(s["w_hi"], 1)

                def c_hi(b):
                    act.wait_ge(s["c_load"], 16 * b + 16)
                    act.wait_ge(s["x_ps"], CT * b)
                    act.copy(c[:, 0], craw[:]).then_inc(s["c_hi"], 1)

                def qk_hi(b):
                    for n, (ready, done) in enumerate(((s["q_ps"], s["q_hi"]), (s["k_ps"], s["k_hi"]))):
                        act.wait_ge(ready, b + 1)
                        act.activation(qk[:, 0, n], pa[n][:], ACT.Identity, bias=small[:, n:n + 1]).then_inc(done, 1)

                def x_in(b):
                    act.wait_ge(s["conv"], CT * b)
                    for ct in range(CT):
                        act.wait_ge(s["x_ps"], CT * b + ct + 1)
                        act.copy(xin[:, ct, NCONV - 1:], pa[2 + ct][:]).then_inc(s["x_in"], 1)

                def scores_exp(b):
                    act.wait_ge(s["a_ps"], NP * b)
                    act.wait_ge(s["e_rec"], b)
                    for n in range(NP):
                        act.wait_ge(s["e_max"], NP * b + n + 1)
                        act.activation(e[:, n], pa[(6 + n) % 8][:], ACT.Exp, bias=nmax[:, n:n + 1],
                                       accum_out=esum[:, n:n + 1]).then_inc(s["e_exp"], 1)

                def batch(b, last):
                    act.wait_ge(s["st_u"], 16 * b)
                    act.wait_ge(s["u_lo"], CT * b)
                    act.wait_ge(s["du"], b)
                    for ct in range(CT):
                        act.wait_ge(s["conv"], CT * b + ct + 1)
                        act.activation(u[:, ct], logs[:, ct], ACT.Silu, bias=conv_b(ct)).then_inc(s["u"], 1)
                    for ct in range(CT):
                        act.wait_ge(s["u"], CT * b + ct + 1)
                        act.wait_ge(s["xd_ps"], b)
                        act.copy(us[:, 0, ct], u[:, ct]).then_inc(s["u_hi"], 1)
                    if not last:
                        c_hi(b + 1)
                    act.wait_ge(s["xd_ps"], b + 1)
                    act.wait_ge(s["dt_ps"], CT * b)
                    act.copy(dlow[32:48, 0], pa[2][32:48]).then_inc(s["d_hi"], 1)
                    act.wait_ge(s["st_bc"], 16 * b)
                    act.copy(bc[:], pa[2][0:32]).then_inc(s["bc"], 1)
                    for n in range(NP):
                        act.wait_ge(s["a_ps"], NP * b + n + 1)
                        act.copy(g.A[:, b, n], pa[n % 2][:]).then_inc(s["a_in"], 1)
                    for ct in range(CT):
                        act.wait_ge(s["dt_relu"], CT * b + ct + 1)
                        act.activation(ta[:, ct], pa[3 + ct][:], ACT.Abs, bias=dt_b(ct)).then_inc(s["dt_abs"], 1)
                    act.wait_ge(s["dt_abs"], CT * b + CT)
                    act.activation(ta[:], ta[:], ACT.Exp, scale=-1.0).then_inc(s["dt_exp"], 1)
                    if not last:
                        qk_hi(b + 1)
                        x_in(b + 1)
                        scores_exp(b + 1)
                    act.wait_ge(s["dt_exp"], b + 1)
                    act.activation(logs[:], ta[:], ACT.Ln, bias=g.one[:, 0:1]).then_inc(s["dt_ln"], 1)

                c_hi(0)
                qk_hi(0)
                act.wait_ge(s["pad"], 1)
                x_in(0)
                scores_exp(0)
                batches(act.Fori, batch)

            @block.gpsimd
            def _(pool):
                with pool.Fori(0, NB) as b:
                    pool.wait_ge(s["dt"], b + 1)
                    pool.tensor_tensor(series[:], u[:], tb[:], ALU.mult).then_inc(s["du"], 1)

            @block.vector
            def _(dve):
                dve.memset(g.one[:], 1.0)
                dve.memset(g.eps[:], EPS)
                dve.memset(xin[:, :, 0:NCONV - 1], 0.0).then_inc(s["pad"], 1)
                dve.wait_ge(s["w_hi"], 2)
                lo_part(dve, w[:, 1], wraw[:], w[:, 0]).then_inc(s["w_lo"], 1)
                lo_part(dve, dtw[32:48, 1], dtw_raw[32:48], dtw[32:48, 0]).then_inc(s["w_lo"], 1)

                def c_lo(b):
                    dve.wait_ge(s["c_hi"], b + 1)
                    lo_part(dve, c[:, 1], craw[:], c[:, 0]).then_inc(s["c_lo"], 1)

                def qk_lo(b):
                    for n, ready in enumerate((s["q_hi"], s["k_hi"])):
                        dve.wait_ge(ready, b + 1)
                        dve.scalar_tensor_tensor(out=qk[:, 1, n], in0=pa[n][:], scalar=small[:, n:n + 1],
                                                 in1=qk[:, 0, n].bitcast(F32), op0=ALU.add,
                                                 op1=ALU.subtract).then_inc(s["qk_lo"], 1)

                def maxima(b):
                    for n in range(NP):
                        dve.wait_ge(s["e_ps"], NP * b + n + 1)
                        dve.tensor_reduce(nmax[:, n:n + 1], pa[(6 + n) % 8][:], AX_X, ALU.max,
                                          negate=True).then_inc(s["e_max"], 1)

                def batch(b, last):
                    for t, dst in enumerate((ta, logs, ta, logs)):
                        for ct in range(CT):
                            if t == 0:
                                dve.wait_ge(s["x_in"], CT * b + ct + 1)
                                last_op = dve.tensor_scalar(dst[:, ct], xin[:, ct, 0:NT], conv_w(ct, 0), None, ALU.mult)
                            else:
                                dve.wait_ge(s[f"t{t}"], CT * b + ct + 1)
                                src = logs if t == 2 else ta
                                last_op = dve.scalar_tensor_tensor(out=dst[:, ct], in0=xin[:, ct, t:t + NT], scalar=conv_w(ct, t),
                                                                   in1=src[:, ct], op0=ALU.mult, op1=ALU.add)
                            last_op.then_inc(s["conv" if t == 3 else f"t{t + 1}"], 1)
                    dve.wait_ge(s["e_exp"], NP * b + NP)
                    dve.reciprocal(erec[:], esum[:]).then_inc(s["e_rec"], 1)
                    dve.wait_ge(s["e_rec"], b + 1)
                    for n in range(NP):
                        dve.tensor_scalar(e[:, n], e[:, n], erec[:, n:n + 1], None, ALU.mult).then_inc(s["a_norm"], 1)
                    for ct in range(CT):
                        dve.wait_ge(s["u_hi"], CT * b + ct + 1)
                        lo_part(dve, us[:, 1, ct], u[:, ct], us[:, 0, ct]).then_inc(s["u_lo"], 1)
                    if not last:
                        c_lo(b + 1)
                    dve.wait_ge(s["d_hi"], b + 1)
                    dve.wait_ge(s["bc"], b + 1)
                    lo_part(dve, dlow[32:48, 1], pa[2][32:48], dlow[32:48, 0]).then_inc(s["d_lo"], 1)
                    dve.wait_ge(s["st_dt"], 16 * b)
                    dve.wait_ge(s["du"], b)
                    for ct in range(CT):
                        dve.wait_ge(s["dt_ps"], CT * b + ct + 1)
                        dve.tensor_scalar(tb[:, ct], pa[3 + ct][:], dt_b(ct), 0.0, ALU.add, ALU.max).then_inc(s["dt_relu"], 1)
                    dve.wait_ge(s["dt_exp"], b + 1)
                    dve.wait_ge(s["st_du"], 16 * b)
                    dve.tensor_scalar(series[:], ta[:], -0.25, 1.0 / 3.0, ALU.mult, ALU.add).then_inc(s["ser"], 1)
                    if not last:
                        qk_lo(b + 1)
                    dve.wait_ge(s["ser"], 6 * b + 1)
                    dve.tensor_tensor(series[:], series[:], ta[:], ALU.mult).then_inc(s["ser"], 1)
                    if not last:
                        maxima(b + 1)
                    for n, term in ((2, -0.5), (3, 1.0)):
                        for ct in range(CT):
                            dve.wait_ge(s["ser"], 6 * b + n)
                            last_op = dve.scalar_tensor_tensor(out=series[:, ct], in0=series[:, ct], scalar=term, in1=ta[:, ct],
                                                               op0=ALU.add, op1=ALU.mult)
                        last_op.then_inc(s["ser"], 1)
                    dve.wait_ge(s["dt_ln"], b + 1)
                    dve.wait_ge(s["ser"], 6 * b + 4)
                    dve.tensor_tensor(series[:], series[:], logs[:], ALU.subtract).then_inc(s["ser"], 1)
                    dve.wait_ge(s["dt_relu"], CT * b + CT)
                    dve.tensor_tensor(tb[:], tb[:], logs[:], ALU.add).then_inc(s["dt_sum"], 1)
                    dve.wait_ge(s["ser"], 6 * b + 5)
                    for ct in range(CT):
                        last_op = dve.scalar_tensor_tensor(out=series[:, ct], in0=ta[:, ct], scalar=SMALL, in1=series[:, ct],
                                                           op0=ALU.is_lt, op1=ALU.mult)
                    last_op.then_inc(s["ser"], 1)
                    dve.wait_ge(s["ser"], 6 * b + 6)
                    dve.wait_ge(s["dt_sum"], b + 1)
                    dve.tensor_tensor(tb[:], tb[:], series[:], ALU.add).then_inc(s["dt"], 1)

                c_lo(0)
                qk_lo(0)
                maxima(0)
                batches(dve.Fori, batch)

            @block.tensor
            def _(pe):
                def front(b, first):
                    pe.wait_ge(s["c_lo"], b + 1)
                    if not first:
                        pe.wait_ge(s["a_in"], NP * b)
                    cs = lambda k: [c[:, h, k] for h in range(2)]
                    for n, done in enumerate((s["q_ps"], s["k_ps"])):
                        for k in range(KC):
                            last = mm3(pe, pa[n][:], wcol(k, n * P, P), cs(k), k == 0, k == KC - 1)
                        last.then_inc(done, 1)
                    for ct in range(CT):
                        if ct == 0 and not first:
                            pe.wait_ge(s["d_lo"], b)
                            pe.wait_ge(s["bc"], b)
                        if not first:
                            pe.wait_ge(s["dt_abs"], CT * (b - 1) + ct)
                        for k in range(KC):
                            last = mm3(pe, pa[2 + ct][:], wcol(k, (2 + ct) * P, P), cs(k), k == 0, k == KC - 1)
                        last.then_inc(s["x_ps"], 1)
                    pe.wait_ge(s["qk_lo"], 2 * b + 2)
                    if not first:
                        pe.wait_ge(s["dt_abs"], CT * b)
                    for n in range(NP):
                        q = [qk[:, h, 0, n * P:(n + 1) * P] for h in range(2)]
                        mm3(pe, pa[(6 + n) % 8][:], q, [qk[:, h, 1] for h in range(2)]).then_inc(s["e_ps"], 1)

                def batch(b, last):
                    pe.wait_ge(s["a_norm"], NP * b + NP)
                    pe.wait_ge(s["e_exp"], NP * b + NP)
                    for n in range(2):
                        for m in range(NP):
                            turned = pe.transpose(pa[n % 2][:, m * P:(m + 1) * P], e[:, m, n * P:(n + 1) * P], g.ident[:])
                        turned.then_inc(s["a_ps"], 1)
                    pe.wait_ge(s["x_in"], CT * b + CT)
                    for ct in range(CT):
                        pe.wait_ge(s["u_lo"], CT * b + ct + 1)
                        done = mm3(pe, pa[2][0:48], xproj(ct), [us[:, h, ct] for h in range(2)], ct == 0, ct == CT - 1)
                    done.then_inc(s["xd_ps"], 1)
                    for n in range(2, NP):
                        pe.wait_ge(s["a_in"], NP * b + n - 1)
                        for m in range(NP):
                            turned = pe.transpose(pa[n % 2][:, m * P:(m + 1) * P], e[:, m, n * P:(n + 1) * P], g.ident[:])
                        turned.then_inc(s["a_ps"], 1)
                    pe.wait_ge(s["d_lo"], b + 1)
                    for ct in range(CT):
                        mm3(pe, pa[3 + ct][:], [dtw[32:48, h, ct * P:(ct + 1) * P] for h in range(2)],
                            [dlow[32:48, h] for h in range(2)]).then_inc(s["dt_ps"], 1)
                    if not last:
                        front(b + 1, False)

                pe.wait_ge(s["w_lo"], 2)
                front(0, True)
                batches(pe.Fori, batch)


def ln_pe_transpose(pe, s, xn, banks, ident, n, base):
    for k in range(n):
        pe.wait_ge(s["norm"], base + k + 1)
        pe.wait_ge(s["lo"], base + max(0, k - 1))
        for c in range(KD):
            last = pe.transpose(banks[k % 2][:, c * P:(c + 1) * P], xn[:, k, c * P:(c + 1) * P], ident[:])
        last.then_inc(s["xt"], 1)


def ln_act_hi(act, s, xt, banks, n, base):
    for k in range(n):
        act.wait_ge(s["xt"], base + k + 1)
        act.copy(xt[:, 0, :, k * P:(k + 1) * P], banks[k % 2][:].rearrange("p (c t) -> p c t", c=KD)).then_inc(s["hi"], 1)


def ln_dve_lo(dve, s, xt, banks, n, base):
    for k in range(n):
        dve.wait_ge(s["hi"], base + k + 1)
        lo_part(dve, xt[:, 1, :, k * P:(k + 1) * P], banks[k % 2][:].rearrange("p (c t) -> p c t", c=KD),
                xt[:, 0, :, k * P:(k + 1) * P]).then_inc(s["lo"], 1)


def stage_attention0(nc, g):
    with ExitStack() as ctx:
        sb, ps, sems = tensors(nc, ctx)
        ln = ln_semaphores(sems, "att0_ln")
        s = sems("att0", "load w_hi w_lo qkv_ps qkv_in prod dot mx sub ex sm rc probs pv sum1 att at_ps at_hi at_lo o_ps x_add mask passed")
        NW = KD * QKV0
        wraw = sb("att0_wraw", [P, KD * (QKV0 + D)])
        w = sb("att0_w", [P, 2, KD * (QKV0 + D)], F32R)
        stats, mv = sb("att0_stats", [P, NB, 6]), sb("att0_mv", [P, NB, 2])
        sd, rstd = sb("att0_sd", [P, NB]), sb("att0_rstd", [P, NB])
        xn = sb("att0_xn", [P, NB, D])
        xt = sb("att0_xt", [P, 2, KD, NB * P], F32R)
        qkv = sb("att0_qkv", [P, 2, NB, QKV0])
        att = sb("att0_att", [P, NB, D])
        at = sb("att0_at", [P, 2, KD, NB * P], F32R)
        prod = sb("att0_prod", [P, 2, D])
        score = sb("att0_score", [P, NB, H0, NB])
        shifted, probs = sb("att0_shifted", [P, NB, H0, NB]), sb("att0_probs", [P, NB, H0, NB])
        mx, sm, rc = (sb(f"att0_{n}", [P, NB * H0]) for n in ("mx", "sm", "rc"))
        pv = wraw[:, 0:2 * NB * D].rearrange("p (i j f) -> p i j f", i=2, j=NB)
        tp = [ps(f"att0_tp{k}", [P, NT]) for k in range(2)]
        qp = [ps(f"att0_q{k}", [P, NT]) for k in range(2)]
        kp = [ps(f"att0_k{k}", [P, NT]) for k in range(2)]
        op = [ps(f"att0_o{k}", [P, NT]) for k in range(2)]
        pairs = [(i, j) for i in range(NB) for j in range(i + 1)]
        NPAIR = len(pairs)
        KO, VO = H0 * DH0, H0 * DH0 + KV0 * DH0

        def wslice(k, a, n):
            return [w[:, h, k * QKV0 + a:k * QKV0 + a + n] for h in range(2)]

        def wo(k):
            return [w[:, h, NW + k * D:NW + (k + 1) * D] for h in range(2)]

        def heads(t):
            return t.rearrange("p (g r d) -> p g r d", g=KV0, r=R0)

        def grouped(t):
            return t.rearrange("p (g r d) -> p g r d", g=KV0, r=1).to_broadcast([P, KV0, R0, DH0])

        def tiles(loop, body):
            with loop(0, NP - 2) as p:
                body(p, 2)
            body(NP - 2, 1)
            body(NP - 1, 0)

        def ring(t, p):
            return t[:, p % 2]

        with nc.Block() as block:
            @block.sync
            def _(sp):
                sp.dma_start(wraw[:], g.dram["att0_w"]).then_inc(s["load"], 16)

            @block.scalar
            def _(act):
                act.wait_ge(s["load"], 16)
                act.copy(w[:, 0], wraw[:]).then_inc(s["w_hi"], 1)

                def qkv_in(p, b):
                    act.wait_ge(s["qkv_ps"], NB * p + b + 1)
                    act.copy(ring(qkv, p)[:, b, 0:KO], qp[b % 2][:])
                    act.copy(ring(qkv, p)[:, b, KO:], kp[b % 2][:, 0:QKV0 - KO]).then_inc(s["qkv_in"], 1)

                ln_act_sqrt(act, ln, mv, sd, g.eps, NB, 0)
                ln_act_hi(act, ln, xt, tp, NB, 0)
                ln_act_sqrt(act, ln, mv, sd, g.eps, NB, 1)
                for b in range(NB):
                    qkv_in(0, b)

                def tile(p, behind):
                    act.wait_ge(s["sub"], p + 1)
                    act.wait_ge(s["pv"], NPAIR * p)
                    act.activation(probs[:], shifted[:], ACT.Exp, scale=float(DH0 ** -0.5)).then_inc(s["ex"], 1)
                    if behind:
                        ln_act_hi(act, ln, xt, tp, NB, NB * (p + 1))
                        for b in range(NB):
                            qkv_in(p + 1, b)
                            if behind == 2 and b == 1:
                                ln_act_sqrt(act, ln, mv, sd, g.eps, NB, p + 2)
                    for i in range(NB):
                        act.wait_ge(s["at_ps"], NB * p + i + 1)
                        act.copy(at[:, 0, :, i * P:(i + 1) * P],
                                 tp[i % 2][:].rearrange("p (c t) -> p c t", c=KD)).then_inc(s["at_hi"], 1)

                tiles(act.Fori, tile)

            @block.gpsimd
            def _(pool):
                def products(p):
                    for n, (i, j) in enumerate(pairs):
                        pool.wait_ge(s["qkv_in"], NB * p + i + 1)
                        pool.wait_ge(s["dot"], NPAIR * p + max(0, n - 1))
                        pool.sem_inc(s["passed"], 1)
                        t = ring(qkv, p)
                        pool.tensor_tensor(heads(prod[:, n % 2]), heads(t[:, i, 0:KO]), grouped(t[:, j, KO:VO]),
                                           ALU.mult).then_inc(s["prod"], 1)

                def tile(p, behind):
                    for i in range(NB):
                        pool.wait_ge(s["pv"], NPAIR * p + (i + 1) * (i + 2) // 2)
                        pool.wait_ge(s["at_ps"], NB * p)
                        v = pv[:, i % 2]
                        if i == 0:
                            pool.sem_inc(s["passed"], 1)
                            pool.tensor_copy(att[:, 0], v[:, 0]).then_inc(s["att"], 1)
                        elif i == 1:
                            pool.tensor_tensor(att[:, 1], v[:, 0], v[:, 1], ALU.add).then_inc(s["att"], 1)
                        elif i == 2:
                            pool.tensor_tensor(v[:, 0], v[:, 0], v[:, 1], ALU.add).then_inc(s["sum1"], 1)
                            pool.wait_ge(s["sum1"], 3 * p + 1)
                            pool.tensor_tensor(att[:, 2], v[:, 0], v[:, 2], ALU.add).then_inc(s["att"], 1)
                        else:
                            pool.tensor_tensor(v[:, 0], v[:, 0], v[:, 1], ALU.add).then_inc(s["sum1"], 1)
                            pool.tensor_tensor(v[:, 2], v[:, 2], v[:, 3], ALU.add).then_inc(s["sum1"], 1)
                            pool.wait_ge(s["sum1"], 3 * p + 3)
                            pool.tensor_tensor(att[:, 3], v[:, 0], v[:, 2], ALU.add).then_inc(s["att"], 1)
                    if behind:
                        products(p + 1)

                products(0)
                tiles(pool.Fori, tile)

            @block.vector
            def _(dve):
                dve.memset(score[:], -1e30).then_inc(s["mask"], 1)

                def normalise(p, first):
                    ln_dve_normalise(dve, ln, [g.X[:, b, p, :] for b in range(NB)], stats, mv, sd, rstd, xn, p, first)

                def x_lo(p, k):
                    dve.wait_ge(ln["hi"], NB * p + k + 1)
                    lo_part(dve, xt[:, 1, :, k * P:(k + 1) * P], tp[k % 2][:].rearrange("p (c t) -> p c t", c=KD),
                            xt[:, 0, :, k * P:(k + 1) * P]).then_inc(ln["lo"], 1)

                def dot(p, n):
                    i, j = pairs[n]
                    dve.wait_ge(s["prod"], NPAIR * p + n + 1)
                    dve.wait_ge(s["sub"], p)
                    dve.tensor_reduce(score[:, i, :, j], prod[:, n % 2].rearrange("p (h d) -> p h d", h=H0), AX_X,
                                      ALU.add).then_inc(s["dot"], 1)

                normalise(0, None)
                dve.wait_ge(s["w_hi"], 1)
                lo_part(dve, w[:, 1], wraw[:], w[:, 0]).then_inc(s["w_lo"], 1)
                for k in range(NB):
                    x_lo(0, k)
                normalise(1, NB)
                dve.wait_ge(s["mask"], 1)
                dve.wait_ge(s["w_lo"], 1)
                for n in range(NPAIR):
                    dot(0, n)
                flat = lambda t: t[:].rearrange("p i h j -> p (i h) j")
                each = lambda t: t[:].rearrange("p (n o) -> p n o", o=1).to_broadcast([P, NB * H0, NB])

                def tile(p, behind):
                    dve.wait_ge(s["dot"], NPAIR * (p + 1))
                    dve.tensor_reduce(mx[:], flat(score), AX_X, ALU.max).then_inc(s["mx"], 1)
                    dve.wait_ge(s["mx"], p + 1)
                    dve.tensor_tensor(flat(shifted), flat(score), each(mx), ALU.subtract).then_inc(s["sub"], 1)
                    if behind:
                        x_lo(p + 1, 0)
                    dve.wait_ge(s["ex"], p + 1)
                    dve.tensor_reduce(sm[:], flat(probs), AX_X, ALU.add).then_inc(s["sm"], 1)
                    dve.wait_ge(s["sm"], p + 1)
                    dve.reciprocal(rc[:], sm[:]).then_inc(s["rc"], 1)
                    if behind:
                        x_lo(p + 1, 1)
                    dve.wait_ge(s["rc"], p + 1)
                    dve.tensor_tensor(flat(probs), flat(probs), each(rc), ALU.mult).then_inc(s["probs"], 1)
                    if behind:
                        x_lo(p + 1, 2)
                    dve.wait_ge(s["probs"], p + 1)
                    for i, j in pairs:
                        if j == 0:
                            dve.wait_ge(s["att"], NB * p + max(0, i - 1))
                        pr = probs[:, i, :, j:j + 1].rearrange("p (g r) o -> p g r o", g=KV0).to_broadcast([P, KV0, R0, DH0])
                        dve.tensor_tensor(heads(pv[:, i % 2, j]), grouped(ring(qkv, p)[:, j, VO:]), pr, ALU.mult).then_inc(s["pv"], 1)
                        if behind and (i, j) == (1, 1):
                            x_lo(p + 1, 3)
                    if behind == 2:
                        normalise(p + 2, NB * (p + 2))
                    for i in range(NB):
                        dve.wait_ge(s["at_hi"], NB * p + i + 1)
                        lo_part(dve, at[:, 1, :, i * P:(i + 1) * P], tp[i % 2][:].rearrange("p (c t) -> p c t", c=KD),
                                at[:, 0, :, i * P:(i + 1) * P]).then_inc(s["at_lo"], 1)
                        if behind and i >= 1:
                            dot(p + 1, i - 1)
                    for i in range(NB):
                        if behind:
                            for n in (3 + 2 * i, 4 + 2 * i):
                                if n < NPAIR:
                                    dot(p + 1, n)
                        dve.wait_ge(s["o_ps"], NB * p + i + 1)
                        dve.tensor_tensor(g.X[:, i, p, :], g.X[:, i, p, :], op[i % 2][:], ALU.add).then_inc(s["x_add"], 1)

                tiles(dve.Fori, tile)

            @block.tensor
            def _(pe):
                def qkv_products(p):
                    for b in range(NB):
                        pe.wait_ge(ln["lo"], NB * p + b + 1)
                        pe.wait_ge(s["qkv_in"], NB * p + max(0, b - 1))
                        x = lambda k: [xt[:, h, k, b * P:(b + 1) * P] for h in range(2)]
                        for k in range(KD):
                            mm3(pe, qp[b % 2][:], x(k), wslice(k, 0, KO), k == 0, k == KD - 1)
                        for k in range(KD):
                            last = mm3(pe, kp[b % 2][:, 0:QKV0 - KO], x(k), wslice(k, KO, QKV0 - KO), k == 0, k == KD - 1)
                        last.then_inc(s["qkv_ps"], 1)

                ln_pe_transpose(pe, ln, xn, tp, g.ident, NB, 0)
                pe.wait_ge(s["w_lo"], 1)
                qkv_products(0)

                def tile(p, behind):
                    if behind:
                        pe.wait_ge(s["at_lo"], NB * p)
                        ln_pe_transpose(pe, ln, xn, tp, g.ident, NB, NB * (p + 1))
                        qkv_products(p + 1)
                        pe.wait_ge(ln["lo"], NB * (p + 2))
                    for i in range(NB):
                        pe.wait_ge(s["att"], NB * p + i + 1)
                        pe.wait_ge(s["at_lo"], NB * p + max(0, i - 1))
                        for c in range(KD):
                            last = pe.transpose(tp[i % 2][:, c * P:(c + 1) * P], att[:, i, c * P:(c + 1) * P], g.ident[:])
                        last.then_inc(s["at_ps"], 1)
                    for i in range(NB):
                        pe.wait_ge(s["at_lo"], NB * p + i + 1)
                        pe.wait_ge(s["x_add"], NB * p + max(0, i - 1))
                        for k in range(KD):
                            last = mm3(pe, op[i % 2][:], [at[:, h, k, i * P:(i + 1) * P] for h in range(2)], wo(k),
                                       k == 0, k == KD - 1)
                        last.then_inc(s["o_ps"], 1)

                tiles(pe.Fori, tile)


def stage_cross0(nc, g):
    with ExitStack() as ctx:
        sb, ps, sems = tensors(nc, ctx)
        ln = ln_semaphores(sems, "cross_ln")
        s = sems("cross", "a_hi a_lo o_ps x_add")
        stats, mv = sb("cross_stats", [P, NP, 6]), sb("cross_mv", [P, NP, 2])
        sd, rstd = sb("cross_sd", [P, NP]), sb("cross_rstd", [P, NP])
        xn = sb("cross_xn", [P, NP, D])
        xt = sb("cross_xt", [P, 2, 2, KD, NT], F32R)
        a = sb("cross_a", [P, 2, 2, NP, NT], F32R)
        tp = [ps(f"cross_tp{k}", [P, NT]) for k in range(2)]
        op = [ps(f"cross_o{k}", [P, NT]) for k in range(4)]
        with nc.Block() as block:
            @block.scalar
            def _(act):
                for b in range(NB):
                    if b < 2:
                        act.copy(a[:, b % 2, 0], g.A[:, b]).then_inc(s["a_hi"], 1)
                    ln_act_sqrt(act, ln, mv, sd, g.eps, NP, b)
                    if b >= 2:
                        act.wait_ge(s["o_ps"], NP * (b - 1))
                        act.copy(a[:, b % 2, 0], g.A[:, b]).then_inc(s["a_hi"], 1)
                    ln_act_hi(act, ln, xt[:, b % 2], tp, NP, NP * b)

            @block.vector
            def _(dve):
                def normalise(b):
                    ln_dve_normalise(dve, ln, [g.X[:, b, t, :] for t in range(NP)], stats, mv, sd, rstd, xn, b,
                                     NP * b if b else None)

                normalise(0)
                for b in range(NB):
                    dve.wait_ge(s["a_hi"], b + 1)
                    lo_part(dve, a[:, b % 2, 1], g.A[:, b], a[:, b % 2, 0]).then_inc(s["a_lo"], 1)
                    ln_dve_lo(dve, ln, xt[:, b % 2], tp, NP, NP * b)
                    if b < NB - 1:
                        normalise(b + 1)
                    for t in range(NP):
                        dve.wait_ge(s["o_ps"], NP * b + t + 1)
                        dve.tensor_tensor(g.X[:, b, t, :], g.X[:, b, t, :], op[t][:], ALU.add).then_inc(s["x_add"], 1)

            @block.tensor
            def _(pe):
                def products(b):
                    pe.wait_ge(s["a_lo"], b + 1)
                    for t in range(NP):
                        pe.wait_ge(ln["lo"], NP * b + t + 1)
                        if b:
                            pe.wait_ge(s["x_add"], NP * (b - 1) + t + 1)
                        for k in range(KD):
                            last = mm3(pe, op[t][:], [xt[:, b % 2, h, k, t * P:(t + 1) * P] for h in range(2)],
                                       [a[:, b % 2, h, k] for h in range(2)], k == 0, k == KD - 1)
                        last.then_inc(s["o_ps"], 1)

                for b in range(NB):
                    ln_pe_transpose(pe, ln, xn, tp, g.ident, NP, NP * b)
                    products(b)


def stage_ffn0(nc, g):
    with ExitStack() as ctx:
        sb, ps, sems = tensors(nc, ctx)
        ln = ln_semaphores(sems, "ffn0_ln")
        s = sems("ffn0", "wg_load wg_hi wg_lo wd_load wd_hi wd_lo gu_ps sg h a cm t1 t2 hs h_hi h_lo o_ps x_add")
        M = 4
        GU = 2 * KD * P
        graw, draw = sb("ffn0_graw", [P, GU]), sb("ffn0_draw", [P, D])
        w = sb("ffn0_w", [P, 2, M, PIECE], F32R)
        xt = sb("ffn0_xt", [P, 2, KD, NB * NT], F32R)
        stats, mv = sb("ffn0_stats", [P, NP, 6]), sb("ffn0_mv", [P, NP, 2])
        sd, rstd = sb("ffn0_sd", [P, NP]), sb("ffn0_rstd", [P, NP])
        sg = sb("ffn0_sg", [P, 2, NT])
        h = sb("ffn0_h", [P, 2, M, NT])
        a = sb("ffn0_abs", [P, M, NT])
        xn = a
        ge = sb("ffn0_ge", [P, 6, NT], BF16)
        rank = sb("ffn0_rank", [P, M, NT], BF16)
        hh = sb("ffn0_hh", [P, 2, M, NT], F32R)
        gp = [ps(f"ffn0_g{k}", [P, NT]) for k in range(2)]
        up = [ps(f"ffn0_u{k}", [P, NT]) for k in range(2)]
        op = [ps(f"ffn0_o{k}", [P, NT]) for k in range(NP)]

        def wgu(j, which, k):
            at = (which * KD + k) * P
            return [w[:, x, j, at:at + P] for x in range(2)]

        def columns(part):
            return slice(0, GU) if part == "gu" else slice(GU, PIECE)

        def chunks(loop, body):
            body(0, True, False)
            with loop(1, C0 - 1) as c:
                body(c, False, False)
            body(C0 - 1, False, True)

        with nc.Block() as block:
            @block.sync
            def _(sp):
                def load(c, j, part):
                    raw, ready, split = (graw, s["wg_load"], s["wg_lo"]) if part == "gu" else (draw, s["wd_load"], s["wd_lo"])
                    sp.wait_ge(split, M * c + j)
                    sp.dma_start(raw[:], g.dram["ffn0_w"][M * c + j, :, columns(part)]).then_inc(ready, 16)

                for j in range(M):
                    load(0, j, "gu")

                def chunk(c, first, last):
                    for j in range(M):
                        load(c, j, "down")
                    if not last:
                        for j in range(M):
                            load(c + 1, j, "gu")

                chunks(sp.Fori, chunk)

            @block.scalar
            def _(act):
                def split_gu(c, j):
                    act.wait_ge(s["wg_load"], 16 * (M * c + j + 1))
                    act.copy(w[:, 0, j, 0:GU], graw[:]).then_inc(s["wg_hi"], 1)

                with act.Fori(0, NB) as b:
                    ln_act_sqrt(act, ln, mv, sd, g.eps, NP, b)
                    ln_act_hi(act, ln, xt[:, :, :, bass.ds(b * NT, NT)], gp, NP, NP * b)
                    split_gu(0, b)

                def h_abs(u, par):
                    act.wait_ge(s["h"], M * u + M)
                    act.wait_ge(s["cm"], 3 * u)
                    act.activation(a[:], h[:, par], ACT.Abs).then_inc(s["a"], 1)

                def h_hi(u, par):
                    act.wait_ge(s["hs"], M * u + M)
                    act.wait_ge(s["o_ps"], NP * u)
                    act.copy(hh[:, 0], h[:, par]).then_inc(s["h_hi"], 1)

                def chunk(c, first, last):
                    for b in range(NB):
                        u = NB * c + b
                        if not (first and b == 0):
                            h_abs(u - 1, (b + 1) % 2)
                        for j in range(M):
                            if b == 2:
                                act.wait_ge(s["wd_load"], 16 * (M * c + j + 1))
                                act.wait_ge(s["o_ps"], NP * NB * c)
                                act.copy(w[:, 0, j, GU:], draw[:]).then_inc(s["wd_hi"], 1)
                            n = M * u + j
                            act.wait_ge(s["gu_ps"], n + 1)
                            if not (first and b == 0 and j < 2):
                                act.wait_ge(s["h"], n - 1)
                            act.activation(sg[:, j % 2], gp[j % 2][:], ACT.Silu).then_inc(s["sg"], 1)
                            if b == NB - 1 and not last:
                                split_gu(c + 1, j)
                        if not (first and b == 0):
                            h_hi(u - 1, (b + 1) % 2)

                chunks(act.Fori, chunk)
                h_abs(NB * C0 - 1, (NB - 1) % 2)
                h_hi(NB * C0 - 1, (NB - 1) % 2)

            @block.vector
            def _(dve):
                def split_gu(c, j):
                    dve.wait_ge(s["wg_hi"], M * c + j + 1)
                    lo_part(dve, w[:, 1, j, 0:GU], graw[:], w[:, 0, j, 0:GU]).then_inc(s["wg_lo"], 1)

                with dve.Fori(0, NB) as b:
                    ln_dve_normalise(dve, ln, [g.X[:, b, t, :] for t in range(NP)], stats, mv, sd, rstd, xn, b, NP * b)
                    ln_dve_lo(dve, ln, xt[:, :, :, bass.ds(b * NT, NT)], gp, NP, NP * b)
                    split_gu(0, b)

                def compare(u, par):
                    dve.wait_ge(s["a"], u + 1)
                    dve.wait_ge(s["t2"], M * u)
                    for i, at, n in ((0, 0, 3), (1, 3, 2), (2, 5, 1)):
                        one = a[:, i:i + 1].to_broadcast([P, n, NT])
                        dve.tensor_tensor(ge[:, at:at + n], one, a[:, i + 1:], ALU.is_ge).then_inc(s["cm"], 1)

                def rank_a(u, par):
                    dve.wait_ge(s["cm"], 3 * u + 3)
                    dve.wait_ge(s["hs"], M * u)
                    for j, (x, y) in enumerate(((0, 1), (3, 4), (1, 3), (4, 5))):
                        dve.tensor_tensor(rank[:, j], ge[:, x], ge[:, y], ALU.add).then_inc(s["t1"], 1)

                def rank_b(u, par):
                    dve.wait_ge(s["t1"], M * u + M)
                    dve.tensor_tensor(rank[:, 0], rank[:, 0], ge[:, 2], ALU.add).then_inc(s["t2"], 1)
                    dve.tensor_tensor(rank[:, 1], rank[:, 1], ge[:, 0], ALU.subtract).then_inc(s["t2"], 1)
                    dve.tensor_tensor(rank[:, 2], ge[:, 5], rank[:, 2], ALU.subtract).then_inc(s["t2"], 1)
                    dve.tensor_tensor(rank[:, 3], rank[:, 3], ge[:, 2], ALU.add).then_inc(s["t2"], 1)

                def select(u, par):
                    dve.wait_ge(s["t2"], M * u + M)
                    for j, (bound, op0) in enumerate(((2.0, ALU.is_ge), (1.0, ALU.is_ge), (0.0, ALU.is_ge), (1.0, ALU.is_le))):
                        dve.scalar_tensor_tensor(out=h[:, par, j], in0=rank[:, j], scalar=bound, in1=h[:, par, j],
                                                 op0=op0, op1=ALU.mult).then_inc(s["hs"], 1)

                def h_lo(u, par):
                    dve.wait_ge(s["h_hi"], u + 1)
                    dve.wait_ge(s["hs"], M * u + M)
                    lo_part(dve, hh[:, 1], h[:, par], hh[:, 0]).then_inc(s["h_lo"], 1)

                def add(b, u):
                    for t in range(NP):
                        dve.wait_ge(s["o_ps"], NP * u + t + 1)
                        dve.wait_ge(s["x_add"], NP * u)
                        dve.tensor_tensor(g.X[:, b, t], g.X[:, b, t], op[t][:], ALU.add).then_inc(s["x_add"], 1)

                def chunk(c, first, last):
                    for b in range(NB):
                        u = NB * c + b
                        for j, step in enumerate((compare, rank_a, rank_b, select)):
                            if b == 2:
                                dve.wait_ge(s["wd_hi"], M * c + j + 1)
                                lo_part(dve, w[:, 1, j, GU:], draw[:], w[:, 0, j, GU:]).then_inc(s["wd_lo"], 1)
                            if not (first and b == 0):
                                step(u - 1, (b + 1) % 2)
                            dve.wait_ge(s["sg"], M * u + j + 1)
                            if not (first and b < 2):
                                dve.wait_ge(s["h_lo"], u - 1)
                            dve.tensor_tensor(h[:, b % 2, j], sg[:, j % 2], up[j % 2][:], ALU.mult).then_inc(s["h"], 1)
                            if b == NB - 1 and not last:
                                split_gu(c + 1, j)
                        if not (first and b < 2):
                            add((b + 2) % NB, u - 2)
                        if not (first and b == 0):
                            h_lo(u - 1, (b + 1) % 2)

                chunks(dve.Fori, chunk)
                u = NB * C0 - 1
                for step in (compare, rank_a, rank_b, select):
                    step(u, u % 2)
                add(NB - 2, u - 1)
                h_lo(u, u % 2)
                add(NB - 1, u)

            @block.tensor
            def _(pe):
                with pe.Fori(0, NB) as b:
                    ln_pe_transpose(pe, ln, xn, gp, g.ident, NP, NP * b)
                pe.wait_ge(ln["lo"], NP * NB)

                def down(u):
                    pe.wait_ge(s["h_lo"], u + 1)
                    pe.wait_ge(s["x_add"], NP * u)
                    for t in range(NP):
                        for j in range(M):
                            last = mm3(pe, op[t][:], [hh[:, y, j, t * P:(t + 1) * P] for y in range(2)],
                                       [w[:, y, j, GU:] for y in range(2)], j == 0, j == M - 1)
                        last.then_inc(s["o_ps"], 1)

                def chunk(c, first, last):
                    for b in range(NB):
                        x = lambda k: [xt[:, y, k, b * NT:(b + 1) * NT] for y in range(2)]
                        for j in range(M):
                            n = M * (NB * c + b) + j
                            if b == 0:
                                pe.wait_ge(s["wg_lo"], M * c + j + 1)
                            if not (first and b == 0 and j < 2):
                                pe.wait_ge(s["sg"], n - 1)
                                pe.wait_ge(s["h"], n - 1)
                            for which, bank in enumerate((gp, up)):
                                for k in range(KD):
                                    done = mm3(pe, bank[j % 2][:], wgu(j, which, k), x(k), k == 0, k == KD - 1)
                            done.then_inc(s["gu_ps"], 1)
                        if b == 2:
                            pe.wait_ge(s["wd_lo"], M * c + M)
                        if not (first and b < 2):
                            down(NB * c + b - 2)

                chunks(pe.Fori, chunk)
                down(NB * C0 - 2)
                down(NB * C0 - 1)


def latent_down(nc, g, bp, s, ln, ln2):
    with ExitStack() as ctx:
        def sb(name, shape, dt=F32):
            return ctx.enter_context(nc.sbuf_tensor(name, shape, dt))

        def ps(name, shape, dt=F32):
            return ctx.enter_context(nc.psum_tensor(name, shape, dt))

        QK = QL + KVL + DR
        wraw = sb("down_wraw", [P, KD * QK])
        w = sb("down_w", [P, 2, KD * QK], F32R)
        stats, mv = sb("down_stats", [P, NP, 6]), sb("down_mv", [P, NP, 2])
        sd, rstd = sb("down_sd", [P, NP]), sb("down_rstd", [P, NP])
        stats2, mv2 = sb("down_stats2", [P, 2 * NP, 6]), sb("down_mv2", [P, 2 * NP, 2])
        sd2, rstd2 = sb("down_sd2", [P, 2 * NP]), sb("down_rstd2", [P, 2 * NP])
        xn = sb("down_xn", [P, NP, D])
        xt = sb("down_xt", [P, 2, KD, NT], F32R)
        down = sb("down_x", [P, NP, QK])
        kr = sb("down_kr", [P, NP, 2, DR])
        kr2 = sb("down_kr2", [P, NP, DR])
        tmp = sb("down_tmp", [P, 2, NT])
        table = sb("down_rope", [P, 2, NP, DR])
        gb = sb("down_gb", [P, 2 * KQ + 2])
        tp = [ps(f"down_tp{k}", [P, NT]) for k in range(2)]
        cp = [ps(f"down_c{k}", [P, NT]) for k in range(2)]
        kp = [ps(f"down_k{k}", [P, NT]) for k in range(2)]
        up = [ps(f"down_t{k}", [P, NT]) for k in range(2)]
        gain = [gb[:, k:k + 1] for k in range(KQ)] + [gb[:, 2 * KQ:2 * KQ + 1]]
        offset = [gb[:, KQ + k:KQ + k + 1] for k in range(KQ)] + [gb[:, 2 * KQ + 1:2 * KQ + 2]]
        NCH = KQ + 1

        def dst(c, bb):
            cols = slice(bb * NT, (bb + 1) * NT)
            return g.cq[:, :, c, cols] if c < KQ else g.ckv[:, :, cols]

        with nc.Block() as block:
            @block.sync
            def _(sp):
                sp.dma_start(wraw[:], g.dram["down1_w"]).then_inc(s["load"], 16)
                sp.dma_start(table[:], g.dram["rope_t"]).then_inc(s["load"], 16)
                sp.dma_start(gb[:], g.dram["ln_gb"]).then_inc(s["load"], 16)

            @block.scalar
            def _(act):
                act.wait_ge(s["load"], 48 * bp + 48)
                act.copy(w[:, 0], wraw[:]).then_inc(s["w_hi"], 1)
                for bb in range(2):
                    b = 2 * bp + bb
                    ln_act_sqrt(act, ln, mv, sd, g.eps, NP, b)
                    ln_act_hi(act, ln, xt, tp, NP, NP * b)
                    act.wait_ge(s["t_ps"], 5 * b)
                    for t in range(NP):
                        act.wait_ge(s["d_ps"], NP * b + t + 1)
                        act.copy(down[:, t, 0:QL], cp[t % 2][:, 0:QL])
                        act.copy(down[:, t, QL:], kp[t % 2][:, 0:QK - QL]).then_inc(s["d_in"], 1)
                    act.wait_ge(ln2["var"], b + 1)
                    act.activation(sd2[:], mv2[:, :, 1], ACT.Sqrt, bias=g.eps[:, 0:1]).then_inc(ln2["sd"], 1)
                    for c in range(NCH):
                        act.wait_ge(s["t_mul"], NCH * b + c + 1)
                        act.copy(dst(c, bb)[:, 0], tmp[:, c % 2]).then_inc(s["t_hi"], 1)
                    act.wait_ge(s["t_ps"], 5 * b + 5)
                    act.copy(g.kr[:, bb], up[NCH % 2][:]).then_inc(s["kr_hi"], 1)

            @block.vector
            def _(dve):
                dve.wait_ge(s["w_hi"], bp + 1)
                lo_part(dve, w[:, 1], wraw[:], w[:, 0]).then_inc(s["w_lo"], 1)
                for bb in range(2):
                    b = 2 * bp + bb
                    ln_dve_normalise(dve, ln, [g.X[:, b, t, :] for t in range(NP)], stats, mv, sd, rstd, xn, b, NP * b)
                    ln_dve_lo(dve, ln, xt, tp, NP, NP * b)
                    for t in range(NP):
                        dve.wait_ge(s["d_in"], NP * b + t + 1)
                        dve.bn_stats(stats2[:, 2 * t, :], down[:, t, 0:QL])
                        last = dve.bn_stats(stats2[:, 2 * t + 1, :], down[:, t, QL:QL + KVL])
                    last.then_inc(ln2["stats"], 1)
                    a = down[:, :, QL + KVL:]
                    half = DR // 2
                    dve.wait_ge(s["t_ps"], 5 * b)
                    dve.tensor_tensor(kr[:, :, 0], a, table[:, 0], ALU.mult).then_inc(s["kr"], 1)
                    dve.tensor_tensor(kr2[:, :, 0:half], a[:, :, half:], table[:, 1, :, 0:half], ALU.mult).then_inc(s["kr"], 1)
                    dve.tensor_tensor(kr2[:, :, half:], a[:, :, 0:half], table[:, 1, :, half:], ALU.mult).then_inc(s["kr"], 1)
                    dve.wait_ge(s["kr"], 5 * b + 3)
                    dve.tensor_tensor(kr[:, :, 0], kr[:, :, 0], kr2[:], ALU.add).then_inc(s["kr"], 1)
                    dve.wait_ge(s["kr"], 5 * b + 4)
                    dve.tensor_copy(kr[:, :, 1], kr[:, :, 0]).then_inc(s["kr"], 1)
                    dve.wait_ge(ln2["stats"], b + 1)
                    dve.sem_inc(ln2["passed"], 1)
                    for n in range(2 * NP):
                        last = dve.bn_aggr(mv2[:, n, :], stats2[:, n, :])
                    last.then_inc(ln2["var"], 1)
                    dve.wait_ge(ln2["sd"], b + 1)
                    dve.reciprocal(rstd2[:], sd2[:]).then_inc(ln2["rstd"], 1)
                    dve.wait_ge(ln2["rstd"], b + 1)
                    for n in range(2 * NP):
                        part = down[:, n // 2, 0:QL] if n % 2 == 0 else down[:, n // 2, QL:QL + KVL]
                        dve.tensor_scalar(part, part, mv2[:, n, 0:1], rstd2[:, n:n + 1], ALU.subtract,
                                          ALU.mult).then_inc(ln2["norm"], 1)
                    for c in range(NCH):
                        dve.wait_ge(s["t_ps"], 5 * b + c + 1)
                        if c >= 2:
                            dve.wait_ge(s["t_lo"], NCH * b + c - 1)
                        dve.tensor_scalar(tmp[:, c % 2], up[c % 2][:], gain[c], offset[c], ALU.mult, ALU.add).then_inc(s["t_mul"], 1)
                        dve.wait_ge(s["t_hi"], NCH * b + c + 1)
                        dve.wait_ge(s["t_mul"], NCH * b + c + 1)
                        lo_part(dve, dst(c, bb)[:, 1], tmp[:, c % 2], dst(c, bb)[:, 0]).then_inc(s["t_lo"], 1)
                    dve.wait_ge(s["kr_hi"], b + 1)
                    up_half = slice(DR, 2 * DR)
                    lo_part(dve, g.kr[up_half, bb], up[NCH % 2][up_half], g.kr[up_half, bb]).then_inc(s["kr_lo"], 1)

            @block.tensor
            def _(pe):
                pe.wait_ge(s["w_lo"], bp + 1)
                for bb in range(2):
                    b = 2 * bp + bb
                    ln_pe_transpose(pe, ln, xn, tp, g.ident, NP, NP * b)
                    for t in range(NP):
                        pe.wait_ge(ln["lo"], NP * b + t + 1)
                        pe.wait_ge(s["d_in"], NP * b + max(0, t - 1))
                        for bank, at, n in ((cp, 0, QL), (kp, QL, QK - QL)):
                            for k in range(KD):
                                last = mm3(pe, bank[t % 2][:, 0:n], [xt[:, h, k, t * P:(t + 1) * P] for h in range(2)],
                                           [w[:, h, k * QK + at:k * QK + at + n] for h in range(2)], k == 0, k == KD - 1)
                        last.then_inc(s["d_ps"], 1)
                    pe.wait_ge(ln2["norm"], 2 * NP * (b + 1))
                    pe.wait_ge(s["kr"], 5 * b + 5)
                    pe.wait_ge(s["kr_lo"], b)
                    for c in range(NCH + 1):
                        if c >= 2:
                            pe.wait_ge(s["t_mul"], NCH * b + c - 1)
                        for t in range(NP):
                            src = down[:, t, c * P:(c + 1) * P] if c < NCH else kr[:, t].rearrange("p a d -> p (a d)")
                            last = pe.transpose(up[c % 2][:, t * P:(t + 1) * P], src, g.ident[:])
                        last.then_inc(s["t_ps"], 1)


def latent_heads(nc, g, bp, s):
    with ExitStack() as ctx:
        def sb(name, shape, dt=F32):
            return ctx.enter_context(nc.sbuf_tensor(name, shape, dt))

        def ps(name, shape, dt=F32):
            return ctx.enter_context(nc.psum_tensor(name, shape, dt))

        U = 4
        w = sb("pair_w", [P, 2, WPAIR], F32R)
        raw = sb("pair_raw", [P, WQ1])
        bias_all = sb("pair_bias_all", [P, PAIRS, 8])
        rope = sb("pair_rope", [P, 2, NT])
        qn = sb("pair_qn", [P, 2, 2, NT], F32R)
        kn = sb("pair_kn", [P, 2, 2, NT], F32R)
        qr1 = sb("pair_qr1", [P, 2, NT], F32R)
        qr2 = sb("pair_qr2", [DR, 2, NT], F32R)
        rot = sb("pair_rot", [P, 2, NT])
        v = sb("pair_v", [P, 2, NP, 2 * DV], F32R)
        pr_ = sb("pair_probs", [P, NP, NT])
        pt = sb("pair_pt", [P, 2, NP, NT], F32R)
        ot = sb("pair_ot", [P, 2, 2, NT], F32R)
        nmax, psum_, prec = (sb(f"pair_{n}", [P, NP]) for n in ("nmax", "psum", "prec"))
        NQ = NS // 4
        rows = sb("scan_rows", [P, 2, NQ, NT])
        dt, du = sb("scan_dt", [P, 2, NT]), sb("scan_du", [P, 2, NT])
        da = sb("scan_da", [P, 2, NT])
        st = sb("scan_state", [P, 3, NT])
        y = sb("scan_y", [P, NT])
        a_all = sb("scan_a_all", [P, CT, NS])
        sc = [ps(f"pair_s{k}", [P, NT]) for k in range(2)]
        tb = [ps(f"pair_t{k}", [P, NT]) for k in range(2)]
        gb = [ps(f"pair_g{k}", [P, NT]) for k in range(2)]
        ob = [ps(f"pair_o{k}", [P, NT]) for k in range(2)]
        KVO, OO = WQ1, WQ1 + WKV1
        PIECES = ((0, WQ1), (KVO, WKV1), (OO, WO1))
        base = 3 * PAIRS * bp
        dtu = (s["dtu0"], s["dtu1"])

        FILLS = [("ra", 0, 0), ("rb", 0, 0), ("qn", 0, 0), ("kn", 0, 0), ("kn", 1, 0), ("qn", 1, 0), ("v", 0, 0), ("v", 0, 1),
                 ("ra", 2, 0), ("rb", 2, 0), ("qn", 2, 0), ("kn", 2, 0), ("kn", 3, 0), ("qn", 3, 0), ("v", 2, 0), ("v", 2, 1)]
        NF = len(FILLS)
        HI = [kind in ("v", "qn", "kn") for kind, _, _ in FILLS]
        NHI = sum(HI)

        def side(u, q):
            ahead, unit = (u + 2) // U, (u + 2) % U
            first = 4 * (unit // 2 * 2)
            if u % 2 == 0:
                return [(ahead, first + q)]
            return {1: [(ahead, first + 4)], 3: [(ahead, first + 5)]}.get(q, [])

        def behind(u):
            return [((u + 1) // U, 8 * ((u + 1) // 2 % 2) + k) for k in (6, 7)] if u % 2 else []

        def target(kind, u, x):
            if kind == "v":
                return v[:, :, 2 * x:2 * x + 2, :]
            return (qn if kind == "qn" else kn)[:, u % 2]

        def bank(f):
            return gb[f % 2][:].rearrange("p (t d) -> p t d", t=2) if FILLS[f][0] == "v" else gb[f % 2][:]

        def bias(r, c):
            return bias_all[:, r, c:c + 1]

        def bias_of(r, kind, u):
            return bias(r, {"qn": 0, "kn": 4}[kind] + u % 2)

        def pairs(loop, body):
            body(0, True, False)
            with loop(1, PAIRS - 1) as r:
                body(r, False, False)
            body(PAIRS - 1, False, True)

        with nc.Block() as block:
            @block.sync
            def _(sp):
                sp.dma_start(bias_all[:], g.dram["pair_b"].rearrange("r p c -> p r c")).then_inc(s["c_load"], 16)
                sp.dma_start(rope[:], g.dram["rope_f"]).then_inc(s["c_load"], 16)
                sp.dma_start(a_all[:], g.dram["scan_ad"][:, 0:CT * NS].rearrange("p (c n) -> p c n", c=CT)).then_inc(s["c_load"], 16)

                def piece(r, n):
                    sp.wait_ge(s["pw_lo"], base + 3 * r + n)
                    at, size = PIECES[n]
                    sp.dma_start(raw[:, 0:size], g.dram["pair_w"][r, :, at:at + size]).then_inc(s["pw_load"], 16)

                def load_rows(r, n):
                    src = g.bc_dram[bp * 2 + r // 4, bass.ds(n * NS + r % 4 * NQ, NQ), :].rearrange("(o n) t -> o n t", o=1)
                    sp.dma_start(rows[:, n], src.to_broadcast([P, NQ, NT])).then_inc(s["rows_c" if n else "rows_b"], 16)

                def load_chunk(r, ct):
                    b = bp * 2 + r // 4
                    sp.dma_start(dt[:, ct % 2], g.dt_dram[b, :, ct, :]).then_inc(dtu[ct % 2], 16)
                    sp.dma_start(du[:, ct % 2], g.du_dram[b, :, ct, :]).then_inc(dtu[ct % 2], 16)

                piece(0, 0)
                load_chunk(0, 0)
                load_rows(0, 0)
                load_rows(0, 1)
                piece(0, 1)
                piece(0, 2)

                def pair(r, first, last):
                    t = bp * PAIRS + r
                    for ct in range(CT):
                        if not (last and ct == CT - 1):
                            if not (first and ct == 0):
                                sp.wait_ge(s["da"], 16 * t + 4 * ct)
                                sp.wait_ge(s["dbu"], 16 * t + 4 * ct)
                            load_chunk(r + (ct + 1) // CT, (ct + 1) % CT)
                        if not last and ct:
                            piece(r + 1, ct - 1)
                        if not last and ct == CT - 1:
                            sp.wait_ge(s["dbu"], 16 * t + 16)
                            load_rows(r + 1, 0)
                            sp.wait_ge(s["z"], 16 * t + 16)
                            load_rows(r + 1, 1)
                        sp.wait_ge(s["y"], 16 * t + 4 * ct + 4)
                        sp.dma_start(g.y_dram[t, :, ct, :], y[:]).then_inc(s["y_st"], 16)

                pairs(sp.Fori, pair)
                sp.wait_ge(s["y_st"], 64 * PAIRS * (bp + 1))
                sp.sem_inc(s["sp_passed"], 1)

            @block.gpsimd
            def _(pool):
                def pair(r, first, last):
                    t = bp * PAIRS + r

                    def dbu(m):
                        ct, n = m // NQ, m % NQ
                        if m == 0:
                            pool.wait_ge(s["rows_b"], 16 * t + 16)
                        if n == 0:
                            pool.wait_ge(dtu[ct % 2], 64 * t + 32 * (ct // 2) + 32)
                        pool.wait_ge(s["z"], 16 * t + max(0, m - 2))
                        pool.wait_ge(s["y"], 16 * t + max(0, m - 2))
                        pool.tensor_tensor(st[:, m % 3], du[:, ct % 2], rows[:, 0, n], ALU.mult).then_inc(s["dbu"], 1)

                    dbu(0)
                    for m in range(16):
                        ct, n = m // NQ, m % NQ
                        if m < 15:
                            dbu(m + 1)
                        if m == 0:
                            pool.wait_ge(s["rows_c"], 16 * t + 16)
                        pool.wait_ge(s["scan"], 16 * t + m + 1)
                        if n == 0:
                            pool.wait_ge(s["y_st"], 64 * t + 16 * ct)
                            pool.tensor_tensor(y[:], st[:, m % 3], rows[:, 1, n], ALU.mult).then_inc(s["z"], 1)
                            pool.wait_ge(s["z"], 16 * t + m + 1)
                            pool.sem_inc(s["y"], 1)
                        else:
                            pool.tensor_tensor(st[:, m % 3], st[:, m % 3], rows[:, 1, n], ALU.mult).then_inc(s["z"], 1)
                            pool.wait_ge(s["z"], 16 * t + m + 1)
                            pool.tensor_tensor(y[:], y[:], st[:, m % 3], ALU.add).then_inc(s["y"], 1)

                pairs(pool.Fori, pair)

            @block.scalar
            def _(act):
                act.wait_ge(s["c_load"], 48 * (bp + 1))
                act.activation(a_all[:], a_all[:], ACT.Exp).then_inc(s["a_exp"], 1)

                def split(r, n):
                    at, size = PIECES[n]
                    act.wait_ge(s["pw_load"], 16 * (base + 3 * r + n + 1))
                    act.activation(w[:, 0, at:at + size], raw[:, 0:size], ACT.Copy,
                                   scale=SCALE1 if n == 0 else 1.0).then_inc(s["pw_hi"], 1)

                def rotary(t, u):
                    act.wait_ge(s["rot"], 3 * (2 * t + u // 2) + 3)
                    hd = u % 2
                    for half in range(2):
                        last = act.copy(qr1[half * DR:(half + 1) * DR, hd], rot[hd * DR:(hd + 1) * DR, 0])
                    last.then_inc(s["qr_hi"], 1)

                def fill(r, f):
                    t = bp * PAIRS + r
                    kind, u, x = FILLS[f]
                    if kind in ("ra", "rb"):
                        return
                    act.wait_ge(s["f_ps"], NF * t + f + 1)
                    if kind == "v":
                        last = act.copy(target(kind, u, x)[:, 0], bank(f))
                    else:
                        last = act.activation(target(kind, u, x)[:, 0], bank(f), ACT.Identity, bias=bias_of(r, kind, u))
                    last.then_inc(s["f_hi"], 1)
                    if kind == "qn":
                        rotary(t, u)

                def exp(n, q):
                    act.wait_ge(s["nmax"], n + 1)
                    act.activation(pr_[:, q], sc[q % 2][:], ACT.Exp, bias=nmax[:, q:q + 1],
                                   accum_out=psum_[:, q:q + 1]).then_inc(s["exp"], 1)

                def norm(n, q):
                    act.wait_ge(s["prec"], n + 1)
                    act.activation(pr_[:, q], pr_[:, q], ACT.Copy, scale=prec[:, q:q + 1]).then_inc(s["norm"], 1)

                split(0, 0)
                split(0, 1)
                act.wait_ge(s["consts"], 2 * bp + 2)
                for f in range(8):
                    fill(0, f)
                for q in range(NP):
                    exp(NP * U * PAIRS * bp + q, q)
                    if q:
                        norm(NP * U * PAIRS * bp + q - 1, q - 1)
                norm(NP * U * PAIRS * bp + NP - 1, NP - 1)

                def pair(r, first, last):
                    t = bp * PAIRS + r
                    for u in range(U):
                        ahead = not (last and u >= 2)
                        more = not (last and u == U - 1)
                        for q in range(NP):
                            m = NP * u + q
                            n = 16 * t + m
                            act.wait_ge(s["t_ps2"], n + 1)
                            act.copy(pt[:, 0, :, q * P:(q + 1) * P], tb[q % 2][:].rearrange("p (k q) -> p k q", k=NP)).then_inc(s["pt_hi"], 1)
                            act.wait_ge(dtu[u % 2], 64 * t + 32 * (u // 2) + 32)
                            act.wait_ge(s["scan"], 16 * t + max(0, m - 1))
                            act.activation(da[:, m % 2], dt[:, u % 2], ACT.Exp,
                                           scale=a_all[:, u, bass.ds(r % 4 * NQ + q, 1)]).then_inc(s["da"], 1)
                            if more:
                                if q:
                                    norm(n + NP - 1, q - 1)
                                exp(n + NP, q)
                            if ahead:
                                for k, f in side(u, q):
                                    fill(r + k, f)
                            if (u, q) == (1, 0):
                                act.wait_ge(s["w_ps"], NP * 2 * t)
                                split(r, 2)
                            if (u, q) == (2, 1) and not last:
                                split(r + 1, 1)
                        if more:
                            norm(n + NP, NP - 1)
                        if u == 1 and not last:
                            split(r + 1, 0)
                        act.wait_ge(s["o_ps"], U * t + u + 1)
                        act.sem_inc(s["act_passed"], 1)
                        act.activation(ot[:, u % 2, 0], ob[0][:], ACT.Identity, bias=bias(r, 6 + u % 2)).then_inc(s["ot_hi"], 1)
                        if not (last and u == U - 1):
                            for k, f in behind(u):
                                fill(r + k, f)

                pairs(act.Fori, pair)

            @block.vector
            def _(dve):
                dve.wait_ge(s["c_load"], 48 * (bp + 1))
                dve.wait_ge(s["a_exp"], bp + 1)
                dve.tensor_scalar(a_all[:], a_all[:], -1.0, None, ALU.mult).then_inc(s["consts"], 1)
                dve.tensor_scalar(bias_all[:, :, 0:4], bias_all[:, :, 0:4], SCALE1, None, ALU.mult).then_inc(s["consts"], 1)

                def split(r, n):
                    at, size = PIECES[n]
                    dve.wait_ge(s["pw_hi"], base + 3 * r + n + 1)
                    dve.scalar_tensor_tensor(out=w[:, 1, at:at + size], in0=raw[:, 0:size], scalar=SCALE1 if n == 0 else 1.0,
                                             in1=w[:, 0, at:at + size].bitcast(F32), op0=ALU.mult,
                                             op1=ALU.subtract).then_inc(s["pw_lo"], 1)

                def fill(r, f):
                    t = bp * PAIRS + r
                    kind, u, x = FILLS[f]
                    if kind in ("ra", "rb"):
                        k = int(kind == "rb")
                        pb = 2 * t + u // 2
                        dve.wait_ge(s["f_ps"], NF * t + f + 1)
                        if kind == "ra":
                            dve.wait_ge(s["qr_hi"], 2 * pb)
                            dve.wait_ge(s["qr_lo"], 2 * pb)
                        dve.scalar_tensor_tensor(out=rot[:, k], in0=gb[f % 2][:], scalar=bias(r, 2 + k),
                                                 in1=rope[:, k], op0=ALU.add, op1=ALU.mult).then_inc(s["rot"], 1)
                        if kind == "rb":
                            dve.wait_ge(s["rot"], 3 * pb + 2)
                            dve.tensor_tensor(rot[:, 0], rot[:, 0], rot[:, 1], ALU.add).then_inc(s["rot"], 1)
                        return
                    dve.wait_ge(s["f_hi"], NHI * t + sum(HI[:f]) + 1)
                    out, hi = target(kind, u, x)[:, 1], target(kind, u, x)[:, 0]
                    if kind == "v":
                        last = lo_part(dve, out, bank(f), hi)
                    else:
                        last = dve.scalar_tensor_tensor(out=out, in0=bank(f), scalar=bias_of(r, kind, u), in1=hi.bitcast(F32),
                                                        op0=ALU.add, op1=ALU.subtract)
                    last.then_inc(s["f_lo"], 1)
                    if kind == "qn":
                        hd = u % 2
                        lanes = slice(hd * DR, (hd + 1) * DR)
                        dve.wait_ge(s["rot"], 3 * (2 * t + u // 2) + 3)
                        dve.wait_ge(s["qr_hi"], U * t + u + 1)
                        lo_part(dve, qr2[:, hd], rot[lanes, 0], qr1[lanes, hd]).then_inc(s["qr_lo"], 1)

                def maximum(n, q):
                    dve.wait_ge(s["s_ps"], n + 1)
                    dve.tensor_reduce(nmax[:, q:q + 1], sc[q % 2][:], AX_X, ALU.max, negate=True).then_inc(s["nmax"], 1)

                def invert(n, q):
                    dve.wait_ge(s["exp"], n + 1)
                    dve.reciprocal(prec[:, q:q + 1], psum_[:, q:q + 1]).then_inc(s["prec"], 1)

                def add(b, t, bb, tok, out):
                    k = NP * (2 * t + bb) + tok
                    dve.wait_ge(s["w_ps"], k + 1)
                    dve.wait_ge(s["x_add"], NP * 2 * t)
                    dve.tensor_tensor(g.X[:, b, tok], g.X[:, b, tok], out[:], ALU.add).then_inc(s["x_add"], 1)

                split(0, 0)
                split(0, 1)
                dve.wait_ge(s["consts"], 2 * bp + 2)
                dve.sem_inc(s["dve_passed"], 1)
                for f in range(8):
                    fill(0, f)
                for q in range(NP):
                    maximum(NP * U * PAIRS * bp + q, q)
                    if q:
                        invert(NP * U * PAIRS * bp + q - 1, q - 1)
                invert(NP * U * PAIRS * bp + NP - 1, NP - 1)

                def pair(r, first, last):
                    t = bp * PAIRS + r
                    for u in range(U):
                        ahead = not (last and u >= 2)
                        more = not (last and u == U - 1)
                        for q in range(NP):
                            m = NP * u + q
                            n = 16 * t + m
                            dve.wait_ge(s["pt_hi"], n + 1)
                            lo_part(dve, pt[:, 1, :, q * P:(q + 1) * P], tb[q % 2][:].rearrange("p (k q) -> p k q", k=NP),
                                    pt[:, 0, :, q * P:(q + 1) * P]).then_inc(s["pt_lo"], 1)
                            if more:
                                maximum(n + NP, q)
                            dve.wait_ge(s["da"], n + 1)
                            dve.wait_ge(s["dbu"], n + 1)
                            dve.tensor_tensor_scan(st[:, m % 3], da[:, m % 2], st[:, m % 3], 0.0, ALU.mult, ALU.add).then_inc(s["scan"], 1)
                            if u == 2:
                                add(2 * bp, t, 0, q, ob[1])
                            if u == 0 and not first:
                                add(2 * bp + 1, t - 1, 1, q, ob[1])
                            if more:
                                invert(n + NP, q)
                            if ahead:
                                for k, f in side(u, q):
                                    fill(r + k, f)
                            if (u, q) == (1, 0):
                                split(r, 2)
                            if (u, q) == (2, 1) and not last:
                                split(r + 1, 1)
                        if u == 1 and not last:
                            split(r + 1, 0)
                        dve.wait_ge(s["ot_hi"], U * t + u + 1)
                        dve.scalar_tensor_tensor(out=ot[:, u % 2, 1], in0=ob[0][:], scalar=bias(r, 6 + u % 2),
                                                 in1=ot[:, u % 2, 0].bitcast(F32), op0=ALU.add, op1=ALU.subtract).then_inc(s["ot_lo"], 1)
                        if not (last and u == U - 1):
                            for k, f in behind(u):
                                fill(r + k, f)
                    if last:
                        for tok in range(NP):
                            add(2 * bp + 1, t, 1, tok, ob[(tok + 1) % 2])

                pairs(dve.Fori, pair)

            @block.tensor
            def _(pe):
                def fill(r, f, first=False):
                    t = bp * PAIRS + r
                    kind, u, x = FILLS[f]
                    bb = u // 2
                    if f < 2:
                        if not first:
                            pe.wait_ge(s["f_lo"], NHI * t - 1 + f)
                    elif FILLS[f - 2][0] in ("ra", "rb"):
                        pe.wait_ge(s["rot"], 3 * (2 * t + FILLS[f - 2][1] // 2) + (1 if FILLS[f - 2][0] == "ra" else 2))
                    else:
                        pe.wait_ge(s["f_lo"], NHI * t + sum(HI[:f - 2]) + 1)
                    if f in (0, 3):
                        pe.wait_ge(s["pw_lo"], base + 3 * r + (1 if f == 0 else 2))
                    out = gb[f % 2]
                    if kind == "v":
                        for half in range(2):
                            tok = bb * NT + (2 * x + half) * P
                            last = mm3(pe, out[:, half * 2 * DV:(half + 1) * 2 * DV], [g.ckv[:, h, tok:tok + P] for h in range(2)],
                                       [w[:, h, KVO + 2 * DN:KVO + 4 * DN] for h in range(2)])
                    elif kind == "kn":
                        at = KVO + (u % 2) * DN
                        last = mm3(pe, out[:], [w[:, h, at:at + DN] for h in range(2)],
                                   [g.ckv[:, h, bb * NT:(bb + 1) * NT] for h in range(2)])
                    else:
                        at = {"qn": u % 2, "ra": 2, "rb": 3}[kind] * P
                        for k in range(KQ):
                            last = mm3(pe, out[:], [w[:, h, k * 4 * P + at:k * 4 * P + at + P] for h in range(2)],
                                       [g.cq[:, h, k, bb * NT:(bb + 1) * NT] for h in range(2)], k == 0, k == KQ - 1)
                    last.then_inc(s["f_ps"], 1)

                def scores(t, u, q, first=False):
                    if q == 0:
                        f = max(FILLS.index((kind, u, 0)) for kind in ("qn", "kn"))
                        pe.wait_ge(s["f_lo"], NHI * t + sum(HI[:f]) + 1)
                        pe.wait_ge(s["qr_lo"], U * t + u + 1)
                    n = NP * (U * t + u) + q
                    if not (first and q < 2):
                        pe.wait_ge(s["exp"], n - 1)
                    cols = slice(q * P, (q + 1) * P)
                    bb, hd = u // 2, u % 2
                    mm3(pe, sc[q % 2][:], [qn[:, u % 2, h, cols] for h in range(2)], [kn[:, u % 2, h] for h in range(2)], True, False)
                    pe.matmul(sc[q % 2][:], qr1[:, hd, cols], g.kr[:, bb], start=False, stop=False)
                    pe.matmul(sc[q % 2][:], qr2[:, hd, cols], g.kr[0:DR, bb], start=False, stop=True).then_inc(s["s_ps"], 1)

                def project(t, bb, tok, out):
                    if tok == 0:
                        pe.wait_ge(s["ot_lo"], U * t + 2 * bb + 2)
                    cols = slice(tok * P, (tok + 1) * P)
                    for hd in range(2):
                        last = mm3(pe, out[:], [ot[:, hd, h, cols] for h in range(2)],
                                   [w[:, h, OO + hd * D:OO + (hd + 1) * D] for h in range(2)], hd == 0, hd == 1)
                    last.then_inc(s["w_ps"], 1)

                for f in range(8):
                    fill(0, f, True)
                for q in range(NP):
                    scores(bp * PAIRS, 0, q, True)

                def pair(r, first, last):
                    t = bp * PAIRS + r
                    for u in range(U):
                        for q in range(NP):
                            n = NP * (U * t + u) + q
                            pe.wait_ge(s["norm"], n + 1)
                            if not (first and u == 0 and q < 2):
                                pe.wait_ge(s["pt_lo"], n - 1)
                            for k in range(NP):
                                turned = pe.transpose(tb[q % 2][:, k * P:(k + 1) * P], pr_[:, q, k * P:(k + 1) * P], g.ident[:])
                            turned.then_inc(s["t_ps2"], 1)
                            if not (last and u == U - 1):
                                scores(t + (u + 1) // U, (u + 1) % U, q)
                            if u == 2:
                                if q == 0:
                                    pe.wait_ge(s["pw_lo"], base + 3 * r + 3)
                                pe.wait_ge(s["x_add"], NP * 2 * t + q)
                                project(t, 0, q, ob[1])
                            if u == 0 and not first:
                                pe.wait_ge(s["x_add"], NP * (2 * t - 1) + q)
                                project(t - 1, 1, q, ob[1])
                            if not (last and u >= 2):
                                for k, f in side(u, q):
                                    fill(r + k, f)
                        pe.wait_ge(s["pt_lo"], NP * (U * t + u) + NP)
                        pe.wait_ge(s["f_lo"], NHI * t + sum(HI[:8 * (u // 2) + 8]))
                        pe.wait_ge(s["ot_lo"], U * t + u)
                        pe.wait_ge(s["x_add"], NP * 2 * bp * PAIRS)
                        hd = u % 2
                        for k in range(NP):
                            done = mm3(pe, ob[0][:], [v[:, h, k, hd * DV:(hd + 1) * DV] for h in range(2)],
                                       [pt[:, h, k] for h in range(2)], k == 0, k == NP - 1)
                        done.then_inc(s["o_ps"], 1)
                        if not (last and u == U - 1):
                            for k, f in behind(u):
                                fill(r + k, f)
                    if last:
                        for tok in range(NP):
                            pe.wait_ge(s["x_add"], NP * (2 * t + 1) + max(0, tok - 1))
                            project(t, 1, tok, ob[(tok + 1) % 2])

                pairs(pe.Fori, pair)


def stage_latent1(nc, g):
    with ExitStack() as ctx:
        sb, ps, sems = tensors(nc, ctx)
        ln, ln2 = ln_semaphores(sems, "down_ln"), ln_semaphores(sems, "down_ln2")
        s1 = sems("down", "load w_hi w_lo d_ps d_in t_ps t_mul t_hi t_lo kr kr_hi kr_lo")
        s2 = sems("pair", "c_load a_exp consts pw_load pw_hi pw_lo rows_b rows_c dtu0 dtu1 dbu da scan z y y_st f_ps f_hi f_lo "
                          "rot qr_hi qr_lo s_ps nmax exp prec norm t_ps2 pt_hi pt_lo o_ps ot_hi ot_lo w_ps x_add sp_passed dve_passed act_passed")
        g.cq = sb("latent_cq", [P, 2, KQ, 2 * NT], F32R)
        g.ckv = sb("latent_ckv", [P, 2, 2 * NT], F32R)
        g.kr = sb("latent_kr", [P, 2, NT], F32R)
        with nc.Fori(0, NB // 2) as bp:
            latent_down(nc, g, bp, s1, ln, ln2)
            latent_heads(nc, g, bp, s2)


def stage_gate1(nc, g):
    with ExitStack() as ctx:
        sb, ps, sems = tensors(nc, ctx)
        ln = ln_semaphores(sems, "gate_ln")
        s = sems("gate", "load y_load silu y01 y23 y yd gated t_ps x_add")
        stats, mv = sb("gate_stats", [P, NP, 6]), sb("gate_mv", [P, NP, 2])
        sd, rstd = sb("gate_sd", [P, NP]), sb("gate_rstd", [P, NP])
        xn = sb("gate_xn", [P, NP, D])
        y = sb("gate_y", [P, 4, CT, NT])
        u = sb("gate_u", [P, CT, NT])
        skip = sb("gate_skip", [P, CT])
        tb = [ps(f"gate_t{k}", [P, NT]) for k in range(NP)]
        with nc.Block() as block:
            @block.sync
            def _(sp):
                sp.dma_start(skip[:], g.dram["scan_ad"][:, CT * NS:]).then_inc(s["load"], 16)
                with sp.Fori(0, NB) as b:
                    sp.wait_ge(s["t_ps"], NP * b)
                    for q in range(4):
                        sp.dma_start(y[:, q], g.y_dram[4 * b + q]).then_inc(s["y_load"], 16)
                    sp.dma_start(u[:], g.u_dram[b]).then_inc(s["y_load"], 16)

            @block.scalar
            def _(act):
                with act.Fori(0, NB) as b:
                    ln_act_sqrt(act, ln, mv, sd, g.eps, NP, b)
                    for ct in range(CT):
                        act.wait_ge(ln["norm"], CT * b + ct + 1)
                        act.activation(xn[:, ct], xn[:, ct], ACT.Silu).then_inc(s["silu"], 1)

            @block.gpsimd
            def _(pool):
                with pool.Fori(0, NB) as b:
                    pool.wait_ge(s["y_load"], 80 * b + 80)
                    pool.tensor_tensor(y[:, 2], y[:, 2], y[:, 3], ALU.add).then_inc(s["y23"], 1)

            @block.vector
            def _(dve):
                dve.wait_ge(s["load"], 16)
                with dve.Fori(0, NB) as b:
                    dve.wait_ge(s["gated"], CT * b)
                    ln_dve_normalise(dve, ln, [g.X[:, b, t, :] for t in range(NP)], stats, mv, sd, rstd, xn, b, None)
                    dve.wait_ge(s["y_load"], 80 * b + 80)
                    dve.tensor_tensor(y[:, 0], y[:, 0], y[:, 1], ALU.add).then_inc(s["y01"], 1)
                    dve.wait_ge(s["y01"], b + 1)
                    for ct in range(CT):
                        last = dve.scalar_tensor_tensor(out=y[:, 0, ct], in0=u[:, ct], scalar=skip[:, ct:ct + 1], in1=y[:, 0, ct],
                                                        op0=ALU.mult, op1=ALU.add)
                    last.then_inc(s["yd"], 1)
                    dve.wait_ge(s["yd"], b + 1)
                    dve.wait_ge(s["y23"], b + 1)
                    dve.tensor_tensor(y[:, 0], y[:, 0], y[:, 2], ALU.add).then_inc(s["y"], 1)
                    dve.wait_ge(s["y"], b + 1)
                    for ct in range(CT):
                        dve.wait_ge(s["silu"], CT * b + ct + 1)
                        dve.tensor_tensor(y[:, 0, ct], y[:, 0, ct], xn[:, ct], ALU.mult).then_inc(s["gated"], 1)
                    for t in range(NP):
                        dve.wait_ge(s["t_ps"], NP * b + t + 1)
                        dve.tensor_tensor(g.X[:, b, t, :], g.X[:, b, t, :], tb[t][:], ALU.add).then_inc(s["x_add"], 1)

            @block.tensor
            def _(pe):
                with pe.Fori(0, NB) as b:
                    pe.wait_ge(s["gated"], CT * b + CT)
                    pe.wait_ge(s["x_add"], NP * b)
                    for t in range(NP):
                        for ct in range(CT):
                            last = pe.transpose(tb[t][:, ct * P:(ct + 1) * P], y[:, 0, ct, t * P:(t + 1) * P], g.ident[:])
                        last.then_inc(s["t_ps"], 1)


def stage_ffn1(nc, g):
    with ExitStack() as ctx:
        sb, ps, sems = tensors(nc, ctx)
        ln = ln_semaphores(sems, "ffn1_ln")
        s = sems("ffn1", "w1_load w2_load w3_load w_sum ones tot mean mclip mrec mq w_a w_b w_q idb a_step xq t_ps t_in g_ps u_ps sg "
                         "h b_step hq1 hq ht_ps ht_in o_ps x_out out passed")
        w_load = (s["w1_load"], s["w2_load"], s["w3_load"])
        NW = KD * FF1
        NTILE = NB * NP
        stats, mv = sb("ffn1_stats", [P, NTILE, 6]), sb("ffn1_mv", [P, NTILE, 2])
        sd, rstd = sb("ffn1_sd", [P, NTILE]), sb("ffn1_rstd", [P, NTILE])
        wraw = sb("ffn1_wraw", [P, 2, NW])
        wq = sb("ffn1_wq", [P, 3, NW], BF16)
        wsum = sb("ffn1_wsum", [P, 3])
        ones = sb("ffn1_ones", [P, P])
        mean, mrec, m127 = (sb(f"ffn1_{n}", [P, 3]) for n in ("mean", "mrec", "m127"))
        idb = sb("ffn1_idb", [P, P], BF16)
        xn = sb("ffn1_xn", [P, D])
        xq = sb("ffn1_xq", [P, D], BF16)
        xt = sb("ffn1_xt", [P, KD, P], BF16)
        xm, xr, xs = (sb(f"ffn1_{n}", [P, NTILE]) for n in ("xm", "xr", "xs"))
        hm, hr, hs = (sb(f"ffn1_{n}", [P, 1]) for n in ("hm", "hr", "hs"))
        dq = sb("ffn1_dq", [P, NTILE, 2])
        dq3 = sb("ffn1_dq3", [P, NTILE])
        sg = sb("ffn1_sg", [P, FF1])
        h = sb("ffn1_h", [P, 2, FF1])
        hq = sb("ffn1_hq", [P, 2, FF1], BF16)
        ht = sb("ffn1_ht", [P, KF1, P], BF16)
        gp, up = ps("ffn1_g", [P, 3 * NT]), ps("ffn1_u", [P, 3 * NT])
        tp = ps("ffn1_t", [P, 2 * NT], BF16)
        op = ps("ffn1_o", [P, NT])
        X = g.X[:].rearrange("p b t f -> p (b t) f")
        out = g.out.rearrange("t b p f -> t (b p) f")
        LOOP = NTILE - 3
        NA, NBS = 5, 5
        sizes = [(0, NT), (NT, NT), (2 * NT, FF1 - 2 * NT)]

        def steps(loop, body):
            with loop(0, LOOP) as t:
                body(t, 3)
            for left in (2, 1, 0):
                body(NTILE - 1 - left, left)

        with nc.Block() as block:
            @block.sync
            def _(sp):
                for n, src in enumerate((g.dram["ffn1_w1"], g.dram["ffn1_w2"], g.dram["ffn1_w3"])):
                    if n == 2:
                        sp.wait_ge(s["w_a"], 1)
                    sp.dma_start(wraw[:, n % 2], src).then_inc(w_load[n], 16)

                def store(t, left):
                    sp.wait_ge(s["x_out"], t + 1)
                    sp.dma_start(out[:, t, :], X[:, t, :]).then_inc(s["out"], 16)

                steps(sp.Fori, store)
                sp.wait_ge(s["out"], 16 * NTILE)

            @block.scalar
            def _(act):
                act.copy(idb[:], g.ident[:]).then_inc(s["idb"], 1)
                act.wait_ge(ln["var"], 1)
                act.activation(sd[:], mv[:, :, 1], ACT.Sqrt, bias=g.eps[:, 0:1]).then_inc(ln["sd"], 1)

                def x_in(t):
                    act.wait_ge(s["t_ps"], t + 1)
                    act.copy(xt[:], tp[:, 0:D].rearrange("p (c t) -> p c t", c=KD)).then_inc(s["t_in"], 1)

                def silu(t):
                    act.wait_ge(s["g_ps"], t + 1)
                    act.wait_ge(s["h"], t)
                    act.activation(sg[:], gp[:, 0:FF1], ACT.Silu, scale=dq[:, t, 0:1]).then_inc(s["sg"], 1)

                def h_in(t):
                    for n, (a, k) in enumerate(((0, 8), (8, KF1 - 8))):
                        act.wait_ge(s["ht_ps"], 2 * t + n + 1)
                        act.copy(ht[:, a:a + k], tp[:, 0:k * P].rearrange("p (c t) -> p c t", c=k)).then_inc(s["ht_in"], 1)

                x_in(0)
                silu(0)
                x_in(1)

                def tile(t, left):
                    if left >= 1:
                        silu(t + 1)
                    if left >= 2:
                        x_in(t + 2)
                    h_in(t)

                steps(act.Fori, tile)

            @block.gpsimd
            def _(pool):
                def quantise(t, par):
                    pool.wait_ge(s["b_step"], NBS * t + NBS)
                    pool.sem_inc(s["passed"], 1)
                    pool.tensor_scalar(h[:, par], h[:, par], hs[:], MAGIC, ALU.mult, ALU.add).then_inc(s["hq1"], 1)
                    pool.wait_ge(s["hq1"], t + 1)
                    pool.wait_ge(s["ht_ps"], 2 * t)
                    pool.sem_inc(s["passed"], 1)
                    pool.tensor_scalar(hq[:, par], h[:, par], -MAGIC, 1.0, ALU.add, ALU.mult).then_inc(s["hq"], 1)

                quantise(0, 0)

                def tile(t, left):
                    if left >= 1:
                        quantise(t + 1, 0)

                steps(pool.Fori, tile)

            @block.vector
            def _(dve):
                for t in range(NTILE):
                    last = dve.bn_stats(stats[:, t, :], X[:, t, :])
                last.then_inc(ln["stats"], 1)
                dve.memset(ones[:], 1.0).then_inc(s["ones"], 1)
                dve.wait_ge(ln["stats"], 1)
                for t in range(NTILE):
                    last = dve.bn_aggr(mv[:, t, :], stats[:, t, :])
                last.then_inc(ln["var"], 1)
                dve.wait_ge(ln["sd"], 1)
                dve.reciprocal(rstd[:], sd[:]).then_inc(ln["rstd"], 1)

                for n in range(3):
                    dve.wait_ge(w_load[n], 16)
                    dve.tensor_reduce(wsum[:, n:n + 1], wraw[:, n % 2], AX_X, ALU.add, apply_absolute_value=True).then_inc(s["w_sum"], 1)
                    dve.wait_ge(s["tot"], n + 1)
                    col = slice(n, n + 1)
                    dve.tensor_scalar(mean[:, col], op[:, col], 1.0 / (D * FF1), 1e-5, ALU.mult, ALU.max).then_inc(s["mean"], 1)
                    dve.wait_ge(s["mean"], n + 1)
                    dve.reciprocal(mrec[:, col], mean[:, col]).then_inc(s["mrec"], 1)
                    dve.tensor_scalar(m127[:, col], mean[:, col], 1.0 / 127.0, None, ALU.mult).then_inc(s["mq"], 1)
                    dve.wait_ge(s["mrec"], n + 1)
                    r = wraw[:, n % 2]
                    dve.tensor_scalar(r, r, mrec[:, col], MAGIC, ALU.mult, ALU.add).then_inc(s["w_b"], 1)
                    dve.wait_ge(s["w_b"], 2 * n + 1)
                    dve.tensor_scalar(r, r, MAGIC, 1.0, ALU.subtract, ALU.min).then_inc(s["w_b"], 1)
                    dve.wait_ge(s["w_b"], 2 * n + 2)
                    dve.tensor_scalar(wq[:, n], r, -1.0, None, ALU.max).then_inc(s["w_a"], 1)
                dve.wait_ge(s["mq"], 3)
                dve.wait_ge(ln["rstd"], 1)

                def x_quant(t):
                    one = lambda a: a[:, bass.ds(t, 1)]
                    dve.wait_ge(s["xq"], t)
                    dve.tensor_scalar(xn[:], X[:, t, :], mv[:, t, 0:1], one(rstd), ALU.subtract, ALU.mult).then_inc(s["a_step"], 1)
                    dve.wait_ge(s["a_step"], NA * t + 1)
                    dve.tensor_reduce(one(xm), xn[:], AX_X, ALU.max, apply_absolute_value=True).then_inc(s["a_step"], 1)
                    dve.wait_ge(s["a_step"], NA * t + 2)
                    dve.tensor_scalar(one(xr), one(xm), 1e-5, 1.0 / 127.0, ALU.max, ALU.mult).then_inc(s["a_step"], 1)
                    dve.wait_ge(s["a_step"], NA * t + 3)
                    dve.reciprocal(one(xs), one(xr)).then_inc(s["a_step"], 1)
                    dve.tensor_scalar(dq[:, t, :], mean[:, 0:2], one(xr), None, ALU.mult)
                    dve.wait_ge(s["a_step"], NA * t + 4)
                    dve.tensor_scalar(xn[:], xn[:], one(xs), MAGIC, ALU.mult, ALU.add).then_inc(s["a_step"], 1)
                    dve.wait_ge(s["a_step"], NA * t + 5)
                    dve.wait_ge(s["t_ps"], t)
                    dve.tensor_scalar(xq[:], xn[:], MAGIC, 127.0, ALU.subtract, ALU.min).then_inc(s["xq"], 1)

                def hidden(t, par):
                    one = lambda a: a[:, bass.ds(t, 1)]
                    dve.wait_ge(s["sg"], t + 1)
                    dve.wait_ge(s["u_ps"], t + 1)
                    dve.wait_ge(s["hq"], t)
                    dve.scalar_tensor_tensor(out=h[:, par], in0=up[:, 0:FF1], scalar=dq[:, t, 1:2], in1=sg[:],
                                             op0=ALU.mult, op1=ALU.mult).then_inc(s["h"], 1)
                    dve.wait_ge(s["h"], t + 1)
                    dve.tensor_reduce(hm[:], h[:, par], AX_X, ALU.max, apply_absolute_value=True).then_inc(s["b_step"], 1)
                    dve.wait_ge(s["b_step"], NBS * t + 1)
                    dve.tensor_scalar(hr[:], hm[:], 1e-5, 1.0 / 127.0, ALU.max, ALU.mult).then_inc(s["b_step"], 1)
                    dve.wait_ge(s["b_step"], NBS * t + 2)
                    dve.reciprocal(hs[:], hr[:]).then_inc(s["b_step"], 1)
                    dve.tensor_tensor(one(dq3), hr[:], mean[:, 2:3], ALU.mult).then_inc(s["b_step"], 2)

                def result(t):
                    dve.wait_ge(s["o_ps"], t + 1)
                    dve.scalar_tensor_tensor(out=X[:, t, :], in0=op[:], scalar=dq3[:, bass.ds(t, 1)], in1=X[:, t, :],
                                             op0=ALU.mult, op1=ALU.add).then_inc(s["x_out"], 1)

                x_quant(0)
                x_quant(1)
                hidden(0, 0)
                x_quant(2)

                def tile(t, left):
                    if left >= 1:
                        hidden(t + 1, 0)
                    if left >= 3:
                        x_quant(t + 3)
                    result(t)

                steps(dve.Fori, tile)

            @block.tensor
            def _(pe):
                pe.wait_ge(s["ones"], 1)
                for n in range(3):
                    pe.wait_ge(s["w_sum"], n + 1)
                    pe.wait_ge(s["mean"], n)
                    pe.matmul(op[:, n:n + 1], ones[:], wsum[:, n:n + 1], start=True, stop=True).then_inc(s["tot"], 1)
                pe.wait_ge(s["idb"], 1)
                pe.wait_ge(s["w_a"], 3)

                def turn_x(t):
                    pe.wait_ge(s["xq"], t + 1)
                    for c in range(KD):
                        last = pe.transpose(tp[:, c * P:(c + 1) * P], xq[:, c * P:(c + 1) * P], idb[:])
                    last.then_inc(s["t_ps"], 1)

                def gate_up(t):
                    pe.wait_ge(s["t_in"], t + 1)
                    for n, (bank, free, done) in enumerate(((gp, s["sg"], s["g_ps"]), (up, s["h"], s["u_ps"]))):
                        pe.wait_ge(free, t)
                        for a, size in sizes:
                            for k in range(KD):
                                last = pe.matmul(bank[:, a:a + size], xt[:, k, :], wq[:, n, k * FF1 + a:k * FF1 + a + size],
                                                 start=k == 0, stop=k == KD - 1)
                        last.then_inc(done, 1)

                def turn_h(t, par):
                    pe.wait_ge(s["hq"], t + 1)
                    for n, (a, k) in enumerate(((0, 8), (8, KF1 - 8))):
                        if n:
                            pe.wait_ge(s["ht_in"], 2 * t + 1)
                        for c in range(k):
                            last = pe.transpose(tp[:, c * P:(c + 1) * P], hq[:, par, (a + c) * P:(a + c + 1) * P], idb[:])
                        last.then_inc(s["ht_ps"], 1)

                def down(t):
                    pe.wait_ge(s["ht_in"], 2 * t + 2)
                    pe.wait_ge(s["x_out"], t)
                    for c in range(KF1):
                        last = pe.matmul(op[:], ht[:, c, :], wq[:, 2, c * D:(c + 1) * D], start=c == 0, stop=c == KF1 - 1)
                    last.then_inc(s["o_ps"], 1)

                turn_x(0)
                gate_up(0)
                turn_x(1)

                def tile(t, left):
                    if left >= 1:
                        gate_up(t + 1)
                    if left >= 2:
                        pe.wait_ge(s["ht_in"], 2 * t)
                        turn_x(t + 2)
                        pe.wait_ge(s["t_in"], t + 3)
                    turn_h(t, 0)
                    down(t)

                steps(pe.Fori, tile)


def decoder(nc, a, stages):
    with ExitStack() as ctx:
        sb, ps, sems = tensors(nc, ctx)
        g = State()
        g.dram = a
        g.x_in = a["x"].rearrange("b (p t) f -> t b p f", t=P)
        g.out = a["out"].rearrange("b (p t) f -> t b p f", t=P)
        g.u_dram = nc.dram_tensor("u_dram", (NB, P, CT, NT), F32).ap()
        g.dt_dram = nc.dram_tensor("dt_dram", (NB, P, CT, NT), F32).ap()
        g.du_dram = nc.dram_tensor("du_dram", (NB, P, CT, NT), F32).ap()
        g.bc_dram = nc.dram_tensor("bc_dram", (NB, 2 * NS, NT), F32).ap()
        g.y_dram = nc.dram_tensor("y_dram", (16, P, CT, NT), F32).ap()
        g.X = sb("X", [P, NB, NP, D])
        g.ident = sb("ident", [P, P])
        g.one, g.eps = sb("one", [P, 1]), sb("eps", [P, 1])
        with ExitStack() as cross:
            g.A = cross.enter_context(nc.sbuf_tensor("attention", [P, NB, NP, NT], F32))
            for f in (stage_context, stage_attention0, stage_cross0)[:stages]:
                f(nc, g)
        for f in (stage_ffn0, stage_latent1, stage_gate1, stage_ffn1)[:max(0, stages - 3)]:
            f(nc, g)
        if stages < 7:
            done = sems("end", "out")["out"]
            with nc.Block() as block:
                @block.sync
                def _(sp):
                    sp.dma_start(g.out, g.X[:]).then_inc(done, 16)
                    sp.wait_ge(done, 16)


STAGES = 7


def layouts(v):
    import numpy as np
    c = np.ascontiguousarray

    def rows(w, n):
        return w.reshape(n, P, -1).transpose(1, 0, 2)

    a = {"x": v["x"], "ident_in": np.eye(P, dtype=np.float32)}
    a["ctx_in"] = v["ctx_1024"].transpose(2, 0, 1).reshape(KC, P, NB * NT).transpose(1, 0, 2)
    wq, wk, wi = v["L0_xattn_Wq"].T, v["L0_xattn_Wk"].T, v["L1_xattn_in_proj_w"].T
    xp = v["L1_xattn_x_proj_w"]
    xp = np.concatenate([xp[DTR:], xp[:DTR]], 0).T
    a["ctx_w"] = np.concatenate([rows(np.concatenate([wq, wk, wi], 1), KC).reshape(P, -1), rows(xp, CT).reshape(P, -1)], 1)
    a["dt_w"] = v["L1_xattn_dt_proj_w"].T
    a["ctx_small"] = np.concatenate([
        v["L0_xattn_bq"][:, None], v["L0_xattn_bk"][:, None],
        v["L1_xattn_conv_w"].reshape(CT, P, NCONV).transpose(1, 0, 2).reshape(P, -1),
        v["L1_xattn_conv_b"].reshape(CT, P).T, v["L1_xattn_dt_proj_b"].reshape(CT, P).T], 1)
    grp = v["L0_attn_weight_qkv"].reshape(KV0, (R0 + 2) * DH0, D)
    n = R0 * DH0
    qkv = np.concatenate([grp[:, :n].reshape(-1, D), grp[:, n:n + DH0].reshape(-1, D), grp[:, n + DH0:].reshape(-1, D)], 0)
    a["att0_w"] = np.concatenate([rows(qkv.T, KD).reshape(P, -1), rows(v["L0_attn_weight_proj"].T, KD).reshape(P, -1)], 1)
    wg, wu = (v[k].reshape(KD, P, C0, P, 4).transpose(2, 4, 1, 0, 3).reshape(C0 * 4, P, KD * P) for k in ("L0_ffn_w_gate", "L0_ffn_w_up"))
    wd = v["L0_ffn_w_down"].reshape(C0, P, 4, D).transpose(0, 2, 1, 3).reshape(C0 * 4, P, D)
    a["ffn0_w"] = np.concatenate([wg, wu, wd], 2)
    def halves(w, axis):
        return np.concatenate([w.take(range(0, DR, 2), axis), w.take(range(1, DR, 2), axis)], axis)
    kvd = v["L1_attn_Wkv_down"]
    a["down1_w"] = rows(np.concatenate([v["L1_attn_Wq_down"], kvd[:KVL], halves(kvd[KVL:], 0)], 0).T, KD).reshape(P, -1)
    wq = np.concatenate([v["L1_attn_Wq_up"], v["L1_attn_bq_up"][:, None]], 1).reshape(H1, DN + DR, QL + 1)
    rope = halves(wq[:, DN:], 1)
    swap = np.concatenate([rope[:, DR // 2:], rope[:, :DR // 2]], 1)
    pair = lambda t: t.reshape(PAIRS, -1, QL + 1)
    wq = np.concatenate([pair(wq[:, :DN]), pair(rope), pair(swap)], 1)
    bq, wq = wq[:, :, QL], wq[:, :, :QL]
    wkv = np.concatenate([v["L1_attn_Wkv_up"], v["L1_attn_bkv_up"][:, None]], 1).reshape(PAIRS, 2, 2, P, KVL + 1)
    wkv = wkv.transpose(0, 2, 1, 3, 4).reshape(PAIRS, 4 * P, KVL + 1)
    bkv, wkv = wkv[:, :, KVL], wkv[:, :, :KVL]
    wo = v["L1_attn_Wo"].T.reshape(PAIRS, 2, P, D)
    a["pair_w"] = np.concatenate([wq.transpose(0, 2, 1).reshape(PAIRS, KQ, P, 4 * P).transpose(0, 2, 1, 3).reshape(PAIRS, P, -1),
                                  wkv.transpose(0, 2, 1), wo.transpose(0, 2, 1, 3).reshape(PAIRS, P, -1)], 2)
    a["pair_b"] = np.concatenate([bq.reshape(PAIRS, 4, P), bkv.reshape(PAIRS, 4, P)], 1).transpose(0, 2, 1)
    a["ln_gb"] = np.stack([v[k].reshape(-1, P)[j] for k in ("L1_attn_q_ln_g", "L1_attn_q_ln_b") for j in range(KQ)]
                          + [v["L1_attn_kv_ln_g"], v["L1_attn_kv_ln_b"]], 1)
    freq = (1.0 / np.float32(10000.0) ** (np.arange(0, DR, 2, dtype=np.float32) / np.float32(DR))).astype(np.float32)
    ang = np.arange(NT, dtype=np.float32)[:, None] * freq
    cos, sin = np.cos(ang).astype(np.float32), np.sin(ang).astype(np.float32)
    cs = np.stack([np.concatenate([cos, cos], 1), np.concatenate([-sin, sin], 1)], 0)
    a["rope_t"] = cs.reshape(2, NP, P, DR).transpose(2, 0, 1, 3)
    a["rope_f"] = np.concatenate([cs, cs], 2).transpose(2, 0, 1)
    a["scan_ad"] = np.concatenate([v["L1_xattn_A_log"].reshape(CT, P, NS).transpose(1, 0, 2).reshape(P, -1),
                                   v["L1_xattn_D"].reshape(CT, P).T], 1)
    a["ffn1_w1"], a["ffn1_w2"] = (rows(v[k].T, KD).reshape(P, -1) for k in ("L1_ffn_w1", "L1_ffn_w2"))
    a["ffn1_w3"] = rows(v["L1_ffn_w3"].T, KF1).reshape(P, -1)
    return {k: c(t) for k, t in a.items()}


def kernel(**inputs):
    import numpy as np
    import concourse.bacc as bacc
    from concourse.bass_utils import run_bass_kernel_spmd

    nc = bacc.Bacc("TRN2", target_bir_lowering=False, num_devices=1)
    arrays = {f"in_{k}": t for k, t in layouts({k: np.asarray(t) for k, t in inputs.items()}).items()}
    drams = {k[3:]: nc.dram_tensor(k, t.shape, mybir.dt.from_np(t.dtype), kind="ExternalInput").ap() for k, t in arrays.items()}
    drams["out"] = nc.dram_tensor("out_dram", (NB, NT, D), F32, kind="ExternalOutput").ap()
    decoder(nc, drams, STAGES)
    r = run_bass_kernel_spmd(nc, [arrays], core_ids=[0])
    return r.results[0]["out_dram"]
```

```python
from contextlib import ExitStack

import concourse.bass as bass
from concourse import mybir

F32 = mybir.dt.float32
F32R = mybir.dt.float32r
BF16 = mybir.dt.bfloat16
ALU = mybir.AluOpType
ACT = mybir.ActivationFunctionType
AX_X = mybir.AxisListType.X

P = 128
NB = 4
NT = 512
NP = NT // P
D = 512
KD = D // P
EPS = 1e-5

H0, KV0, DH0 = 16, 4, 32
R0 = H0 // KV0
QKV0 = H0 * DH0 + 2 * KV0 * DH0
DC = 256
KC = DC // P
DI = 512
CT = DI // P
NS = 16
DTR = 16
NCONV = 4
SMALL = 2.0 ** -7
FF0 = 2048
C0 = FF0 // (4 * P)
PIECE = 2 * KD * P + D
H1, DN, DR, DV, QL, KVL = 16, 128, 64, 128, 384, 128
KQ = QL // P
PAIRS = H1 // 2
WQ1, WKV1, WO1 = KQ * 3 * P, 4 * P, 2 * D
WPAIR = WQ1 + WKV1 + WO1
W1_PIECES = ((0, WQ1), (WQ1, WKV1), (WQ1 + WKV1, WO1))
SCALE1 = float((DN + DR) ** -0.5)
FF1 = 1408
KF1 = FF1 // P
MAGIC = 12582912.0


class State:
    pass


def clear_semaphores(nc, handles):
    nc.clear_and_free_semaphores(handles)
    with nc.Block():
        pass


def tensors(nc, ctx):
    handles = []
    ctx.callback(clear_semaphores, nc, handles)

    def sb(name, shape, dt=F32):
        return ctx.enter_context(nc.sbuf_tensor(name, shape, dt))

    def ps(name, shape, dt=F32):
        return ctx.enter_context(nc.psum_tensor(name, shape, dt))

    def sems(prefix, names):
        made = {n: nc.alloc_semaphore(f"{prefix}_{n}") for n in names.split()}
        handles.extend(made.values())
        return made

    return sb, ps, sems


def mm3(pe, out, a, b, start=True, stop=True):
    pe.matmul(out, a[0], b[0], start=start, stop=False)
    pe.matmul(out, a[0], b[1], start=False, stop=False)
    return pe.matmul(out, a[1], b[0], start=False, stop=stop)


def lo_part(dve, out, full, hi):
    return dve.tensor_tensor(out, full, hi.bitcast(F32), ALU.subtract)


def ln_semaphores(sems, prefix):
    return sems(prefix, "stats passed var sd rstd norm xt hi lo")


def ln_dve_normalise(dve, s, tiles, stats, mv, sd, rstd, xn, count, first, width=D):
    n = len(tiles)
    for k, tile in enumerate(tiles):
        last = dve.bn_stats(stats[:, k, :], tile)
    last.then_inc(s["stats"], 1)
    dve.wait_ge(s["stats"], count + 1)
    dve.sem_inc(s["passed"], 1)
    for k in range(n):
        last = dve.bn_aggr(mv[:, k, :], stats[:, k, :])
    last.then_inc(s["var"], 1)
    dve.wait_ge(s["sd"], count + 1)
    dve.reciprocal(rstd[:, 0:n], sd[:, 0:n]).then_inc(s["rstd"], 1)
    dve.wait_ge(s["rstd"], count + 1)
    if first is not None:
        dve.wait_ge(s["xt"], first)
    for k, tile in enumerate(tiles):
        dve.tensor_scalar(xn[:, k, :], tile, mv[:, k, 0:1], rstd[:, k:k + 1], ALU.subtract,
                          ALU.mult).then_inc(s["norm"], 1)


def ln_act_sqrt(act, s, mv, sd, eps, n, count):
    act.wait_ge(s["var"], count + 1)
    act.activation(sd[:, 0:n], mv[:, 0:n, 1], ACT.Sqrt, bias=eps[:, 0:1]).then_inc(s["sd"], 1)


def stage_context(nc, g):
    with ExitStack() as ctx:
        sb, ps, sems = tensors(nc, ctx)
        s = sems("ctx", "load x_load w_hi w_lo c_load c_hi c_lo q_ps k_ps q_hi k_hi qk_lo x_ps x_in "
                        "e_ps e_max e_exp e_rec a_norm a_ps a_in t1 t2 t3 conv u u_hi u_lo xd_ps d_hi d_lo bc dt_ps "
                        "dt_abs dt_exp dt_ln dt_relu dt_sum ser dt du st_du st_u st_bc st_dt pad")
        craw = sb("ctx_raw", [P, KC, NT])
        c = sb("ctx_split", [P, 2, KC, NT], F32R)
        wraw = sb("ctx_wraw", [P, g.dram["ctx_w"].shape[1]])
        w = sb("ctx_w", [P, 2, g.dram["ctx_w"].shape[1]], F32R)
        dtw_raw = sb("ctx_dtw_raw", [48, DI])
        dtw = sb("ctx_dtw", [48, 2, DI], F32R)
        small = sb("ctx_small", [P, 2 + CT * NCONV + 2 * CT])
        qk = sb("ctx_qk", [P, 2, 2, NT], F32R)
        e = sb("ctx_exp", [P, NP, NT])
        nmax, esum, erec = sb("ctx_nmax", [P, NP]), sb("ctx_esum", [P, NP]), sb("ctx_erec", [P, NP])
        xin = sb("ctx_xin", [P, CT, NT + NCONV - 1])
        ta, tb = sb("ctx_ta", [P, CT, NT]), sb("ctx_tb", [P, CT, NT])
        series, logs = sb("ctx_series", [P, CT, NT]), sb("ctx_logs", [P, CT, NT])
        u = sb("ctx_u", [P, CT, NT])
        us = sb("ctx_us", [P, 2, CT, NT], F32R)
        dlow = sb("ctx_dlow", [48, 2, NT], F32R)
        bc = sb("ctx_bc", [32, NT])
        pa = [ps(f"ctx_p{k}", [P, NT]) for k in range(8)]

        CW = 2 * P + DI

        def wcol(k, a, n):
            return [w[:, h, k * CW + a:k * CW + a + n] for h in range(2)]

        def xproj(k):
            return [w[:, h, KC * CW + 48 * k:KC * CW + 48 * k + 48] for h in range(2)]

        conv_w = lambda ct, t: small[:, 2 + ct * NCONV + t:3 + ct * NCONV + t]
        conv_b = lambda ct: small[:, 2 + CT * NCONV + ct:3 + CT * NCONV + ct]
        dt_b = lambda ct: small[:, 2 + CT * (NCONV + 1) + ct:3 + CT * (NCONV + 1) + ct]

        def batches(loop, body):
            with loop(0, NB - 1) as b:
                body(b, False)
            body(NB - 1, True)

        with nc.Block() as block:
            @block.sync
            def _(sp):
                sp.dma_start(craw[:], g.dram["ctx_in"][:, :, 0:NT]).then_inc(s["c_load"], 16)
                sp.dma_start(wraw[:], g.dram["ctx_w"]).then_inc(s["load"], 16)
                sp.dma_start(dtw_raw[32:48, :], g.dram["dt_w"]).then_inc(s["load"], 16)
                sp.dma_start(small[:], g.dram["ctx_small"]).then_inc(s["load"], 16)
                sp.dma_start(g.ident[:], g.dram["ident_in"]).then_inc(s["load"], 16)
                sp.dma_start(g.X[:, 0:2], g.x_in[:, 0:2]).then_inc(s["x_load"], 16)
                sp.dma_start(g.X[:, 2:4], g.x_in[:, 2:4]).then_inc(s["x_load"], 16)

                def batch(b, last):
                    if not last:
                        sp.wait_ge(s["c_lo"], b + 1)
                        sp.dma_start(craw[:], g.dram["ctx_in"][:, :, bass.ds((b + 1) * NT, NT)]).then_inc(s["c_load"], 16)
                    sp.wait_ge(s["u"], CT * b + CT)
                    sp.dma_start(g.u_dram[b], u[:]).then_inc(s["st_u"], 16)
                    sp.wait_ge(s["bc"], b + 1)
                    sp.dma_start(g.bc_dram[b], bc[:]).then_inc(s["st_bc"], 16)
                    sp.wait_ge(s["dt"], b + 1)
                    sp.dma_start(g.dt_dram[b], tb[:]).then_inc(s["st_dt"], 16)
                    sp.wait_ge(s["du"], b + 1)
                    sp.dma_start(g.du_dram[b], series[:]).then_inc(s["st_du"], 16)

                batches(sp.Fori, batch)
                for stored in ("st_u", "st_bc", "st_dt", "st_du"):
                    sp.wait_ge(s[stored], 16 * NB)
                sp.wait_ge(s["load"], 64)
                sp.wait_ge(s["x_load"], 32)

            @block.scalar
            def _(act):
                act.wait_ge(s["load"], 64)
                act.copy(w[:, 0], wraw[:]).then_inc(s["w_hi"], 1)
                act.copy(dtw[32:48, 0], dtw_raw[32:48]).then_inc(s["w_hi"], 1)

                def c_hi(b):
                    act.wait_ge(s["c_load"], 16 * b + 16)
                    act.wait_ge(s["x_ps"], CT * b)
                    act.copy(c[:, 0], craw[:]).then_inc(s["c_hi"], 1)

                def qk_hi(b):
                    for n, (ready, done) in enumerate(((s["q_ps"], s["q_hi"]), (s["k_ps"], s["k_hi"]))):
                        act.wait_ge(ready, b + 1)
                        act.activation(qk[:, 0, n], pa[n][:], ACT.Identity, bias=small[:, n:n + 1]).then_inc(done, 1)

                def x_in(b):
                    act.wait_ge(s["conv"], CT * b)
                    for ct in range(CT):
                        act.wait_ge(s["x_ps"], CT * b + ct + 1)
                        act.copy(xin[:, ct, NCONV - 1:], pa[2 + ct][:]).then_inc(s["x_in"], 1)

                def scores_exp(b):
                    act.wait_ge(s["a_ps"], NP * b)
                    act.wait_ge(s["e_rec"], b)
                    for n in range(NP):
                        act.wait_ge(s["e_max"], NP * b + n + 1)
                        act.activation(e[:, n], pa[(6 + n) % 8][:], ACT.Exp, bias=nmax[:, n:n + 1],
                                       accum_out=esum[:, n:n + 1]).then_inc(s["e_exp"], 1)

                def batch(b, last):
                    act.wait_ge(s["st_u"], 16 * b)
                    act.wait_ge(s["u_lo"], CT * b)
                    act.wait_ge(s["du"], b)
                    for ct in range(CT):
                        act.wait_ge(s["conv"], CT * b + ct + 1)
                        act.activation(u[:, ct], logs[:, ct], ACT.Silu, bias=conv_b(ct)).then_inc(s["u"], 1)
                    for ct in range(CT):
                        act.wait_ge(s["u"], CT * b + ct + 1)
                        act.wait_ge(s["xd_ps"], b)
                        act.copy(us[:, 0, ct], u[:, ct]).then_inc(s["u_hi"], 1)
                    if not last:
                        c_hi(b + 1)
                    act.wait_ge(s["xd_ps"], b + 1)
                    act.wait_ge(s["dt_ps"], CT * b)
                    act.copy(dlow[32:48, 0], pa[2][32:48]).then_inc(s["d_hi"], 1)
                    act.wait_ge(s["st_bc"], 16 * b)
                    act.copy(bc[:], pa[2][0:32]).then_inc(s["bc"], 1)
                    for n in range(NP):
                        act.wait_ge(s["a_ps"], NP * b + n + 1)
                        act.copy(g.A[:, b, n], pa[n % 2][:]).then_inc(s["a_in"], 1)
                    for ct in range(CT):
                        act.wait_ge(s["dt_relu"], CT * b + ct + 1)
                        act.activation(ta[:, ct], pa[3 + ct][:], ACT.Abs, bias=dt_b(ct)).then_inc(s["dt_abs"], 1)
                    act.wait_ge(s["dt_abs"], CT * b + CT)
                    act.activation(ta[:], ta[:], ACT.Exp, scale=-1.0).then_inc(s["dt_exp"], 1)
                    if not last:
                        qk_hi(b + 1)
                        x_in(b + 1)
                        scores_exp(b + 1)
                    act.wait_ge(s["dt_exp"], b + 1)
                    act.activation(logs[:], ta[:], ACT.Ln, bias=g.one[:, 0:1]).then_inc(s["dt_ln"], 1)

                c_hi(0)
                qk_hi(0)
                act.wait_ge(s["pad"], 1)
                x_in(0)
                scores_exp(0)
                batches(act.Fori, batch)

            @block.gpsimd
            def _(pool):
                with pool.Fori(0, NB) as b:
                    pool.wait_ge(s["dt"], b + 1)
                    pool.tensor_tensor(series[:], u[:], tb[:], ALU.mult).then_inc(s["du"], 1)

            @block.vector
            def _(dve):
                dve.memset(g.one[:], 1.0)
                dve.memset(g.eps[:], EPS)
                dve.memset(xin[:, :, 0:NCONV - 1], 0.0).then_inc(s["pad"], 1)
                dve.wait_ge(s["w_hi"], 2)
                lo_part(dve, w[:, 1], wraw[:], w[:, 0]).then_inc(s["w_lo"], 1)
                lo_part(dve, dtw[32:48, 1], dtw_raw[32:48], dtw[32:48, 0]).then_inc(s["w_lo"], 1)

                def c_lo(b):
                    dve.wait_ge(s["c_hi"], b + 1)
                    lo_part(dve, c[:, 1], craw[:], c[:, 0]).then_inc(s["c_lo"], 1)

                def qk_lo(b):
                    for n, ready in enumerate((s["q_hi"], s["k_hi"])):
                        dve.wait_ge(ready, b + 1)
                        dve.scalar_tensor_tensor(out=qk[:, 1, n], in0=pa[n][:], scalar=small[:, n:n + 1],
                                                 in1=qk[:, 0, n].bitcast(F32), op0=ALU.add,
                                                 op1=ALU.subtract).then_inc(s["qk_lo"], 1)

                def maxima(b):
                    for n in range(NP):
                        dve.wait_ge(s["e_ps"], NP * b + n + 1)
                        dve.tensor_reduce(nmax[:, n:n + 1], pa[(6 + n) % 8][:], AX_X, ALU.max,
                                          negate=True).then_inc(s["e_max"], 1)

                def batch(b, last):
                    for t, dst in enumerate((ta, logs, ta, logs)):
                        for ct in range(CT):
                            if t == 0:
                                dve.wait_ge(s["x_in"], CT * b + ct + 1)
                                last_op = dve.tensor_scalar(dst[:, ct], xin[:, ct, 0:NT], conv_w(ct, 0), None, ALU.mult)
                            else:
                                dve.wait_ge(s[f"t{t}"], CT * b + ct + 1)
                                src = logs if t == 2 else ta
                                last_op = dve.scalar_tensor_tensor(out=dst[:, ct], in0=xin[:, ct, t:t + NT], scalar=conv_w(ct, t),
                                                                   in1=src[:, ct], op0=ALU.mult, op1=ALU.add)
                            last_op.then_inc(s["conv" if t == 3 else f"t{t + 1}"], 1)
                    dve.wait_ge(s["e_exp"], NP * b + NP)
                    dve.reciprocal(erec[:], esum[:]).then_inc(s["e_rec"], 1)
                    dve.wait_ge(s["e_rec"], b + 1)
                    for n in range(NP):
                        dve.tensor_scalar(e[:, n], e[:, n], erec[:, n:n + 1], None, ALU.mult).then_inc(s["a_norm"], 1)
                    for ct in range(CT):
                        dve.wait_ge(s["u_hi"], CT * b + ct + 1)
                        lo_part(dve, us[:, 1, ct], u[:, ct], us[:, 0, ct]).then_inc(s["u_lo"], 1)
                    if not last:
                        c_lo(b + 1)
                    dve.wait_ge(s["d_hi"], b + 1)
                    dve.wait_ge(s["bc"], b + 1)
                    lo_part(dve, dlow[32:48, 1], pa[2][32:48], dlow[32:48, 0]).then_inc(s["d_lo"], 1)
                    dve.wait_ge(s["st_dt"], 16 * b)
                    dve.wait_ge(s["du"], b)
                    for ct in range(CT):
                        dve.wait_ge(s["dt_ps"], CT * b + ct + 1)
                        dve.tensor_scalar(tb[:, ct], pa[3 + ct][:], dt_b(ct), 0.0, ALU.add, ALU.max).then_inc(s["dt_relu"], 1)
                    dve.wait_ge(s["dt_exp"], b + 1)
                    dve.wait_ge(s["st_du"], 16 * b)
                    dve.tensor_scalar(series[:], ta[:], -0.25, 1.0 / 3.0, ALU.mult, ALU.add).then_inc(s["ser"], 1)
                    if not last:
                        qk_lo(b + 1)
                    dve.wait_ge(s["ser"], 6 * b + 1)
                    dve.tensor_tensor(series[:], series[:], ta[:], ALU.mult).then_inc(s["ser"], 1)
                    if not last:
                        maxima(b + 1)
                    for n, term in ((2, -0.5), (3, 1.0)):
                        for ct in range(CT):
                            dve.wait_ge(s["ser"], 6 * b + n)
                            last_op = dve.scalar_tensor_tensor(out=series[:, ct], in0=series[:, ct], scalar=term, in1=ta[:, ct],
                                                               op0=ALU.add, op1=ALU.mult)
                        last_op.then_inc(s["ser"], 1)
                    dve.wait_ge(s["dt_ln"], b + 1)
                    dve.wait_ge(s["ser"], 6 * b + 4)
                    dve.tensor_tensor(series[:], series[:], logs[:], ALU.subtract).then_inc(s["ser"], 1)
                    dve.wait_ge(s["dt_relu"], CT * b + CT)
                    dve.tensor_tensor(tb[:], tb[:], logs[:], ALU.add).then_inc(s["dt_sum"], 1)
                    dve.wait_ge(s["ser"], 6 * b + 5)
                    for ct in range(CT):
                        last_op = dve.scalar_tensor_tensor(out=series[:, ct], in0=ta[:, ct], scalar=SMALL, in1=series[:, ct],
                                                           op0=ALU.is_lt, op1=ALU.mult)
                    last_op.then_inc(s["ser"], 1)
                    dve.wait_ge(s["ser"], 6 * b + 6)
                    dve.wait_ge(s["dt_sum"], b + 1)
                    dve.tensor_tensor(tb[:], tb[:], series[:], ALU.add).then_inc(s["dt"], 1)

                c_lo(0)
                qk_lo(0)
                maxima(0)
                batches(dve.Fori, batch)

            @block.tensor
            def _(pe):
                def front(b, first):
                    pe.wait_ge(s["c_lo"], b + 1)
                    if not first:
                        pe.wait_ge(s["a_in"], NP * b)
                    cs = lambda k: [c[:, h, k] for h in range(2)]
                    for n, done in enumerate((s["q_ps"], s["k_ps"])):
                        for k in range(KC):
                            last = mm3(pe, pa[n][:], wcol(k, n * P, P), cs(k), k == 0, k == KC - 1)
                        last.then_inc(done, 1)
                    for ct in range(CT):
                        if ct == 0 and not first:
                            pe.wait_ge(s["d_lo"], b)
                            pe.wait_ge(s["bc"], b)
                        if not first:
                            pe.wait_ge(s["dt_abs"], CT * (b - 1) + ct)
                        for k in range(KC):
                            last = mm3(pe, pa[2 + ct][:], wcol(k, (2 + ct) * P, P), cs(k), k == 0, k == KC - 1)
                        last.then_inc(s["x_ps"], 1)
                    pe.wait_ge(s["qk_lo"], 2 * b + 2)
                    if not first:
                        pe.wait_ge(s["dt_abs"], CT * b)
                    for n in range(NP):
                        q = [qk[:, h, 0, n * P:(n + 1) * P] for h in range(2)]
                        mm3(pe, pa[(6 + n) % 8][:], q, [qk[:, h, 1] for h in range(2)]).then_inc(s["e_ps"], 1)

                def batch(b, last):
                    pe.wait_ge(s["a_norm"], NP * b + NP)
                    pe.wait_ge(s["e_exp"], NP * b + NP)
                    for n in range(2):
                        for m in range(NP):
                            turned = pe.transpose(pa[n % 2][:, m * P:(m + 1) * P], e[:, m, n * P:(n + 1) * P], g.ident[:])
                        turned.then_inc(s["a_ps"], 1)
                    pe.wait_ge(s["x_in"], CT * b + CT)
                    for ct in range(CT):
                        pe.wait_ge(s["u_lo"], CT * b + ct + 1)
                        done = mm3(pe, pa[2][0:48], xproj(ct), [us[:, h, ct] for h in range(2)], ct == 0, ct == CT - 1)
                    done.then_inc(s["xd_ps"], 1)
                    for n in range(2, NP):
                        pe.wait_ge(s["a_in"], NP * b + n - 1)
                        for m in range(NP):
                            turned = pe.transpose(pa[n % 2][:, m * P:(m + 1) * P], e[:, m, n * P:(n + 1) * P], g.ident[:])
                        turned.then_inc(s["a_ps"], 1)
                    pe.wait_ge(s["d_lo"], b + 1)
                    for ct in range(CT):
                        mm3(pe, pa[3 + ct][:], [dtw[32:48, h, ct * P:(ct + 1) * P] for h in range(2)],
                            [dlow[32:48, h] for h in range(2)]).then_inc(s["dt_ps"], 1)
                    if not last:
                        front(b + 1, False)

                pe.wait_ge(s["w_lo"], 2)
                front(0, True)
                batches(pe.Fori, batch)


def ln_pe_transpose(pe, s, xn, banks, ident, n, base):
    for k in range(n):
        pe.wait_ge(s["norm"], base + k + 1)
        pe.wait_ge(s["lo"], base + max(0, k - 1))
        for c in range(KD):
            last = pe.transpose(banks[k % 2][:, c * P:(c + 1) * P], xn[:, k, c * P:(c + 1) * P], ident[:])
        last.then_inc(s["xt"], 1)


def ln_act_hi(act, s, xt, banks, n, base):
    for k in range(n):
        act.wait_ge(s["xt"], base + k + 1)
        act.copy(xt[:, 0, :, k * P:(k + 1) * P], banks[k % 2][:].rearrange("p (c t) -> p c t", c=KD)).then_inc(s["hi"], 1)


def ln_dve_lo(dve, s, xt, banks, n, base):
    for k in range(n):
        dve.wait_ge(s["hi"], base + k + 1)
        lo_part(dve, xt[:, 1, :, k * P:(k + 1) * P], banks[k % 2][:].rearrange("p (c t) -> p c t", c=KD),
                xt[:, 0, :, k * P:(k + 1) * P]).then_inc(s["lo"], 1)


def stage_attention0(nc, g):
    with ExitStack() as ctx:
        sb, ps, sems = tensors(nc, ctx)
        ln = ln_semaphores(sems, "att0_ln")
        s = sems("att0", "load w_hi w_lo qkv_ps qkv_in prod dot mx sub ex sm rc probs pv sum1 att at_ps at_hi at_lo o_ps x_add mask passed")
        NW = KD * QKV0
        wraw = sb("att0_wraw", [P, KD * (QKV0 + D)])
        w = sb("att0_w", [P, 2, KD * (QKV0 + D)], F32R)
        stats, mv = sb("att0_stats", [P, NB, 6]), sb("att0_mv", [P, NB, 2])
        sd, rstd = sb("att0_sd", [P, NB]), sb("att0_rstd", [P, NB])
        xn = sb("att0_xn", [P, NB, D])
        xt = sb("att0_xt", [P, 2, KD, NB * P], F32R)
        qkv = sb("att0_qkv", [P, 2, NB, QKV0])
        att = sb("att0_att", [P, NB, D])
        at = sb("att0_at", [P, 2, KD, NB * P], F32R)
        prod = sb("att0_prod", [P, 2, D])
        score = sb("att0_score", [P, NB, H0, NB])
        shifted, probs = sb("att0_shifted", [P, NB, H0, NB]), sb("att0_probs", [P, NB, H0, NB])
        mx, sm, rc = (sb(f"att0_{n}", [P, NB * H0]) for n in ("mx", "sm", "rc"))
        pv = wraw[:, 0:2 * NB * D].rearrange("p (i j f) -> p i j f", i=2, j=NB)
        tp = [ps(f"att0_tp{k}", [P, NT]) for k in range(2)]
        qp = [ps(f"att0_q{k}", [P, NT]) for k in range(2)]
        kp = [ps(f"att0_k{k}", [P, NT]) for k in range(2)]
        op = [ps(f"att0_o{k}", [P, NT]) for k in range(2)]
        pairs = [(i, j) for i in range(NB) for j in range(i + 1)]
        NPAIR = len(pairs)
        KO, VO = H0 * DH0, H0 * DH0 + KV0 * DH0

        def wslice(k, a, n):
            return [w[:, h, k * QKV0 + a:k * QKV0 + a + n] for h in range(2)]

        def wo(k):
            return [w[:, h, NW + k * D:NW + (k + 1) * D] for h in range(2)]

        def heads(t):
            return t.rearrange("p (g r d) -> p g r d", g=KV0, r=R0)

        def grouped(t):
            return t.rearrange("p (g r d) -> p g r d", g=KV0, r=1).to_broadcast([P, KV0, R0, DH0])

        def tiles(loop, body):
            with loop(0, NP - 2) as p:
                body(p, 2)
            body(NP - 2, 1)
            body(NP - 1, 0)

        def ring(t, p):
            return t[:, p % 2]

        with nc.Block() as block:
            @block.sync
            def _(sp):
                sp.dma_start(wraw[:], g.dram["att0_w"]).then_inc(s["load"], 16)

            @block.scalar
            def _(act):
                act.wait_ge(s["load"], 16)
                act.copy(w[:, 0], wraw[:]).then_inc(s["w_hi"], 1)

                def qkv_in(p, b):
                    act.wait_ge(s["qkv_ps"], NB * p + b + 1)
                    act.copy(ring(qkv, p)[:, b, 0:KO], qp[b % 2][:])
                    act.copy(ring(qkv, p)[:, b, KO:], kp[b % 2][:, 0:QKV0 - KO]).then_inc(s["qkv_in"], 1)

                ln_act_sqrt(act, ln, mv, sd, g.eps, NB, 0)
                ln_act_hi(act, ln, xt, tp, NB, 0)
                ln_act_sqrt(act, ln, mv, sd, g.eps, NB, 1)
                for b in range(NB):
                    qkv_in(0, b)

                def tile(p, behind):
                    act.wait_ge(s["sub"], p + 1)
                    act.wait_ge(s["pv"], NPAIR * p)
                    act.activation(probs[:], shifted[:], ACT.Exp, scale=float(DH0 ** -0.5)).then_inc(s["ex"], 1)
                    if behind:
                        ln_act_hi(act, ln, xt, tp, NB, NB * (p + 1))
                        for b in range(NB):
                            qkv_in(p + 1, b)
                            if behind == 2 and b == 1:
                                ln_act_sqrt(act, ln, mv, sd, g.eps, NB, p + 2)
                    for i in range(NB):
                        act.wait_ge(s["at_ps"], NB * p + i + 1)
                        act.copy(at[:, 0, :, i * P:(i + 1) * P],
                                 tp[i % 2][:].rearrange("p (c t) -> p c t", c=KD)).then_inc(s["at_hi"], 1)

                tiles(act.Fori, tile)

            @block.gpsimd
            def _(pool):
                def products(p):
                    for n, (i, j) in enumerate(pairs):
                        pool.wait_ge(s["qkv_in"], NB * p + i + 1)
                        pool.wait_ge(s["dot"], NPAIR * p + max(0, n - 1))
                        pool.sem_inc(s["passed"], 1)
                        t = ring(qkv, p)
                        pool.tensor_tensor(heads(prod[:, n % 2]), heads(t[:, i, 0:KO]), grouped(t[:, j, KO:VO]),
                                           ALU.mult).then_inc(s["prod"], 1)

                def tile(p, behind):
                    for i in range(NB):
                        pool.wait_ge(s["pv"], NPAIR * p + (i + 1) * (i + 2) // 2)
                        pool.wait_ge(s["at_ps"], NB * p)
                        v = pv[:, i % 2]
                        if i == 0:
                            pool.sem_inc(s["passed"], 1)
                            pool.tensor_copy(att[:, 0], v[:, 0]).then_inc(s["att"], 1)
                        elif i == 1:
                            pool.tensor_tensor(att[:, 1], v[:, 0], v[:, 1], ALU.add).then_inc(s["att"], 1)
                        elif i == 2:
                            pool.tensor_tensor(v[:, 0], v[:, 0], v[:, 1], ALU.add).then_inc(s["sum1"], 1)
                            pool.wait_ge(s["sum1"], 3 * p + 1)
                            pool.tensor_tensor(att[:, 2], v[:, 0], v[:, 2], ALU.add).then_inc(s["att"], 1)
                        else:
                            pool.tensor_tensor(v[:, 0], v[:, 0], v[:, 1], ALU.add).then_inc(s["sum1"], 1)
                            pool.tensor_tensor(v[:, 2], v[:, 2], v[:, 3], ALU.add).then_inc(s["sum1"], 1)
                            pool.wait_ge(s["sum1"], 3 * p + 3)
                            pool.tensor_tensor(att[:, 3], v[:, 0], v[:, 2], ALU.add).then_inc(s["att"], 1)
                    if behind:
                        products(p + 1)

                products(0)
                tiles(pool.Fori, tile)

            @block.vector
            def _(dve):
                dve.memset(score[:], -1e30).then_inc(s["mask"], 1)

                def normalise(p, first):
                    ln_dve_normalise(dve, ln, [g.X[:, b, p, :] for b in range(NB)], stats, mv, sd, rstd, xn, p, first)

                def x_lo(p, k):
                    dve.wait_ge(ln["hi"], NB * p + k + 1)
                    lo_part(dve, xt[:, 1, :, k * P:(k + 1) * P], tp[k % 2][:].rearrange("p (c t) -> p c t", c=KD),
                            xt[:, 0, :, k * P:(k + 1) * P]).then_inc(ln["lo"], 1)

                def dot(p, n):
                    i, j = pairs[n]
                    dve.wait_ge(s["prod"], NPAIR * p + n + 1)
                    dve.wait_ge(s["sub"], p)
                    dve.tensor_reduce(score[:, i, :, j], prod[:, n % 2].rearrange("p (h d) -> p h d", h=H0), AX_X,
                                      ALU.add).then_inc(s["dot"], 1)

                normalise(0, None)
                dve.wait_ge(s["w_hi"], 1)
                lo_part(dve, w[:, 1], wraw[:], w[:, 0]).then_inc(s["w_lo"], 1)
                for k in range(NB):
                    x_lo(0, k)
                normalise(1, NB)
                dve.wait_ge(s["mask"], 1)
                dve.wait_ge(s["w_lo"], 1)
                for n in range(NPAIR):
                    dot(0, n)
                flat = lambda t: t[:].rearrange("p i h j -> p (i h) j")
                each = lambda t: t[:].rearrange("p (n o) -> p n o", o=1).to_broadcast([P, NB * H0, NB])

                def tile(p, behind):
                    dve.wait_ge(s["dot"], NPAIR * (p + 1))
                    dve.tensor_reduce(mx[:], flat(score), AX_X, ALU.max).then_inc(s["mx"], 1)
                    dve.wait_ge(s["mx"], p + 1)
                    dve.tensor_tensor(flat(shifted), flat(score), each(mx), ALU.subtract).then_inc(s["sub"], 1)
                    if behind:
                        x_lo(p + 1, 0)
                    dve.wait_ge(s["ex"], p + 1)
                    dve.tensor_reduce(sm[:], flat(probs), AX_X, ALU.add).then_inc(s["sm"], 1)
                    dve.wait_ge(s["sm"], p + 1)
                    dve.reciprocal(rc[:], sm[:]).then_inc(s["rc"], 1)
                    if behind:
                        x_lo(p + 1, 1)
                    dve.wait_ge(s["rc"], p + 1)
                    dve.tensor_tensor(flat(probs), flat(probs), each(rc), ALU.mult).then_inc(s["probs"], 1)
                    if behind:
                        x_lo(p + 1, 2)
                    dve.wait_ge(s["probs"], p + 1)
                    for i, j in pairs:
                        if j == 0:
                            dve.wait_ge(s["att"], NB * p + max(0, i - 1))
                        pr = probs[:, i, :, j:j + 1].rearrange("p (g r) o -> p g r o", g=KV0).to_broadcast([P, KV0, R0, DH0])
                        dve.tensor_tensor(heads(pv[:, i % 2, j]), grouped(ring(qkv, p)[:, j, VO:]), pr, ALU.mult).then_inc(s["pv"], 1)
                        if behind and (i, j) == (1, 1):
                            x_lo(p + 1, 3)
                    if behind == 2:
                        normalise(p + 2, NB * (p + 2))
                    for i in range(NB):
                        dve.wait_ge(s["at_hi"], NB * p + i + 1)
                        lo_part(dve, at[:, 1, :, i * P:(i + 1) * P], tp[i % 2][:].rearrange("p (c t) -> p c t", c=KD),
                                at[:, 0, :, i * P:(i + 1) * P]).then_inc(s["at_lo"], 1)
                        if behind and i >= 1:
                            dot(p + 1, i - 1)
                    for i in range(NB):
                        if behind:
                            for n in (3 + 2 * i, 4 + 2 * i):
                                if n < NPAIR:
                                    dot(p + 1, n)
                        dve.wait_ge(s["o_ps"], NB * p + i + 1)
                        dve.tensor_tensor(g.X[:, i, p, :], g.X[:, i, p, :], op[i % 2][:], ALU.add).then_inc(s["x_add"], 1)

                tiles(dve.Fori, tile)

            @block.tensor
            def _(pe):
                def qkv_products(p):
                    for b in range(NB):
                        pe.wait_ge(ln["lo"], NB * p + b + 1)
                        pe.wait_ge(s["qkv_in"], NB * p + max(0, b - 1))
                        x = lambda k: [xt[:, h, k, b * P:(b + 1) * P] for h in range(2)]
                        for k in range(KD):
                            mm3(pe, qp[b % 2][:], x(k), wslice(k, 0, KO), k == 0, k == KD - 1)
                        for k in range(KD):
                            last = mm3(pe, kp[b % 2][:, 0:QKV0 - KO], x(k), wslice(k, KO, QKV0 - KO), k == 0, k == KD - 1)
                        last.then_inc(s["qkv_ps"], 1)

                ln_pe_transpose(pe, ln, xn, tp, g.ident, NB, 0)
                pe.wait_ge(s["w_lo"], 1)
                qkv_products(0)

                def tile(p, behind):
                    if behind:
                        pe.wait_ge(s["at_lo"], NB * p)
                        ln_pe_transpose(pe, ln, xn, tp, g.ident, NB, NB * (p + 1))
                        qkv_products(p + 1)
                        pe.wait_ge(ln["lo"], NB * (p + 2))
                    for i in range(NB):
                        pe.wait_ge(s["att"], NB * p + i + 1)
                        pe.wait_ge(s["at_lo"], NB * p + max(0, i - 1))
                        for c in range(KD):
                            last = pe.transpose(tp[i % 2][:, c * P:(c + 1) * P], att[:, i, c * P:(c + 1) * P], g.ident[:])
                        last.then_inc(s["at_ps"], 1)
                    for i in range(NB):
                        pe.wait_ge(s["at_lo"], NB * p + i + 1)
                        pe.wait_ge(s["x_add"], NB * p + max(0, i - 1))
                        for k in range(KD):
                            last = mm3(pe, op[i % 2][:], [at[:, h, k, i * P:(i + 1) * P] for h in range(2)], wo(k),
                                       k == 0, k == KD - 1)
                        last.then_inc(s["o_ps"], 1)

                tiles(pe.Fori, tile)


def stage_cross0(nc, g):
    with ExitStack() as ctx:
        sb, ps, sems = tensors(nc, ctx)
        ln = ln_semaphores(sems, "cross_ln")
        s = sems("cross", "a_hi a_lo o_ps x_add")
        stats, mv = sb("cross_stats", [P, NP, 6]), sb("cross_mv", [P, NP, 2])
        sd, rstd = sb("cross_sd", [P, NP]), sb("cross_rstd", [P, NP])
        xn = sb("cross_xn", [P, NP, D])
        xt = sb("cross_xt", [P, 2, 2, KD, NT], F32R)
        a = sb("cross_a", [P, 2, 2, NP, NT], F32R)
        tp = [ps(f"cross_tp{k}", [P, NT]) for k in range(2)]
        op = [ps(f"cross_o{k}", [P, NT]) for k in range(4)]
        with nc.Block() as block:
            @block.scalar
            def _(act):
                for b in range(NB):
                    if b < 2:
                        act.copy(a[:, b % 2, 0], g.A[:, b]).then_inc(s["a_hi"], 1)
                    ln_act_sqrt(act, ln, mv, sd, g.eps, NP, b)
                    if b >= 2:
                        act.wait_ge(s["o_ps"], NP * (b - 1))
                        act.copy(a[:, b % 2, 0], g.A[:, b]).then_inc(s["a_hi"], 1)
                    ln_act_hi(act, ln, xt[:, b % 2], tp, NP, NP * b)

            @block.vector
            def _(dve):
                def normalise(b):
                    ln_dve_normalise(dve, ln, [g.X[:, b, t, :] for t in range(NP)], stats, mv, sd, rstd, xn, b,
                                     NP * b if b else None)

                normalise(0)
                for b in range(NB):
                    dve.wait_ge(s["a_hi"], b + 1)
                    lo_part(dve, a[:, b % 2, 1], g.A[:, b], a[:, b % 2, 0]).then_inc(s["a_lo"], 1)
                    ln_dve_lo(dve, ln, xt[:, b % 2], tp, NP, NP * b)
                    if b < NB - 1:
                        normalise(b + 1)
                    for t in range(NP):
                        dve.wait_ge(s["o_ps"], NP * b + t + 1)
                        dve.tensor_tensor(g.X[:, b, t, :], g.X[:, b, t, :], op[t][:], ALU.add).then_inc(s["x_add"], 1)

            @block.tensor
            def _(pe):
                def products(b):
                    pe.wait_ge(s["a_lo"], b + 1)
                    for t in range(NP):
                        pe.wait_ge(ln["lo"], NP * b + t + 1)
                        if b:
                            pe.wait_ge(s["x_add"], NP * (b - 1) + t + 1)
                        for k in range(KD):
                            last = mm3(pe, op[t][:], [xt[:, b % 2, h, k, t * P:(t + 1) * P] for h in range(2)],
                                       [a[:, b % 2, h, k] for h in range(2)], k == 0, k == KD - 1)
                        last.then_inc(s["o_ps"], 1)

                for b in range(NB):
                    ln_pe_transpose(pe, ln, xn, tp, g.ident, NP, NP * b)
                    products(b)


def stage_ffn0(nc, g):
    with ExitStack() as ctx:
        sb, ps, sems = tensors(nc, ctx)
        ln = ln_semaphores(sems, "ffn0_ln")
        s = sems("ffn0", "wg_load wg_hi wg_lo wd_load wd_hi wd_lo gu_ps sg h a cm t1 t2 hs h_hi h_lo o_ps x_add")
        M = 4
        GU = 2 * KD * P
        graw, draw = sb("ffn0_graw", [P, GU]), sb("ffn0_draw", [P, D])
        w = sb("ffn0_w", [P, 2, M, PIECE], F32R)
        xt = sb("ffn0_xt", [P, 2, KD, NB * NT], F32R)
        stats, mv = sb("ffn0_stats", [P, NP, 6]), sb("ffn0_mv", [P, NP, 2])
        sd, rstd = sb("ffn0_sd", [P, NP]), sb("ffn0_rstd", [P, NP])
        sg = sb("ffn0_sg", [P, 2, NT])
        h = sb("ffn0_h", [P, 2, M, NT])
        a = sb("ffn0_abs", [P, M, NT])
        xn = a
        ge = sb("ffn0_ge", [P, 6, NT], BF16)
        rank = sb("ffn0_rank", [P, M, NT], BF16)
        hh = sb("ffn0_hh", [P, 2, M, NT], F32R)
        gp = [ps(f"ffn0_g{k}", [P, NT]) for k in range(2)]
        up = [ps(f"ffn0_u{k}", [P, NT]) for k in range(2)]
        op = [ps(f"ffn0_o{k}", [P, NT]) for k in range(NP)]

        def wgu(j, which, k):
            at = (which * KD + k) * P
            return [w[:, x, j, at:at + P] for x in range(2)]

        def columns(part):
            return slice(0, GU) if part == "gu" else slice(GU, PIECE)

        def chunks(loop, body):
            body(0, True, False)
            with loop(1, C0 - 1) as c:
                body(c, False, False)
            body(C0 - 1, False, True)

        with nc.Block() as block:
            @block.sync
            def _(sp):
                def load(c, j, part):
                    raw, ready, split = (graw, s["wg_load"], s["wg_lo"]) if part == "gu" else (draw, s["wd_load"], s["wd_lo"])
                    sp.wait_ge(split, M * c + j)
                    sp.dma_start(raw[:], g.dram["ffn0_w"][M * c + j, :, columns(part)]).then_inc(ready, 16)

                for j in range(M):
                    load(0, j, "gu")

                def chunk(c, first, last):
                    for j in range(M):
                        load(c, j, "down")
                    if not last:
                        for j in range(M):
                            load(c + 1, j, "gu")

                chunks(sp.Fori, chunk)

            @block.scalar
            def _(act):
                def split_gu(c, j):
                    act.wait_ge(s["wg_load"], 16 * (M * c + j + 1))
                    act.copy(w[:, 0, j, 0:GU], graw[:]).then_inc(s["wg_hi"], 1)

                with act.Fori(0, NB) as b:
                    ln_act_sqrt(act, ln, mv, sd, g.eps, NP, b)
                    ln_act_hi(act, ln, xt[:, :, :, bass.ds(b * NT, NT)], gp, NP, NP * b)
                    split_gu(0, b)

                def h_abs(u, par):
                    act.wait_ge(s["h"], M * u + M)
                    act.wait_ge(s["cm"], 3 * u)
                    act.activation(a[:], h[:, par], ACT.Abs).then_inc(s["a"], 1)

                def h_hi(u, par):
                    act.wait_ge(s["hs"], M * u + M)
                    act.wait_ge(s["o_ps"], NP * u)
                    act.copy(hh[:, 0], h[:, par]).then_inc(s["h_hi"], 1)

                def chunk(c, first, last):
                    for b in range(NB):
                        u = NB * c + b
                        if not (first and b == 0):
                            h_abs(u - 1, (b + 1) % 2)
                        for j in range(M):
                            if b == 2:
                                act.wait_ge(s["wd_load"], 16 * (M * c + j + 1))
                                act.wait_ge(s["o_ps"], NP * NB * c)
                                act.copy(w[:, 0, j, GU:], draw[:]).then_inc(s["wd_hi"], 1)
                            n = M * u + j
                            act.wait_ge(s["gu_ps"], n + 1)
                            if not (first and b == 0 and j < 2):
                                act.wait_ge(s["h"], n - 1)
                            act.activation(sg[:, j % 2], gp[j % 2][:], ACT.Silu).then_inc(s["sg"], 1)
                            if b == NB - 1 and not last:
                                split_gu(c + 1, j)
                        if not (first and b == 0):
                            h_hi(u - 1, (b + 1) % 2)

                chunks(act.Fori, chunk)
                h_abs(NB * C0 - 1, (NB - 1) % 2)
                h_hi(NB * C0 - 1, (NB - 1) % 2)

            @block.vector
            def _(dve):
                def split_gu(c, j):
                    dve.wait_ge(s["wg_hi"], M * c + j + 1)
                    lo_part(dve, w[:, 1, j, 0:GU], graw[:], w[:, 0, j, 0:GU]).then_inc(s["wg_lo"], 1)

                with dve.Fori(0, NB) as b:
                    ln_dve_normalise(dve, ln, [g.X[:, b, t, :] for t in range(NP)], stats, mv, sd, rstd, xn, b, NP * b)
                    ln_dve_lo(dve, ln, xt[:, :, :, bass.ds(b * NT, NT)], gp, NP, NP * b)
                    split_gu(0, b)

                def compare(u, par):
                    dve.wait_ge(s["a"], u + 1)
                    dve.wait_ge(s["t2"], M * u)
                    for i, at, n in ((0, 0, 3), (1, 3, 2), (2, 5, 1)):
                        one = a[:, i:i + 1].to_broadcast([P, n, NT])
                        dve.tensor_tensor(ge[:, at:at + n], one, a[:, i + 1:], ALU.is_ge).then_inc(s["cm"], 1)

                def rank_a(u, par):
                    dve.wait_ge(s["cm"], 3 * u + 3)
                    dve.wait_ge(s["hs"], M * u)
                    for j, (x, y) in enumerate(((0, 1), (3, 4), (1, 3), (4, 5))):
                        dve.tensor_tensor(rank[:, j], ge[:, x], ge[:, y], ALU.add).then_inc(s["t1"], 1)

                def rank_b(u, par):
                    dve.wait_ge(s["t1"], M * u + M)
                    dve.tensor_tensor(rank[:, 0], rank[:, 0], ge[:, 2], ALU.add).then_inc(s["t2"], 1)
                    dve.tensor_tensor(rank[:, 1], rank[:, 1], ge[:, 0], ALU.subtract).then_inc(s["t2"], 1)
                    dve.tensor_tensor(rank[:, 2], ge[:, 5], rank[:, 2], ALU.subtract).then_inc(s["t2"], 1)
                    dve.tensor_tensor(rank[:, 3], rank[:, 3], ge[:, 2], ALU.add).then_inc(s["t2"], 1)

                def select(u, par):
                    dve.wait_ge(s["t2"], M * u + M)
                    for j, (bound, op0) in enumerate(((2.0, ALU.is_ge), (1.0, ALU.is_ge), (0.0, ALU.is_ge), (1.0, ALU.is_le))):
                        dve.scalar_tensor_tensor(out=h[:, par, j], in0=rank[:, j], scalar=bound, in1=h[:, par, j],
                                                 op0=op0, op1=ALU.mult).then_inc(s["hs"], 1)

                def h_lo(u, par):
                    dve.wait_ge(s["h_hi"], u + 1)
                    dve.wait_ge(s["hs"], M * u + M)
                    lo_part(dve, hh[:, 1], h[:, par], hh[:, 0]).then_inc(s["h_lo"], 1)

                def add(b, u):
                    for t in range(NP):
                        dve.wait_ge(s["o_ps"], NP * u + t + 1)
                        dve.wait_ge(s["x_add"], NP * u)
                        dve.tensor_tensor(g.X[:, b, t], g.X[:, b, t], op[t][:], ALU.add).then_inc(s["x_add"], 1)

                def chunk(c, first, last):
                    for b in range(NB):
                        u = NB * c + b
                        for j, step in enumerate((compare, rank_a, rank_b, select)):
                            if b == 2:
                                dve.wait_ge(s["wd_hi"], M * c + j + 1)
                                lo_part(dve, w[:, 1, j, GU:], draw[:], w[:, 0, j, GU:]).then_inc(s["wd_lo"], 1)
                            if not (first and b == 0):
                                step(u - 1, (b + 1) % 2)
                            dve.wait_ge(s["sg"], M * u + j + 1)
                            if not (first and b < 2):
                                dve.wait_ge(s["h_lo"], u - 1)
                            dve.tensor_tensor(h[:, b % 2, j], sg[:, j % 2], up[j % 2][:], ALU.mult).then_inc(s["h"], 1)
                            if b == NB - 1 and not last:
                                split_gu(c + 1, j)
                        if not (first and b < 2):
                            add((b + 2) % NB, u - 2)
                        if not (first and b == 0):
                            h_lo(u - 1, (b + 1) % 2)

                chunks(dve.Fori, chunk)
                u = NB * C0 - 1
                for step in (compare, rank_a, rank_b, select):
                    step(u, u % 2)
                add(NB - 2, u - 1)
                h_lo(u, u % 2)
                add(NB - 1, u)

            @block.tensor
            def _(pe):
                with pe.Fori(0, NB) as b:
                    ln_pe_transpose(pe, ln, xn, gp, g.ident, NP, NP * b)
                pe.wait_ge(ln["lo"], NP * NB)

                def down(u):
                    pe.wait_ge(s["h_lo"], u + 1)
                    pe.wait_ge(s["x_add"], NP * u)
                    for t in range(NP):
                        for j in range(M):
                            last = mm3(pe, op[t][:], [hh[:, y, j, t * P:(t + 1) * P] for y in range(2)],
                                       [w[:, y, j, GU:] for y in range(2)], j == 0, j == M - 1)
                        last.then_inc(s["o_ps"], 1)

                def chunk(c, first, last):
                    for b in range(NB):
                        x = lambda k: [xt[:, y, k, b * NT:(b + 1) * NT] for y in range(2)]
                        for j in range(M):
                            n = M * (NB * c + b) + j
                            if b == 0:
                                pe.wait_ge(s["wg_lo"], M * c + j + 1)
                            if not (first and b == 0 and j < 2):
                                pe.wait_ge(s["sg"], n - 1)
                                pe.wait_ge(s["h"], n - 1)
                            for which, bank in enumerate((gp, up)):
                                for k in range(KD):
                                    done = mm3(pe, bank[j % 2][:], wgu(j, which, k), x(k), k == 0, k == KD - 1)
                            done.then_inc(s["gu_ps"], 1)
                        if b == 2:
                            pe.wait_ge(s["wd_lo"], M * c + M)
                        if not (first and b < 2):
                            down(NB * c + b - 2)

                chunks(pe.Fori, chunk)
                down(NB * C0 - 2)
                down(NB * C0 - 1)


def pair_piece(g, t, n):
    if n == 1:
        return W1_PIECES[1], g.raw_kv, [g.s[k] for k in ("kv_load", "kv_hi", "kv_lo")], t
    return W1_PIECES[n], g.raw, [g.s[k] for k in ("pw_load", "pw_hi", "pw_lo")], 2 * t + n // 2


def pair_load(sp, g, t, r, n):
    (at, size), raw, (loaded, _, low), before = pair_piece(g, t, n)
    sp.wait_ge(low, before)
    sp.sem_inc(g.s["sp_passed"], 1)
    sp.dma_start(raw[:, 0:size], g.dram["pair_w"][r, :, at:at + size]).then_inc(loaded, 16)


def pair_split_hi(act, g, t, n):
    (at, size), raw, (loaded, high, _), before = pair_piece(g, t, n)
    act.wait_ge(loaded, 16 * (before + 1))
    act.activation(g.pair_w[:, 0, at:at + size], raw[:, 0:size], ACT.Copy, scale=SCALE1 if n == 0 else 1.0).then_inc(high, 1)


def pair_split_lo(dve, g, t, n):
    (at, size), raw, (_, high, low), before = pair_piece(g, t, n)
    dve.wait_ge(high, before + 1)
    dve.scalar_tensor_tensor(out=g.pair_w[:, 1, at:at + size], in0=raw[:, 0:size], scalar=SCALE1 if n == 0 else 1.0,
                             in1=g.pair_w[:, 0, at:at + size].bitcast(F32), op0=ALU.mult, op1=ALU.subtract).then_inc(low, 1)


def latent_down(nc, g, bp, s, ln, ln2):
    with ExitStack() as ctx:
        def sb(name, shape, dt=F32):
            return ctx.enter_context(nc.sbuf_tensor(name, shape, dt))

        def ps(name, shape, dt=F32):
            return ctx.enter_context(nc.psum_tensor(name, shape, dt))

        QK = QL + KVL + DR
        wraw = sb("down_wraw", [P, KD * QK])
        w = sb("down_w", [P, 2, KD * QK], F32R)
        stats, mv = sb("down_stats", [P, NP, 6]), sb("down_mv", [P, NP, 2])
        sd, rstd = sb("down_sd", [P, NP]), sb("down_rstd", [P, NP])
        stats2, mv2 = sb("down_stats2", [P, 2 * NP, 6]), sb("down_mv2", [P, 2, 2 * NP, 2])
        sd2, rstd2 = sb("down_sd2", [P, 2, 2 * NP]), sb("down_rstd2", [P, 2, 2 * NP])
        xn = sb("down_xn", [P, NP, D])
        xt = sb("down_xt", [P, 2, KD, NT], F32R)
        down = sb("down_x", [P, 2, NP, QK])
        kr = sb("down_kr", [P, 2, NP, 2, DR])
        kr2 = sb("down_kr2", [P, 2, NP, DR])
        tmp = sb("down_tmp", [P, 2, NT])
        table = sb("down_rope", [P, 2, NP, DR])
        gb = sb("down_gb", [P, 2 * KQ + 2])
        tp = [ps(f"down_tp{k}", [P, NT]) for k in range(2)]
        cp = [ps(f"down_c{k}", [P, NT]) for k in range(2)]
        kp = [ps(f"down_k{k}", [P, NT]) for k in range(2)]
        up = [ps(f"down_t{k}", [P, NT]) for k in range(2)]
        gain = [gb[:, k:k + 1] for k in range(KQ)] + [gb[:, 2 * KQ:2 * KQ + 1]]
        offset = [gb[:, KQ + k:KQ + k + 1] for k in range(KQ)] + [gb[:, 2 * KQ + 1:2 * KQ + 2]]
        NCH = KQ + 1

        def dst(c, bb):
            cols = slice(bb * NT, (bb + 1) * NT)
            return g.cq[:, :, c, cols] if c < KQ else g.ckv[:, :, cols]

        with nc.Block() as block:
            @block.sync
            def _(sp):
                sp.dma_start(wraw[:], g.dram["down1_w"]).then_inc(s["load"], 16)
                sp.dma_start(table[:], g.dram["rope_t"]).then_inc(s["load"], 16)
                sp.dma_start(gb[:], g.dram["ln_gb"]).then_inc(s["load"], 16)
                for n in range(2):
                    pair_load(sp, g, bp * PAIRS, 0, n)
                sp.dma_start(g.bias[:], g.dram["pair_b"].rearrange("r p c -> p r c")).then_inc(g.s["c_load"], 16)
                sp.dma_start(g.rope[:], g.dram["rope_f"]).then_inc(g.s["c_load"], 16)
                sp.dma_start(g.a_all[:], g.dram["scan_ad"][:, 0:CT * NS].rearrange("p (c n) -> p c n", c=CT)).then_inc(g.s["c_load"], 16)

            @block.scalar
            def _(act):
                def turned(bb):
                    b = 2 * bp + bb
                    for c in range(NCH):
                        act.wait_ge(s["t_mul"], NCH * b + c + 1)
                        act.copy(dst(c, bb)[:, 0], tmp[:, c % 2]).then_inc(s["t_hi"], 1)
                    act.wait_ge(s["t_ps"], 5 * b + 5)
                    act.copy(g.kr[:, bb], up[NCH % 2][:]).then_inc(s["kr_hi"], 1)

                ln_act_sqrt(act, ln, mv, sd, g.eps, NP, 2 * bp)
                act.wait_ge(s["load"], 48 * bp + 48)
                act.copy(w[:, 0], wraw[:]).then_inc(s["w_hi"], 1)
                ln_act_hi(act, ln, xt, tp, NP, NP * 2 * bp)
                ln_act_sqrt(act, ln, mv, sd, g.eps, NP, 2 * bp + 1)
                for bb in range(2):
                    b = 2 * bp + bb
                    for t in range(NP):
                        act.wait_ge(s["d_ps"], NP * b + t + 1)
                        act.copy(down[:, bb, t, 0:QL], cp[t % 2][:, 0:QL])
                        act.copy(down[:, bb, t, QL:], kp[t % 2][:, 0:QK - QL]).then_inc(s["d_in"], 1)
                    act.wait_ge(ln2["var"], b + 1)
                    act.activation(sd2[:, bb], mv2[:, bb, :, 1], ACT.Sqrt, bias=g.eps[:, 0:1]).then_inc(ln2["sd"], 1)
                    if bb == 0:
                        ln_act_hi(act, ln, xt, tp, NP, NP * (b + 1))
                        turned(0)
                        pair_split_hi(act, g, bp * PAIRS, 0)
                pair_split_hi(act, g, bp * PAIRS, 1)
                turned(1)

            @block.vector
            def _(dve):
                def normalise(b):
                    ln_dve_normalise(dve, ln, [g.X[:, b, t, :] for t in range(NP)], stats, mv, sd, rstd, xn, b, NP * b)

                def latents(bb):
                    b = 2 * bp + bb
                    for t in range(NP):
                        dve.wait_ge(s["d_in"], NP * b + t + 1)
                        dve.bn_stats(stats2[:, 2 * t, :], down[:, bb, t, 0:QL])
                        last = dve.bn_stats(stats2[:, 2 * t + 1, :], down[:, bb, t, QL:QL + KVL])
                    last.then_inc(ln2["stats"], 1)
                    dve.wait_ge(ln2["stats"], b + 1)
                    dve.sem_inc(ln2["passed"], 1)
                    for n in range(2 * NP):
                        last = dve.bn_aggr(mv2[:, bb, n, :], stats2[:, n, :])
                    last.then_inc(ln2["var"], 1)
                    a = down[:, bb, :, QL + KVL:]
                    half = DR // 2
                    dve.tensor_tensor(kr[:, bb, :, 0], a, table[:, 0], ALU.mult).then_inc(s["kr"], 1)
                    dve.tensor_tensor(kr2[:, bb, :, 0:half], a[:, :, half:], table[:, 1, :, 0:half], ALU.mult).then_inc(s["kr"], 1)
                    dve.tensor_tensor(kr2[:, bb, :, half:], a[:, :, 0:half], table[:, 1, :, half:], ALU.mult).then_inc(s["kr"], 1)
                    dve.wait_ge(s["kr"], 5 * b + 3)
                    dve.tensor_tensor(kr[:, bb, :, 0], kr[:, bb, :, 0], kr2[:, bb], ALU.add).then_inc(s["kr"], 1)
                    dve.wait_ge(s["kr"], 5 * b + 4)
                    dve.tensor_copy(kr[:, bb, :, 1], kr[:, bb, :, 0]).then_inc(s["kr"], 1)
                    dve.wait_ge(ln2["sd"], b + 1)
                    dve.reciprocal(rstd2[:, bb], sd2[:, bb]).then_inc(ln2["rstd"], 1)
                    dve.wait_ge(ln2["rstd"], b + 1)
                    for n in range(2 * NP):
                        part = down[:, bb, n // 2, 0:QL] if n % 2 == 0 else down[:, bb, n // 2, QL:QL + KVL]
                        dve.tensor_scalar(part, part, mv2[:, bb, n, 0:1], rstd2[:, bb, n:n + 1], ALU.subtract,
                                          ALU.mult).then_inc(ln2["norm"], 1)

                def turned(bb):
                    b = 2 * bp + bb

                    def low(c):
                        dve.wait_ge(s["t_hi"], NCH * b + c + 1)
                        dve.wait_ge(s["t_mul"], NCH * b + c + 1)
                        lo_part(dve, dst(c, bb)[:, 1], tmp[:, c % 2], dst(c, bb)[:, 0]).then_inc(s["t_lo"], 1)

                    for c in range(NCH):
                        dve.wait_ge(s["t_ps"], 5 * b + c + 1)
                        dve.wait_ge(s["t_lo"], NCH * b + max(0, c - 1))
                        dve.tensor_scalar(tmp[:, c % 2], up[c % 2][:], gain[c], offset[c], ALU.mult, ALU.add).then_inc(s["t_mul"], 1)
                        if c:
                            low(c - 1)
                    low(NCH - 1)
                    dve.wait_ge(s["kr_hi"], b + 1)
                    up_half = slice(DR, 2 * DR)
                    lo_part(dve, g.kr[up_half, bb], up[NCH % 2][up_half], g.kr[up_half, bb]).then_inc(s["kr_lo"], 1)

                normalise(2 * bp)
                dve.wait_ge(s["w_hi"], bp + 1)
                lo_part(dve, w[:, 1], wraw[:], w[:, 0]).then_inc(s["w_lo"], 1)
                ln_dve_lo(dve, ln, xt, tp, NP, NP * 2 * bp)
                normalise(2 * bp + 1)
                latents(0)
                ln_dve_lo(dve, ln, xt, tp, NP, NP * (2 * bp + 1))
                turned(0)
                pair_split_lo(dve, g, bp * PAIRS, 0)
                latents(1)
                pair_split_lo(dve, g, bp * PAIRS, 1)
                turned(1)

            @block.tensor
            def _(pe):
                def turn(bb):
                    b = 2 * bp + bb
                    pe.wait_ge(ln2["norm"], 2 * NP * (b + 1))
                    pe.wait_ge(s["kr"], 5 * b + 5)
                    for c in range(NCH + 1):
                        pe.wait_ge(s["t_mul"], NCH * b + max(0, c - 1))
                        if c < 2:
                            pe.wait_ge(s["kr_lo"], b)
                        for t in range(NP):
                            src = down[:, bb, t, c * P:(c + 1) * P] if c < NCH else kr[:, bb, t].rearrange("p a d -> p (a d)")
                            last = pe.transpose(up[c % 2][:, t * P:(t + 1) * P], src, g.ident[:])
                        last.then_inc(s["t_ps"], 1)

                for bb in range(2):
                    b = 2 * bp + bb
                    ln_pe_transpose(pe, ln, xn, tp, g.ident, NP, NP * b)
                    if bb:
                        turn(0)
                    pe.wait_ge(s["w_lo"], bp + 1)
                    for t in range(NP):
                        pe.wait_ge(ln["lo"], NP * b + t + 1)
                        pe.wait_ge(s["d_in"], NP * b + max(0, t - 1))
                        for bank, at, n in ((cp, 0, QL), (kp, QL, QK - QL)):
                            for k in range(KD):
                                last = mm3(pe, bank[t % 2][:, 0:n], [xt[:, h, k, t * P:(t + 1) * P] for h in range(2)],
                                           [w[:, h, k * QK + at:k * QK + at + n] for h in range(2)], k == 0, k == KD - 1)
                        last.then_inc(s["d_ps"], 1)
                turn(1)


def latent_heads(nc, g, bp, s):
    with ExitStack() as ctx:
        def sb(name, shape, dt=F32):
            return ctx.enter_context(nc.sbuf_tensor(name, shape, dt))

        def ps(name, shape, dt=F32):
            return ctx.enter_context(nc.psum_tensor(name, shape, dt))

        U = 4
        w, bias_all, rope, a_all = g.pair_w, g.bias, g.rope, g.a_all
        qn = sb("pair_qn", [P, 2, 2, NT], F32R)
        kn = sb("pair_kn", [P, 2, 2, NT], F32R)
        qr1 = sb("pair_qr1", [P, 2, NT], F32R)
        qr2 = sb("pair_qr2", [DR, 2, NT], F32R)
        rot = sb("pair_rot", [P, 2, NT])
        v = sb("pair_v", [P, 2, NP, 2 * DV], F32R)
        pr_ = sb("pair_probs", [P, NP, NT])
        pt = sb("pair_pt", [P, 2, NP, NT], F32R)
        ot = sb("pair_ot", [P, 2, 2, NT], F32R)
        nmax, psum_, prec = (sb(f"pair_{n}", [P, NP]) for n in ("nmax", "psum", "prec"))
        NQ = NS // 4
        rows = sb("scan_rows", [P, 2, NQ, NT])
        dt, du = sb("scan_dt", [P, 2, NT]), sb("scan_du", [P, 2, NT])
        da = sb("scan_da", [P, 2, NT])
        st = sb("scan_state", [P, 3, NT])
        y = sb("scan_y", [P, 2, NT])
        sc = [ps(f"pair_s{k}", [P, NT]) for k in range(2)]
        tb = [ps(f"pair_t{k}", [P, NT]) for k in range(2)]
        gb = [ps(f"pair_g{k}", [P, NT]) for k in range(2)]
        ob = [ps(f"pair_o{k}", [P, NT]) for k in range(2)]
        _, (KVO, _), (OO, _) = W1_PIECES
        dtu, y_st = (s["dtu0"], s["dtu1"]), (s["y_st0"], s["y_st1"])

        FILLS = [("qr", 0, 0), ("kn", 0, 0), ("qn", 0, 0), ("kn", 1, 0), ("qn", 1, 0), ("v", 0, 0), ("v", 0, 1),
                 ("qr", 2, 0), ("kn", 2, 0), ("qn", 2, 0), ("kn", 3, 0), ("qn", 3, 0), ("v", 2, 0), ("v", 2, 1)]
        NF = len(FILLS)
        HI = [kind in ("v", "qn", "kn") for kind, _, _ in FILLS]
        NHI = sum(HI)

        def side(u, q):
            ahead, unit = (u + 2) // U, (u + 2) % U
            first = NF // 2 * (unit // 2)
            order = {1: 3, 3: 4} if u % 2 else {0: 0, 2: 1, 3: 2}
            return [(ahead, first + order[q])] if q in order else []

        def behind(u):
            return [((u + 1) // U, NF // 2 * ((u + 1) // 2 % 2) + k) for k in (5, 6)] if u % 2 else []

        norm_sem = (s["norm_dve"], s["norm_act"])

        def norms(t, u, q):
            return NP * (2 * t + u // 2) + q + 1

        STEPS = [[n] for n in range(U * NP)]

        def target(kind, u, x):
            if kind == "v":
                return v[:, :, 2 * x:2 * x + 2, :]
            return (qn if kind == "qn" else kn)[:, u % 2]

        def bank(f):
            return gb[f % 2][:].rearrange("p (t d) -> p t d", t=2) if FILLS[f][0] == "v" else gb[f % 2][:]

        def bias(r, c):
            return bias_all[:, r, c:c + 1]

        def bias_of(r, kind, u):
            return bias(r, {"qn": 0, "kn": 3}[kind] + u % 2)

        def pairs(loop, body):
            body(0, True, False)
            with loop(1, PAIRS - 1) as r:
                body(r, False, False)
            body(PAIRS - 1, False, True)

        with nc.Block() as block:
            @block.sync
            def _(sp):
                def load_rows(r, n):
                    src = g.bc_dram[bp * 2 + r // 4, bass.ds(n * NS + r % 4 * NQ, NQ), :].rearrange("(o n) t -> o n t", o=1)
                    sp.dma_start(rows[:, n], src.to_broadcast([P, NQ, NT])).then_inc(s["rows_c" if n else "rows_b"], 16)

                def load_chunk(r, ct):
                    b = bp * 2 + r // 4
                    sp.dma_start(dt[:, ct % 2], g.dt_dram[b, :, ct, :]).then_inc(dtu[ct % 2], 16)
                    sp.dma_start(du[:, ct % 2], g.du_dram[b, :, ct, :]).then_inc(dtu[ct % 2], 16)

                load_chunk(0, 0)
                load_rows(0, 0)
                load_rows(0, 1)
                pair_load(sp, g, bp * PAIRS, 0, 2)

                def pair(r, first, last):
                    t = bp * PAIRS + r
                    for ct in range(CT):
                        if not (last and ct == CT - 1):
                            if not (first and ct == 0):
                                sp.wait_ge(s["da"], 16 * t + 4 * ct)
                                sp.wait_ge(s["dbu"], 16 * t + 4 * ct)
                            load_chunk(r + (ct + 1) // CT, (ct + 1) % CT)
                        if not last:
                            for n in {1: (1, 0), 3: (2,)}.get(ct, ()):
                                pair_load(sp, g, t + 1, r + 1, n)
                        if not last and ct == CT - 1:
                            sp.wait_ge(s["dbu"], 16 * t + 16)
                            load_rows(r + 1, 0)
                            sp.wait_ge(s["z"], 16 * t + 16)
                            load_rows(r + 1, 1)
                        sp.wait_ge(s["y"], 16 * t + 4 * ct + 4)
                        sp.dma_start(g.y_dram[t, :, ct, :], y[:, ct % 2]).then_inc(y_st[ct % 2], 16)

                pairs(sp.Fori, pair)
                for n in range(2):
                    sp.wait_ge(y_st[n], 32 * PAIRS * (bp + 1))
                sp.sem_inc(s["sp_passed"], 1)

            @block.gpsimd
            def _(pool):
                def pair(r, first, last):
                    t = bp * PAIRS + r

                    def dbu(m):
                        ct, n = m // NQ, m % NQ
                        if m == 0:
                            pool.wait_ge(s["rows_b"], 16 * t + 16)
                        if n == 0:
                            pool.wait_ge(dtu[ct % 2], 64 * t + 32 * (ct // 2) + 32)
                        pool.wait_ge(s["z"], 16 * t + max(0, m - 2))
                        pool.wait_ge(s["y"], 16 * t + max(0, m - 2))
                        pool.tensor_tensor(st[:, m % 3], du[:, ct % 2], rows[:, 0, n], ALU.mult).then_inc(s["dbu"], 1)

                    dbu(0)
                    for m in range(16):
                        ct, n = m // NQ, m % NQ
                        if m < 15:
                            dbu(m + 1)
                        if m == 0:
                            pool.wait_ge(s["rows_c"], 16 * t + 16)
                        pool.wait_ge(s["scan"], 16 * t + m + 1)
                        if n == 0:
                            pool.wait_ge(y_st[ct % 2], 32 * t + 16 * (ct // 2))
                            pool.tensor_tensor(y[:, ct % 2], st[:, m % 3], rows[:, 1, n], ALU.mult).then_inc(s["z"], 1)
                            pool.wait_ge(s["z"], 16 * t + m + 1)
                            pool.sem_inc(s["y"], 1)
                        else:
                            pool.tensor_tensor(st[:, m % 3], st[:, m % 3], rows[:, 1, n], ALU.mult).then_inc(s["z"], 1)
                            pool.wait_ge(s["z"], 16 * t + m + 1)
                            pool.tensor_tensor(y[:, ct % 2], y[:, ct % 2], st[:, m % 3], ALU.add).then_inc(s["y"], 1)

                pairs(pool.Fori, pair)

            @block.scalar
            def _(act):
                act.wait_ge(s["c_load"], 48 * (bp + 1))
                act.activation(a_all[:], a_all[:], ACT.Exp).then_inc(s["a_exp"], 1)

                def split(r, n):
                    pair_split_hi(act, g, bp * PAIRS + r, n)

                def rotary(t, u):
                    act.wait_ge(s["rot"], 6 * (2 * t + u // 2) + 6)
                    hd = u % 2
                    for half in range(2):
                        last = act.copy(qr1[half * DR:(half + 1) * DR, hd], rot[hd * DR:(hd + 1) * DR, 0])
                    last.then_inc(s["qr_hi"], 1)

                def fill(r, f):
                    t = bp * PAIRS + r
                    kind, u, x = FILLS[f]
                    if kind == "qr":
                        return
                    act.wait_ge(s["f_ps"], NF * t + f + 1)
                    if kind == "v":
                        last = act.copy(target(kind, u, x)[:, 0], bank(f))
                    else:
                        last = act.activation(target(kind, u, x)[:, 0], bank(f), ACT.Identity, bias=bias_of(r, kind, u))
                    last.then_inc(s["f_hi"], 1)
                    if kind == "kn":
                        rotary(t, u)

                def exp(n, q):
                    act.wait_ge(s["nmax"], n + 1)
                    act.activation(pr_[:, q], sc[q % 2][:], ACT.Exp, bias=nmax[:, q:q + 1],
                                   accum_out=psum_[:, q:q + 1]).then_inc(s["exp"], 1)

                act.wait_ge(s["consts"], 2 * bp + 2)
                def norm(t, u, q):
                    act.wait_ge(s["prec"], NP * (U * t + u) + q + 1)
                    act.activation(pr_[:, q], pr_[:, q], ACT.Copy, scale=prec[:, q:q + 1]).then_inc(norm_sem[1], 1)

                for f in range(NF // 2):
                    fill(0, f)
                for q in range(NP):
                    exp(NP * U * PAIRS * bp + q, q)

                def pair(r, first, last):
                    t = bp * PAIRS + r
                    for u in range(U):
                        ahead = not (last and u >= 2)
                        more = not (last and u == U - 1)
                        for q in range(NP):
                            n = 16 * t + NP * u + q
                            act.wait_ge(s["t_ps2"], n + 1)
                            act.copy(pt[:, 0, :, q * P:(q + 1) * P], tb[q % 2][:].rearrange("p (k q) -> p k q", k=NP)).then_inc(s["pt_hi"], 1)
                            if u % 2 and more and q:
                                exp(n + NP - 1, q - 1)
                            for m in STEPS[NP * u + q]:
                                ct = m // NQ
                                act.wait_ge(dtu[ct % 2], 64 * t + 32 * (ct // 2) + 32)
                                act.wait_ge(s["scan"], 16 * t + max(0, m - 1))
                                act.activation(da[:, m % 2], dt[:, ct % 2], ACT.Exp,
                                               scale=a_all[:, ct, bass.ds(r % 4 * NQ + m % NQ, 1)]).then_inc(s["da"], 1)
                            if more and q and u % 2 == 0:
                                if q >= 2:
                                    norm(t, u + 1, q - 2)
                                exp(n + NP - 1, q - 1)
                            if ahead:
                                for k, f in side(u, q):
                                    fill(r + k, f)
                            if (u, q) == (2, 0) and not last:
                                split(r + 1, 1)
                        if more:
                            exp(16 * t + NP * (u + 2) - 1, NP - 1)
                        if u % 2 == 0:
                            norm(t, u + 1, NP - 2)
                            norm(t, u + 1, NP - 1)
                        if u == 0:
                            act.wait_ge(s["w_ps"], NP * 2 * t)
                            split(r, 2)
                        if u == 1 and not last:
                            split(r + 1, 0)
                        act.wait_ge(s["o_ps"], U * t + u + 1)
                        act.sem_inc(s["act_passed"], 1)
                        act.activation(ot[:, u % 2, 0], ob[0][:], ACT.Identity, bias=bias(r, 5 + u % 2)).then_inc(s["ot_hi"], 1)
                        if not (last and u == U - 1):
                            for k, f in behind(u):
                                fill(r + k, f)

                pairs(act.Fori, pair)

            @block.vector
            def _(dve):
                dve.wait_ge(s["c_load"], 48 * (bp + 1))
                dve.wait_ge(s["a_exp"], bp + 1)
                dve.tensor_scalar(a_all[:], a_all[:], -1.0, None, ALU.mult).then_inc(s["consts"], 1)
                dve.tensor_scalar(bias_all[:, :, 0:3], bias_all[:, :, 0:3], SCALE1, None, ALU.mult).then_inc(s["consts"], 1)

                def split(r, n):
                    pair_split_lo(dve, g, bp * PAIRS + r, n)

                def rotate(r, u, quarters):
                    pb = 2 * (bp * PAIRS + r) + u // 2
                    half = DR // 2
                    for k in quarters:
                        src, dst = slice(k * half, (k + 1) * half), slice((k ^ 1) * half, ((k ^ 1) + 1) * half)
                        dve.scalar_tensor_tensor(out=rot[dst, 1], in0=gb[FILLS.index(("qr", u, 0)) % 2][src, :], scalar=bias_all[src, r, 2:3],
                                                 in1=rope[src, 1], op0=ALU.add, op1=ALU.mult).then_inc(s["rot"], 1)
                    if 3 in quarters:
                        dve.wait_ge(s["rot"], 6 * pb + 5)
                        dve.tensor_tensor(rot[:, 0], rot[:, 0], rot[:, 1], ALU.add).then_inc(s["rot"], 1)

                def fill(r, f):
                    t = bp * PAIRS + r
                    kind, u, x = FILLS[f]
                    if kind == "qr":
                        pb = 2 * t + u // 2
                        dve.wait_ge(s["f_ps"], NF * t + f + 1)
                        dve.wait_ge(s["qr_hi"], 2 * pb)
                        dve.wait_ge(s["qr_lo"], 2 * pb)
                        dve.scalar_tensor_tensor(out=rot[:, 0], in0=gb[f % 2][:], scalar=bias(r, 2),
                                                 in1=rope[:, 0], op0=ALU.add, op1=ALU.mult).then_inc(s["rot"], 1)
                        rotate(r, u, (0, 1))
                        return
                    dve.wait_ge(s["f_hi"], NHI * t + sum(HI[:f]) + 1)
                    out, hi = target(kind, u, x)[:, 1], target(kind, u, x)[:, 0]
                    if kind == "v":
                        last = lo_part(dve, out, bank(f), hi)
                    else:
                        last = dve.scalar_tensor_tensor(out=out, in0=bank(f), scalar=bias_of(r, kind, u), in1=hi.bitcast(F32),
                                                        op0=ALU.add, op1=ALU.subtract)
                    last.then_inc(s["f_lo"], 1)
                    if kind == "kn":
                        hd = u % 2
                        lanes = slice(hd * DR, (hd + 1) * DR)
                        dve.wait_ge(s["rot"], 6 * (2 * t + u // 2) + 6)
                        dve.wait_ge(s["qr_hi"], U * t + u + 1)
                        lo_part(dve, qr2[:, hd], rot[lanes, 0], qr1[lanes, hd]).then_inc(s["qr_lo"], 1)

                def maximum(n, q):
                    dve.wait_ge(s["s_ps"], n + 1)
                    dve.tensor_reduce(nmax[:, q:q + 1], sc[q % 2][:], AX_X, ALU.max, negate=True).then_inc(s["nmax"], 1)

                def normalise(n, u, q):
                    dve.wait_ge(s["exp"], n + 1)
                    dve.reciprocal(prec[:, q:q + 1], psum_[:, q:q + 1]).then_inc(s["prec"], 1)
                    if u % 2 == 0:
                        dve.wait_ge(s["prec"], n + 1)
                        dve.tensor_scalar(pr_[:, q], pr_[:, q], prec[:, q:q + 1], None, ALU.mult).then_inc(norm_sem[0], 1)

                def add(b, t, bb, tok, out):
                    k = NP * (2 * t + bb) + tok
                    dve.wait_ge(s["w_ps"], k + 1)
                    dve.wait_ge(s["x_add"], NP * 2 * t)
                    dve.tensor_tensor(g.X[:, b, tok], g.X[:, b, tok], out[:], ALU.add).then_inc(s["x_add"], 1)

                dve.wait_ge(s["consts"], 2 * bp + 2)
                dve.sem_inc(s["dve_passed"], 1)
                for f in range(NF // 2):
                    fill(0, f)
                    if f == 0:
                        rotate(0, 0, (2, 3))
                for q in range(NP):
                    maximum(NP * U * PAIRS * bp + q, q)
                    if q:
                        normalise(NP * U * PAIRS * bp + q - 1, 0, q - 1)
                normalise(NP * U * PAIRS * bp + NP - 1, 0, NP - 1)

                def pair(r, first, last):
                    t = bp * PAIRS + r
                    for u in range(U):
                        ahead = not (last and u >= 2)
                        more = not (last and u == U - 1)
                        for q in range(NP):
                            n = 16 * t + NP * u + q
                            dve.wait_ge(s["pt_hi"], n + 1)
                            lo_part(dve, pt[:, 1, :, q * P:(q + 1) * P], tb[q % 2][:].rearrange("p (k q) -> p k q", k=NP),
                                    pt[:, 0, :, q * P:(q + 1) * P]).then_inc(s["pt_lo"], 1)
                            if more:
                                maximum(n + NP, q)
                            if u == 2:
                                add(2 * bp, t, 0, q, ob[1])
                            if u == 0 and not first:
                                add(2 * bp + 1, t - 1, 1, q, ob[1])
                            for m in STEPS[NP * u + q]:
                                dve.wait_ge(s["da"], 16 * t + m + 1)
                                dve.wait_ge(s["dbu"], 16 * t + m + 1)
                                dve.tensor_tensor_scan(st[:, m % 3], da[:, m % 2], st[:, m % 3], 0.0, ALU.mult, ALU.add).then_inc(s["scan"], 1)
                            if more and q:
                                normalise(n + NP - 1, u + 1, q - 1)
                            if ahead:
                                for k, f in side(u, q):
                                    fill(r + k, f)
                                if u % 2 == 0 and q == 1:
                                    rotate(r + (u + 2) // U, (u + 2) % U, (2, 3))
                            if (u, q) == (2, 0) and not last:
                                split(r + 1, 1)
                        if more:
                            normalise(16 * t + NP * (u + 2) - 1, u + 1, NP - 1)
                        if u == 0:
                            split(r, 2)
                        if u == 1 and not last:
                            split(r + 1, 0)
                        dve.wait_ge(s["ot_hi"], U * t + u + 1)
                        dve.scalar_tensor_tensor(out=ot[:, u % 2, 1], in0=ob[0][:], scalar=bias(r, 5 + u % 2),
                                                 in1=ot[:, u % 2, 0].bitcast(F32), op0=ALU.add, op1=ALU.subtract).then_inc(s["ot_lo"], 1)
                        if not (last and u == U - 1):
                            for k, f in behind(u):
                                fill(r + k, f)
                    if last:
                        for tok in range(NP):
                            add(2 * bp + 1, t, 1, tok, ob[(tok + 1) % 2])

                pairs(dve.Fori, pair)

            @block.tensor
            def _(pe):
                def fill(r, f, first=False):
                    t = bp * PAIRS + r
                    kind, u, x = FILLS[f]
                    bb = u // 2
                    if f < 2:
                        if not first:
                            pe.wait_ge(s["f_lo"], NHI * t - 1 + f)
                    elif FILLS[f - 2][0] == "qr":
                        pe.wait_ge(s["rot"], 6 * (2 * t + u // 2) + 5)
                    else:
                        pe.wait_ge(s["f_lo"], NHI * t + sum(HI[:f - 2]) + 1)
                    if f in (0, 1):
                        pe.wait_ge(*((s["kv_lo"], t + 1) if f else (s["pw_lo"], 2 * t + 1)))
                    out = gb[f % 2]
                    if kind == "v":
                        for half in range(2):
                            tok = bb * NT + (2 * x + half) * P
                            last = mm3(pe, out[:, half * 2 * DV:(half + 1) * 2 * DV], [g.ckv[:, h, tok:tok + P] for h in range(2)],
                                       [w[:, h, KVO + 2 * DN:KVO + 4 * DN] for h in range(2)])
                    elif kind == "kn":
                        at = KVO + (u % 2) * DN
                        last = mm3(pe, out[:], [w[:, h, at:at + DN] for h in range(2)],
                                   [g.ckv[:, h, bb * NT:(bb + 1) * NT] for h in range(2)])
                    else:
                        at = {"qn": u % 2, "qr": 2}[kind] * P
                        for k in range(KQ):
                            last = mm3(pe, out[:], [w[:, h, k * 3 * P + at:k * 3 * P + at + P] for h in range(2)],
                                       [g.cq[:, h, k, bb * NT:(bb + 1) * NT] for h in range(2)], k == 0, k == KQ - 1)
                    last.then_inc(s["f_ps"], 1)

                def scores(t, u, q, first=False):
                    if q == 0:
                        f = FILLS.index(("qn", u, 0))
                        pe.wait_ge(s["f_lo"], NHI * t + sum(HI[:f]) + 1)
                        pe.wait_ge(s["qr_lo"], U * t + u + 1)
                    n = NP * (U * t + u) + q
                    if not (first and q < 2):
                        pe.wait_ge(s["exp"], n - 1)
                    cols = slice(q * P, (q + 1) * P)
                    bb, hd = u // 2, u % 2
                    mm3(pe, sc[q % 2][:], [qn[:, u % 2, h, cols] for h in range(2)], [kn[:, u % 2, h] for h in range(2)], True, False)
                    pe.matmul(sc[q % 2][:], qr1[:, hd, cols], g.kr[:, bb], start=False, stop=False)
                    pe.matmul(sc[q % 2][:], qr2[:, hd, cols], g.kr[0:DR, bb], start=False, stop=True).then_inc(s["s_ps"], 1)

                def project(t, bb, tok, out):
                    if tok == 0:
                        pe.wait_ge(s["ot_lo"], U * t + 2 * bb + 2)
                    cols = slice(tok * P, (tok + 1) * P)
                    for hd in range(2):
                        last = mm3(pe, out[:], [ot[:, hd, h, cols] for h in range(2)],
                                   [w[:, h, OO + hd * D:OO + (hd + 1) * D] for h in range(2)], hd == 0, hd == 1)
                    last.then_inc(s["w_ps"], 1)

                for f in range(NF // 2):
                    fill(0, f, True)
                for q in range(NP):
                    scores(bp * PAIRS, 0, q, True)

                def pair(r, first, last):
                    t = bp * PAIRS + r
                    for u in range(U):
                        for q in range(NP):
                            n = NP * (U * t + u) + q
                            pe.wait_ge(norm_sem[u % 2], norms(t, u, q))
                            if not (first and u == 0 and q < 2):
                                pe.wait_ge(s["pt_lo"], n - 1)
                            for k in range(NP):
                                turned = pe.transpose(tb[q % 2][:, k * P:(k + 1) * P], pr_[:, q, k * P:(k + 1) * P], g.ident[:])
                            turned.then_inc(s["t_ps2"], 1)
                            if not (last and u == U - 1):
                                scores(t + (u + 1) // U, (u + 1) % U, q)
                            if u == 2:
                                if q == 0:
                                    pe.wait_ge(s["pw_lo"], 2 * t + 2)
                                pe.wait_ge(s["x_add"], NP * 2 * t + q)
                                project(t, 0, q, ob[1])
                            if u == 0 and not first:
                                pe.wait_ge(s["x_add"], NP * (2 * t - 1) + q)
                                project(t - 1, 1, q, ob[1])
                            if not (last and u >= 2):
                                for k, f in side(u, q):
                                    fill(r + k, f)
                        pe.wait_ge(s["pt_lo"], NP * (U * t + u) + NP)
                        pe.wait_ge(s["f_lo"], NHI * t + sum(HI[:NF // 2 * (u // 2 + 1)]))
                        pe.wait_ge(s["ot_lo"], U * t + u)
                        pe.wait_ge(s["x_add"], NP * 2 * bp * PAIRS)
                        hd = u % 2
                        for k in range(NP):
                            done = mm3(pe, ob[0][:], [v[:, h, k, hd * DV:(hd + 1) * DV] for h in range(2)],
                                       [pt[:, h, k] for h in range(2)], k == 0, k == NP - 1)
                        done.then_inc(s["o_ps"], 1)
                        if not (last and u == U - 1):
                            for k, f in behind(u):
                                fill(r + k, f)
                    if last:
                        for tok in range(NP):
                            pe.wait_ge(s["x_add"], NP * (2 * t + 1) + max(0, tok - 1))
                            project(t, 1, tok, ob[(tok + 1) % 2])

                pairs(pe.Fori, pair)


def stage_latent1(nc, g):
    with ExitStack() as ctx:
        sb, ps, sems = tensors(nc, ctx)
        ln, ln2 = ln_semaphores(sems, "down_ln"), ln_semaphores(sems, "down_ln2")
        s1 = sems("down", "load w_hi w_lo d_ps d_in t_ps t_mul t_hi t_lo kr kr_hi kr_lo")
        s2 = sems("pair", "c_load a_exp consts pw_load pw_hi pw_lo kv_load kv_hi kv_lo rows_b rows_c dtu0 dtu1 dbu da scan z y y_st0 y_st1 f_ps f_hi f_lo "
                          "rot qr_hi qr_lo s_ps nmax exp prec norm_dve norm_act t_ps2 pt_hi pt_lo o_ps ot_hi ot_lo w_ps x_add sp_passed dve_passed act_passed")
        g.raw, g.raw_kv = sb("pair_raw", [P, WQ1]), sb("pair_raw_kv", [P, WKV1])
        g.pair_w = sb("pair_w", [P, 2, WPAIR], F32R)
        g.bias = sb("pair_bias", [P, PAIRS, 7])
        g.rope = sb("pair_rope", [P, 2, NT])
        g.a_all = sb("scan_a_all", [P, CT, NS])
        g.s = s2
        g.cq = sb("latent_cq", [P, 2, KQ, 2 * NT], F32R)
        g.ckv = sb("latent_ckv", [P, 2, 2 * NT], F32R)
        g.kr = sb("latent_kr", [P, 2, NT], F32R)
        with nc.Fori(0, NB // 2) as bp:
            latent_down(nc, g, bp, s1, ln, ln2)
            latent_heads(nc, g, bp, s2)


def stage_gate1(nc, g):
    with ExitStack() as ctx:
        sb, ps, sems = tensors(nc, ctx)
        ln = ln_semaphores(sems, "gate_ln")
        s = sems("gate", "load y_load0 y_load1 silu y01 y23 y yd gated t_ps x_add ones w_load0 w_load1 w_load2 w_sum tot mean mrec w_a w_b "
                         "f_stats")
        stats, mv = sb("gate_stats", [P, NP, 6]), sb("gate_mv", [P, NP, 2])
        sd, rstd = sb("gate_sd", [P, NP]), sb("gate_rstd", [P, NP])
        xn = sb("gate_xn", [P, NP, D])
        y = sb("gate_y", [P, 2, 4, CT, NT])
        u = sb("gate_u", [P, 2, CT, NT])
        skip = sb("gate_skip", [P, CT])
        wraw = sb("gate_wraw", [P, 2, KD * FF1])
        wsum = sb("gate_wsum", [P, 3])
        ones = sb("gate_ones", [P, P])
        mrec = sb("gate_mrec", [P, 3])
        tb = [ps(f"gate_t{k}", [P, NT]) for k in range(NP)]
        wp = ps("gate_w", [P, NT])
        y_load = (s["y_load0"], s["y_load1"])
        w_load = (s["w_load0"], s["w_load1"], s["w_load2"])

        with nc.Block() as block:
            @block.sync
            def _(sp):
                def load_weights(n):
                    if n == 2:
                        sp.wait_ge(s["w_a"], 1)
                    sp.dma_start(wraw[:, n % 2], g.dram[f"ffn1_w{n + 1}"]).then_inc(w_load[n], 16)

                sp.dma_start(skip[:], g.dram["scan_ad"][:, CT * NS:]).then_inc(s["load"], 16)
                for b in range(NB):
                    if b >= 2:
                        sp.wait_ge(s["t_ps"], NP * (b - 1))
                    for q in range(4):
                        sp.dma_start(y[:, b % 2, q], g.y_dram[4 * b + q]).then_inc(y_load[b % 2], 16)
                    sp.dma_start(u[:, b % 2], g.u_dram[b]).then_inc(y_load[b % 2], 16)
                    if b < 3:
                        load_weights(b)

            @block.scalar
            def _(act):
                for b in range(NB):
                    ln_act_sqrt(act, ln, mv, sd, g.eps, NP, b)
                    for ct in range(CT):
                        act.wait_ge(ln["norm"], CT * b + ct + 1)
                        act.activation(xn[:, ct], xn[:, ct], ACT.Silu).then_inc(s["silu"], 1)
                    if b < 3:
                        act.wait_ge(w_load[b], 16)
                        act.activation(g.wq[:, b], wraw[:, b % 2], ACT.Abs, accum_out=wsum[:, b:b + 1]).then_inc(s["w_sum"], 1)

            @block.gpsimd
            def _(pool):
                for b in range(NB):
                    v = y[:, b % 2]
                    pool.wait_ge(y_load[b % 2], 80 * (b // 2) + 80)
                    pool.tensor_tensor(v[:, 2], v[:, 2], v[:, 3], ALU.add).then_inc(s["y23"], 1)
                    pool.tensor_tensor(v[:, 0], v[:, 0], v[:, 1], ALU.add).then_inc(s["y01"], 1)

            @block.vector
            def _(dve):
                def weights(n):
                    dve.wait_ge(s["tot"], n + 1)
                    col = slice(n, n + 1)
                    dve.tensor_scalar(g.mean[:, col], wp[:, col], 1.0 / (D * FF1), 1e-5, ALU.mult, ALU.max).then_inc(s["mean"], 1)
                    dve.wait_ge(s["mean"], n + 1)
                    dve.reciprocal(mrec[:, col], g.mean[:, col]).then_inc(s["mrec"], 1)
                    dve.wait_ge(s["mrec"], n + 1)
                    r = wraw[:, n % 2]
                    dve.tensor_scalar(r, r, mrec[:, col], MAGIC, ALU.mult, ALU.add).then_inc(s["w_b"], 1)
                    dve.wait_ge(s["w_b"], 2 * n + 1)
                    dve.tensor_scalar(r, r, MAGIC, 1.0, ALU.subtract, ALU.min).then_inc(s["w_b"], 1)
                    dve.wait_ge(s["w_b"], 2 * n + 2)
                    dve.tensor_scalar(g.wq[:, n], r, -1.0, None, ALU.max).then_inc(s["w_a"], 1)

                def add(b):
                    for t in range(NP):
                        dve.wait_ge(s["t_ps"], NP * b + t + 1)
                        dve.tensor_tensor(g.X[:, b, t, :], g.X[:, b, t, :], tb[t][:], ALU.add).then_inc(s["x_add"], 1)
                    for t in range(NP):
                        dve.wait_ge(s["x_add"], NP * b + t + 1)
                        dve.bn_stats(g.stats[:, NP * b + t, :], g.X[:, b, t, :]).then_inc(s["f_stats"], 1)

                dve.memset(ones[:], 1.0).then_inc(s["ones"], 1)
                dve.wait_ge(s["load"], 16)
                for b in range(NB):
                    v = y[:, b % 2]
                    dve.wait_ge(s["gated"], CT * b)
                    ln_dve_normalise(dve, ln, [g.X[:, b, t, :] for t in range(NP)], stats, mv, sd, rstd, xn, b, None)
                    if b:
                        add(b - 1)
                    dve.wait_ge(s["y01"], b + 1)
                    for ct in range(CT):
                        last = dve.scalar_tensor_tensor(out=v[:, 0, ct], in0=u[:, b % 2, ct], scalar=skip[:, ct:ct + 1], in1=v[:, 0, ct],
                                                        op0=ALU.mult, op1=ALU.add)
                    last.then_inc(s["yd"], 1)
                    dve.wait_ge(s["yd"], b + 1)
                    dve.wait_ge(s["y23"], b + 1)
                    dve.tensor_tensor(v[:, 0], v[:, 0], v[:, 2], ALU.add).then_inc(s["y"], 1)
                    dve.wait_ge(s["y"], b + 1)
                    for ct in range(CT):
                        dve.wait_ge(s["silu"], CT * b + ct + 1)
                        dve.tensor_tensor(v[:, 0, ct], v[:, 0, ct], xn[:, ct], ALU.mult).then_inc(s["gated"], 1)
                    if b < 3:
                        weights(b)
                add(NB - 1)

            @block.tensor
            def _(pe):
                for b in range(NB):
                    if b < 3:
                        pe.wait_ge(s["ones"], 1)
                        pe.wait_ge(s["w_sum"], b + 1)
                        pe.wait_ge(s["mean"], b)
                        pe.matmul(wp[:, b:b + 1], ones[:], wsum[:, b:b + 1], start=True, stop=True).then_inc(s["tot"], 1)
                    pe.wait_ge(s["gated"], CT * b + CT)
                    pe.wait_ge(s["x_add"], NP * b)
                    for t in range(NP):
                        for ct in range(CT):
                            last = pe.transpose(tb[t][:, ct * P:(ct + 1) * P], y[:, b % 2, 0, ct, t * P:(t + 1) * P], g.ident[:])
                        last.then_inc(s["t_ps"], 1)


def stage_ffn1(nc, g):
    with ExitStack() as ctx:
        sb, ps, sems = tensors(nc, ctx)
        ln = ln_semaphores(sems, "ffn1_ln")
        s = sems("ffn1", "idb a_step xq t_ps t_in g_ps u_ps sg h b_step hq1 hq ht_ps ht_in o_ps x_out out")
        NTILE = NB * NP
        mv = sb("ffn1_mv", [P, NTILE, 2])
        sd, rstd = sb("ffn1_sd", [P, NTILE]), sb("ffn1_rstd", [P, NTILE])
        idb = sb("ffn1_idb", [P, P], BF16)
        xn = sb("ffn1_xn", [P, D])
        xq = sb("ffn1_xq", [P, D], BF16)
        xt = sb("ffn1_xt", [P, KD, P], BF16)
        xm, xr, xs = (sb(f"ffn1_{n}", [P, NTILE]) for n in ("xm", "xr", "xs"))
        hm, hr, hs = (sb(f"ffn1_{n}", [P, 1]) for n in ("hm", "hr", "hs"))
        dq = sb("ffn1_dq", [P, NTILE, 2])
        dq3 = sb("ffn1_dq3", [P, NTILE])
        sg = sb("ffn1_sg", [P, FF1])
        h = sb("ffn1_h", [P, FF1])
        hq = sb("ffn1_hq", [P, FF1], BF16)
        ht = sb("ffn1_ht", [P, KF1, P], BF16)
        gp, up = ps("ffn1_g", [P, 3 * NT]), ps("ffn1_u", [P, 3 * NT])
        tp = ps("ffn1_t", [P, 2 * NT], BF16)
        op = ps("ffn1_o", [P, NT])
        mean, wq = g.mean, g.wq
        X = g.X[:].rearrange("p b t f -> p (b t) f")
        out = g.out.rearrange("t b p f -> t (b p) f")
        LOOP = NTILE - 3
        NA, NBS = 5, 5
        sizes = [(0, NT), (NT, NT), (2 * NT, FF1 - 2 * NT)]
        HA = 8
        HB = KF1 - HA

        def steps(loop, body):
            with loop(0, LOOP) as t:
                body(t, 3)
            for left in (2, 1, 0):
                body(NTILE - 1 - left, left)

        with nc.Block() as block:
            @block.sync
            def _(sp):
                def store(t, left):
                    sp.wait_ge(s["x_out"], t + 1)
                    sp.dma_start(out[:, t, :], X[:, t, :]).then_inc(s["out"], 16)

                steps(sp.Fori, store)
                sp.wait_ge(s["out"], 16 * NTILE)

            @block.scalar
            def _(act):
                act.copy(idb[:], g.ident[:]).then_inc(s["idb"], 1)
                act.wait_ge(ln["var"], 1)
                act.activation(sd[:], mv[:, :, 1], ACT.Sqrt, bias=g.eps[:, 0:1]).then_inc(ln["sd"], 1)

                def x_in(t):
                    act.wait_ge(s["t_ps"], t + 1)
                    act.copy(xt[:], tp[:, HB * P:(HB + KD) * P].rearrange("p (c t) -> p c t", c=KD)).then_inc(s["t_in"], 1)

                def silu(t):
                    act.wait_ge(s["g_ps"], t + 1)
                    act.wait_ge(s["h"], t)
                    act.activation(sg[:], gp[:, 0:FF1], ACT.Silu, scale=dq[:, t, 0:1]).then_inc(s["sg"], 1)

                def h_in(t, n, a, k):
                    act.wait_ge(s["ht_ps"], 2 * t + n + 1)
                    act.copy(ht[:, a:a + k], tp[:, 0:k * P].rearrange("p (c t) -> p c t", c=k)).then_inc(s["ht_in"], 1)

                x_in(0)
                silu(0)
                x_in(1)

                def tile(t, left):
                    if left >= 1:
                        silu(t + 1)
                    h_in(t, 0, 0, HA)
                    act.wait_ge(s["ht_ps"], 2 * t + 2)
                    if left >= 2:
                        x_in(t + 2)
                    h_in(t, 1, HA, HB)

                steps(act.Fori, tile)

            @block.vector
            def _(dve):
                for t in range(NTILE):
                    last = dve.bn_aggr(mv[:, t, :], g.stats[:, t, :])
                last.then_inc(ln["var"], 1)
                dve.wait_ge(ln["sd"], 1)
                dve.reciprocal(rstd[:], sd[:]).then_inc(ln["rstd"], 1)
                dve.wait_ge(ln["rstd"], 1)

                def x_quant(t):
                    one = lambda a: a[:, bass.ds(t, 1)]
                    dve.wait_ge(s["xq"], t)
                    dve.tensor_scalar(xn[:], X[:, t, :], mv[:, t, 0:1], one(rstd), ALU.subtract, ALU.mult).then_inc(s["a_step"], 1)
                    dve.wait_ge(s["a_step"], NA * t + 1)
                    dve.tensor_reduce(one(xm), xn[:], AX_X, ALU.max, apply_absolute_value=True).then_inc(s["a_step"], 1)
                    dve.wait_ge(s["a_step"], NA * t + 2)
                    dve.tensor_scalar(one(xr), one(xm), 1e-5, 1.0 / 127.0, ALU.max, ALU.mult).then_inc(s["a_step"], 1)
                    dve.wait_ge(s["a_step"], NA * t + 3)
                    dve.reciprocal(one(xs), one(xr)).then_inc(s["a_step"], 1)
                    dve.tensor_scalar(dq[:, t, :], mean[:, 0:2], one(xr), None, ALU.mult)
                    dve.wait_ge(s["a_step"], NA * t + 4)
                    dve.tensor_scalar(xn[:], xn[:], one(xs), MAGIC, ALU.mult, ALU.add).then_inc(s["a_step"], 1)
                    dve.wait_ge(s["a_step"], NA * t + 5)
                    dve.wait_ge(s["t_ps"], t)
                    dve.tensor_scalar(xq[:], xn[:], MAGIC, 127.0, ALU.subtract, ALU.min).then_inc(s["xq"], 1)

                def hidden(t):
                    one = lambda a: a[:, bass.ds(t, 1)]
                    dve.wait_ge(s["sg"], t + 1)
                    dve.wait_ge(s["u_ps"], t + 1)
                    dve.wait_ge(s["hq"], t)
                    dve.scalar_tensor_tensor(out=h[:], in0=up[:, 0:FF1], scalar=dq[:, t, 1:2], in1=sg[:],
                                             op0=ALU.mult, op1=ALU.mult).then_inc(s["h"], 1)
                    dve.wait_ge(s["h"], t + 1)
                    dve.tensor_reduce(hm[:], h[:], AX_X, ALU.max, apply_absolute_value=True).then_inc(s["b_step"], 1)
                    dve.wait_ge(s["b_step"], NBS * t + 1)
                    dve.tensor_scalar(hr[:], hm[:], 1e-5, 1.0 / 127.0, ALU.max, ALU.mult).then_inc(s["b_step"], 1)
                    dve.wait_ge(s["b_step"], NBS * t + 2)
                    dve.reciprocal(hs[:], hr[:]).then_inc(s["b_step"], 1)
                    dve.tensor_tensor(one(dq3), hr[:], mean[:, 2:3], ALU.mult).then_inc(s["b_step"], 2)
                    dve.wait_ge(s["b_step"], NBS * t + NBS)
                    dve.tensor_scalar(h[:], h[:], hs[:], MAGIC, ALU.mult, ALU.add).then_inc(s["hq1"], 1)
                    dve.wait_ge(s["hq1"], t + 1)
                    dve.wait_ge(s["ht_ps"], 2 * t)
                    dve.tensor_scalar(hq[:], h[:], MAGIC, 127.0, ALU.subtract, ALU.min).then_inc(s["hq"], 1)

                def result(t):
                    dve.wait_ge(s["o_ps"], t + 1)
                    dve.scalar_tensor_tensor(out=X[:, t, :], in0=op[:], scalar=dq3[:, bass.ds(t, 1)], in1=X[:, t, :],
                                             op0=ALU.mult, op1=ALU.add).then_inc(s["x_out"], 1)

                x_quant(0)
                x_quant(1)
                hidden(0)
                x_quant(2)

                def tile(t, left):
                    if left >= 1:
                        hidden(t + 1)
                    if left >= 3:
                        x_quant(t + 3)
                    result(t)

                steps(dve.Fori, tile)

            @block.tensor
            def _(pe):
                pe.wait_ge(s["idb"], 1)

                def turn_x(t):
                    pe.wait_ge(s["xq"], t + 1)
                    for c in range(KD):
                        last = pe.transpose(tp[:, (HB + c) * P:(HB + c + 1) * P], xq[:, c * P:(c + 1) * P], idb[:])
                    last.then_inc(s["t_ps"], 1)

                def product(t, n, bank, free, done):
                    pe.wait_ge(free, t)
                    for a, size in sizes:
                        for k in range(KD):
                            last = pe.matmul(bank[:, a:a + size], xt[:, k, :], wq[:, n, k * FF1 + a:k * FF1 + a + size],
                                             start=k == 0, stop=k == KD - 1)
                    last.then_inc(done, 1)

                def gate(t):
                    pe.wait_ge(s["t_in"], t + 1)
                    product(t, 0, gp, s["sg"], s["g_ps"])

                def up_(t):
                    product(t, 1, up, s["h"], s["u_ps"])

                def turn_h(t, a, k):
                    pe.wait_ge(s["hq"], t + 1)
                    for c in range(k):
                        last = pe.transpose(tp[:, c * P:(c + 1) * P], hq[:, (a + c) * P:(a + c + 1) * P], idb[:])
                    last.then_inc(s["ht_ps"], 1)

                def down(t):
                    pe.wait_ge(s["x_out"], t)
                    for c in range(KF1):
                        if c in (0, HA):
                            pe.wait_ge(s["ht_in"], 2 * t + (1 if c == 0 else 2))
                        last = pe.matmul(op[:], ht[:, c, :], wq[:, 2, c * D:(c + 1) * D], start=c == 0, stop=c == KF1 - 1)
                    last.then_inc(s["o_ps"], 1)

                turn_x(0)
                gate(0)
                up_(0)
                turn_x(1)

                def tile(t, left):
                    if left >= 1:
                        gate(t + 1)
                    pe.wait_ge(s["ht_in"], 2 * t)
                    if left >= 1:
                        pe.wait_ge(s["t_in"], t + 2)
                    turn_h(t, 0, HA)
                    if left >= 1:
                        up_(t + 1)
                    pe.wait_ge(s["ht_in"], 2 * t + 1)
                    if left >= 2:
                        turn_x(t + 2)
                    turn_h(t, HA, HB)
                    down(t)

                steps(pe.Fori, tile)


def decoder(nc, a, stages):
    with ExitStack() as ctx:
        sb, ps, sems = tensors(nc, ctx)
        g = State()
        g.dram = a
        g.x_in = a["x"].rearrange("b (p t) f -> t b p f", t=P)
        g.out = a["out"].rearrange("b (p t) f -> t b p f", t=P)
        g.u_dram = nc.dram_tensor("u_dram", (NB, P, CT, NT), F32).ap()
        g.dt_dram = nc.dram_tensor("dt_dram", (NB, P, CT, NT), F32).ap()
        g.du_dram = nc.dram_tensor("du_dram", (NB, P, CT, NT), F32).ap()
        g.bc_dram = nc.dram_tensor("bc_dram", (NB, 2 * NS, NT), F32).ap()
        g.y_dram = nc.dram_tensor("y_dram", (16, P, CT, NT), F32).ap()
        g.X = sb("X", [P, NB, NP, D])
        g.ident = sb("ident", [P, P])
        g.one, g.eps = sb("one", [P, 1]), sb("eps", [P, 1])
        with ExitStack() as cross:
            g.A = cross.enter_context(nc.sbuf_tensor("attention", [P, NB, NP, NT], F32))
            for f in (stage_context, stage_attention0, stage_cross0)[:stages]:
                f(nc, g)
        for f in (stage_ffn0, stage_latent1)[:max(0, stages - 3)]:
            f(nc, g)
        g.wq, g.mean, g.stats = sb("wq", [P, 3, KD * FF1], BF16), sb("w_mean", [P, 3]), sb("x_stats", [P, NB * NP, 6])
        for f in (stage_gate1, stage_ffn1)[:max(0, stages - 5)]:
            f(nc, g)
        if stages < 7:
            done = sems("end", "out")["out"]
            with nc.Block() as block:
                @block.sync
                def _(sp):
                    sp.dma_start(g.out, g.X[:]).then_inc(done, 16)
                    sp.wait_ge(done, 16)


STAGES = 7


def layouts(v):
    import numpy as np
    c = np.ascontiguousarray

    def rows(w, n):
        return w.reshape(n, P, -1).transpose(1, 0, 2)

    a = {"x": v["x"], "ident_in": np.eye(P, dtype=np.float32)}
    a["ctx_in"] = v["ctx_1024"].transpose(2, 0, 1).reshape(KC, P, NB * NT).transpose(1, 0, 2)
    wq, wk, wi = v["L0_xattn_Wq"].T, v["L0_xattn_Wk"].T, v["L1_xattn_in_proj_w"].T
    xp = v["L1_xattn_x_proj_w"]
    xp = np.concatenate([xp[DTR:], xp[:DTR]], 0).T
    a["ctx_w"] = np.concatenate([rows(np.concatenate([wq, wk, wi], 1), KC).reshape(P, -1), rows(xp, CT).reshape(P, -1)], 1)
    a["dt_w"] = v["L1_xattn_dt_proj_w"].T
    a["ctx_small"] = np.concatenate([
        v["L0_xattn_bq"][:, None], v["L0_xattn_bk"][:, None],
        v["L1_xattn_conv_w"].reshape(CT, P, NCONV).transpose(1, 0, 2).reshape(P, -1),
        v["L1_xattn_conv_b"].reshape(CT, P).T, v["L1_xattn_dt_proj_b"].reshape(CT, P).T], 1)
    grp = v["L0_attn_weight_qkv"].reshape(KV0, (R0 + 2) * DH0, D)
    n = R0 * DH0
    qkv = np.concatenate([grp[:, :n].reshape(-1, D), grp[:, n:n + DH0].reshape(-1, D), grp[:, n + DH0:].reshape(-1, D)], 0)
    a["att0_w"] = np.concatenate([rows(qkv.T, KD).reshape(P, -1), rows(v["L0_attn_weight_proj"].T, KD).reshape(P, -1)], 1)
    wg, wu = (v[k].reshape(KD, P, C0, P, 4).transpose(2, 4, 1, 0, 3).reshape(C0 * 4, P, KD * P) for k in ("L0_ffn_w_gate", "L0_ffn_w_up"))
    wd = v["L0_ffn_w_down"].reshape(C0, P, 4, D).transpose(0, 2, 1, 3).reshape(C0 * 4, P, D)
    a["ffn0_w"] = np.concatenate([wg, wu, wd], 2)
    def halves(w, axis):
        return np.concatenate([w.take(range(0, DR, 2), axis), w.take(range(1, DR, 2), axis)], axis)
    kvd = v["L1_attn_Wkv_down"]
    a["down1_w"] = rows(np.concatenate([v["L1_attn_Wq_down"], kvd[:KVL], halves(kvd[KVL:], 0)], 0).T, KD).reshape(P, -1)
    wq = np.concatenate([v["L1_attn_Wq_up"], v["L1_attn_bq_up"][:, None]], 1).reshape(H1, DN + DR, QL + 1)
    rope = halves(wq[:, DN:], 1)
    pair = lambda t: t.reshape(PAIRS, -1, QL + 1)
    wq = np.concatenate([pair(wq[:, :DN]), pair(rope)], 1)
    bq, wq = wq[:, :, QL], wq[:, :, :QL]
    wkv = np.concatenate([v["L1_attn_Wkv_up"], v["L1_attn_bkv_up"][:, None]], 1).reshape(PAIRS, 2, 2, P, KVL + 1)
    wkv = wkv.transpose(0, 2, 1, 3, 4).reshape(PAIRS, 4 * P, KVL + 1)
    bkv, wkv = wkv[:, :, KVL], wkv[:, :, :KVL]
    wo = v["L1_attn_Wo"].T.reshape(PAIRS, 2, P, D)
    a["pair_w"] = np.concatenate([wq.transpose(0, 2, 1).reshape(PAIRS, KQ, P, 3 * P).transpose(0, 2, 1, 3).reshape(PAIRS, P, -1),
                                  wkv.transpose(0, 2, 1), wo.transpose(0, 2, 1, 3).reshape(PAIRS, P, -1)], 2)
    a["pair_b"] = np.concatenate([bq.reshape(PAIRS, 3, P), bkv.reshape(PAIRS, 4, P)], 1).transpose(0, 2, 1)
    a["ln_gb"] = np.stack([v[k].reshape(-1, P)[j] for k in ("L1_attn_q_ln_g", "L1_attn_q_ln_b") for j in range(KQ)]
                          + [v["L1_attn_kv_ln_g"], v["L1_attn_kv_ln_b"]], 1)
    freq = (1.0 / np.float32(10000.0) ** (np.arange(0, DR, 2, dtype=np.float32) / np.float32(DR))).astype(np.float32)
    ang = np.arange(NT, dtype=np.float32)[:, None] * freq
    cos, sin = np.cos(ang).astype(np.float32), np.sin(ang).astype(np.float32)
    cs = np.stack([np.concatenate([cos, cos], 1), np.concatenate([-sin, sin], 1)], 0)
    a["rope_t"] = cs.reshape(2, NP, P, DR).transpose(2, 0, 1, 3)
    cs = np.stack([np.concatenate([cos, cos], 1), np.concatenate([sin, -sin], 1)], 0)
    a["rope_f"] = np.concatenate([cs, cs], 2).transpose(2, 0, 1)
    a["scan_ad"] = np.concatenate([v["L1_xattn_A_log"].reshape(CT, P, NS).transpose(1, 0, 2).reshape(P, -1),
                                   v["L1_xattn_D"].reshape(CT, P).T], 1)
    a["ffn1_w1"], a["ffn1_w2"] = (rows(v[k].T, KD).reshape(P, -1) for k in ("L1_ffn_w1", "L1_ffn_w2"))
    a["ffn1_w3"] = rows(v["L1_ffn_w3"].T, KF1).reshape(P, -1)
    return {k: c(t) for k, t in a.items()}


def kernel(**inputs):
    import numpy as np
    import concourse.bacc as bacc
    from concourse.bass_utils import run_bass_kernel_spmd

    nc = bacc.Bacc("TRN2", target_bir_lowering=False, num_devices=1)
    arrays = {f"in_{k}": t for k, t in layouts({k: np.asarray(t) for k, t in inputs.items()}).items()}
    drams = {k[3:]: nc.dram_tensor(k, t.shape, mybir.dt.from_np(t.dtype), kind="ExternalInput").ap() for k, t in arrays.items()}
    drams["out"] = nc.dram_tensor("out_dram", (NB, NT, D), F32, kind="ExternalOutput").ap()
    decoder(nc, drams, STAGES)
    r = run_bass_kernel_spmd(nc, [arrays], core_ids=[0])
    return r.results[0]["out_dram"]
```
